# Optimizing a Trainium2 kernel written in Bass

```python
import numpy as np
import jax
import jax.numpy as jnp

def _softmax(x, axis=-1):
    return jax.nn.softmax(x, axis=axis)

def _gelu(x):
    return jax.nn.gelu(x, approximate=True)

def _silu(x):
    return jax.nn.silu(x)

def _sigmoid(x):
    return jax.nn.sigmoid(x)

def _layernorm(x, axis=-1, eps=1e-05):
    m = jnp.mean(x, axis=axis, keepdims=True)
    v = jnp.var(x, axis=axis, keepdims=True)
    return (x - m) / jnp.sqrt(v + eps)

def _scatter_add(tgt, idx, src, axis=0):
    return tgt.at[idx].add(src)

def _segment_sum(src, seg, n):
    return jax.ops.segment_sum(src, seg, n)
kernel_name = 'mk_gnn_ffn_d4_gnn_r32_87bccc'

def setup_inputs(seed: int=0):
    np.random.seed(seed)
    _w = jnp.asarray

    def _rec_inputs():
        import jax
        import jax.numpy as jnp
        _gk = jax.random.key(seed)
        x = -0.0002117 + 1 * jax.random.normal(jax.random.fold_in(_gk, 1), (3125, 256), jnp.float32)
        src = jax.random.randint(jax.random.fold_in(_gk, 2), (50000,), 0, 3125, jnp.int32)
        dst = jax.random.randint(jax.random.fold_in(_gk, 3), (50000,), 0, 3125, jnp.int32)
        _o = jnp.argsort(dst, stable=True)
        src = src[_o]
        dst = dst[_o]
        edge_weight = jax.random.uniform(jax.random.fold_in(_gk, 13), (50000,), jnp.float32, 0.0, 0.03125)
        return (x, src, dst, edge_weight)
    x, src, dst, edge_weight = _rec_inputs()

    def _L0_gnn_setup():
        import jax, jax.numpy as jnp
        import numpy as np
        N_NODES = 3125
        N_EDGES = 100000
        D_IN = 256
        D_OUT = 256
        key = jax.random.key(seed)
        k1, k2, k3, k4, k5 = jax.random.split(key, 5)
        x = jax.random.normal(k1, (N_NODES, D_IN), dtype=jnp.float32)
        edge_row = jax.random.randint(k2, (N_EDGES,), 0, N_NODES, dtype=jnp.int32)
        edge_col = jax.random.randint(k3, (N_EDGES,), 0, N_NODES, dtype=jnp.int32)
        edge_val = jax.random.uniform(k4, (N_EDGES,), dtype=jnp.float32) / 32.0
        bound = 1.0 / np.sqrt(D_IN)
        weight = jax.random.uniform(k5, (D_IN, D_OUT), minval=-bound, maxval=bound, dtype=jnp.float32)
        return {'x': x, 'edge_row': edge_row, 'edge_col': edge_col, 'edge_val': edge_val, 'weight': weight}
    _L0_gnn_all = _L0_gnn_setup()
    _L0_gnn_in = {k: v for k, v in _L0_gnn_all.items() if k in ('weight',)}
    del _L0_gnn_all

    def _L0_ffn_setup():
        import jax, jax.numpy as jnp
        import numpy as np
        B, S, H, F, E, K = (8, 128, 256, 512, 16, 2)
        EPS = 1e-05
        key = jax.random.key(seed)
        ks = jax.random.split(key, 9)
        sc = 0.02
        return {'x': jax.random.normal(ks[0], (B, S, H), dtype=jnp.float32), 'gate_w': jax.random.normal(ks[1], (H, E), dtype=jnp.float32) * sc, 'gate_b': jnp.zeros((E,), dtype=jnp.float32), 'w1': jax.random.normal(ks[2], (E, H, F), dtype=jnp.float32) * sc, 'b1': jnp.zeros((E, F), dtype=jnp.float32), 'w2': jax.random.normal(ks[3], (E, F, H), dtype=jnp.float32) * sc, 'b2': jnp.zeros((E, H), dtype=jnp.float32), 'gamma': jnp.ones((H,), dtype=jnp.float32), 'beta': jnp.zeros((H,), dtype=jnp.float32)}
    _L0_ffn_all = _L0_ffn_setup()
    _L0_ffn_in = {k: v for k, v in _L0_ffn_all.items() if k in ('gate_w', 'gate_b', 'w1', 'b1', 'w2', 'b2', 'gamma', 'beta')}
    del _L0_ffn_all

    def _L1_gnn_setup():
        import jax, jax.numpy as jnp
        import numpy as np
        N_NODES = 3125
        N_EDGES = 100000
        D_IN = 256
        D_OUT = 256
        key = jax.random.key(seed)
        k1, k2, k3, k4, k5, k6 = jax.random.split(key, 6)
        x = jax.random.normal(k1, (N_NODES, D_IN), dtype=jnp.float32)
        edge_row = jax.random.randint(k2, (N_EDGES,), 0, N_NODES, dtype=jnp.int32)
        edge_col = jax.random.randint(k3, (N_EDGES,), 0, N_NODES, dtype=jnp.int32)
        edge_weight = jax.random.uniform(k4, (N_EDGES,), dtype=jnp.float32)
        stdv = 1.0 / np.sqrt(D_OUT)
        weight = jax.random.uniform(k5, (2 * D_IN, D_OUT), minval=-stdv, maxval=stdv, dtype=jnp.float32)
        bias = jax.random.uniform(k6, (D_OUT,), minval=-stdv, maxval=stdv, dtype=jnp.float32)
        return {'x': x, 'edge_row': edge_row, 'edge_col': edge_col, 'edge_weight': edge_weight, 'weight': weight, 'bias': bias}
    _L1_gnn_all = _L1_gnn_setup()
    _L1_gnn_in = {k: v for k, v in _L1_gnn_all.items() if k in ('weight', 'bias')}
    del _L1_gnn_all

    def _L1_ffn_setup():
        import jax, jax.numpy as jnp
        import numpy as np
        B, S, D, E, H, K = (4, 128, 256, 8, 512, 2)
        key = jax.random.key(seed)
        ks = jax.random.split(key, 6)
        x = jax.random.normal(ks[0], (B, S, D), jnp.float32)
        Wg = jax.random.normal(ks[1], (D, E), jnp.float32) * 0.02
        bg = jnp.zeros((E,), jnp.float32)
        W1 = jax.random.normal(ks[2], (E, D, H), jnp.float32) * 0.02
        b1 = jnp.zeros((E, H), jnp.float32)
        W2 = jax.random.normal(ks[3], (E, H, D), jnp.float32) * 0.02
        b2 = jnp.zeros((E, D), jnp.float32)
        return {'x': x, 'Wg': Wg, 'bg': bg, 'W1': W1, 'b1': b1, 'W2': W2, 'b2': b2}
    _L1_ffn_all = _L1_ffn_setup()
    _L1_ffn_in = {k: v for k, v in _L1_ffn_all.items() if k in ('Wg', 'bg', 'W1', 'b1', 'W2', 'b2')}
    del _L1_ffn_all

    def _L2_gnn_setup():
        import jax, jax.numpy as jnp
        import numpy as np
        N, E, D, H, DK, DV, L, HUS = (625, 10000, 256, 8, 32, 32, 2, 1024)

        def _layer_norm(x, g, b, eps=1e-05):
            mu = jnp.mean(x, axis=-1, keepdims=True)
            var = jnp.mean((x - mu) ** 2, axis=-1, keepdims=True)
            return (x - mu) * jax.lax.rsqrt(var + eps) * g + b

        def _ga_layer(h, src, dst, Wq, Wk, Wv, Wo, g, b):
            n = h.shape[0]
            q = (h @ Wq).reshape(n, H, DK)
            k = (h @ Wk).reshape(n, H, DK)
            v = (h @ Wv).reshape(n, H, DV)
            e = jnp.sum(q[dst] * k[src], axis=-1) / np.sqrt(DK).astype(np.float32)
            m = jax.ops.segment_max(e, dst, num_segments=n)
            a = jnp.exp(e - m[dst])
            z = jax.ops.segment_sum(a, dst, num_segments=n)
            alpha = a / (z[dst] + 1e-09)
            msg = v[src] * alpha[:, :, None]
            agg = jax.ops.segment_sum(msg, dst, num_segments=n).reshape(n, H * DV)
            out = agg @ Wo
            return _layer_norm(out + h, g, b)
        key = jax.random.key(seed)
        ks = jax.random.split(key, 12)
        s = 0.02
        return {'h': jax.random.normal(ks[0], (N, D), jnp.float32), 'src': jax.random.randint(ks[1], (E,), 0, N, jnp.int32), 'dst': jax.random.randint(ks[2], (E,), 0, N, jnp.int32), 'Wq': jax.random.normal(ks[3], (L, D, H * DK), jnp.float32) * s, 'Wk': jax.random.normal(ks[4], (L, D, H * DK), jnp.float32) * s, 'Wv': jax.random.normal(ks[5], (L, D, H * DV), jnp.float32) * s, 'Wo': jax.random.normal(ks[6], (L, H * DV, D), jnp.float32) * s, 'ln_g': jnp.ones((L, D), jnp.float32), 'ln_b': jnp.zeros((L, D), jnp.float32), 'w1': jax.random.normal(ks[7], (D, HUS), jnp.float32) * s, 'b1': jnp.zeros((HUS,), jnp.float32), 'w2': jax.random.normal(ks[8], (HUS, D), jnp.float32) * s, 'b2': jnp.zeros((D,), jnp.float32)}
    _L2_gnn_all = _L2_gnn_setup()
    _L2_gnn_in = {k: v for k, v in _L2_gnn_all.items() if k in ('Wq', 'Wk', 'Wv', 'Wo', 'ln_g', 'ln_b', 'w1', 'b1', 'w2', 'b2')}
    del _L2_gnn_all

    def _L2_ffn_setup():
        import jax, jax.numpy as jnp
        import numpy as np
        B, T, D, H, E = (16, 128, 256, 512, 8)
        key = jax.random.key(seed)
        ks = jax.random.split(key, 5)
        x = jax.random.normal(ks[0], (B, T, D), dtype=jnp.float32)
        gate_w = jax.random.normal(ks[1], (D, E), dtype=jnp.float32) * 0.02
        gate_b = jnp.zeros((E,), dtype=jnp.float32)
        W1 = jax.random.normal(ks[2], (E, D, H), dtype=jnp.float32) * 0.02
        b1 = jnp.zeros((E, H), dtype=jnp.float32)
        W2 = jax.random.normal(ks[3], (E, H, D), dtype=jnp.float32) * 0.02
        b2 = jnp.zeros((E, D), dtype=jnp.float32)
        return {'x': x, 'gate_w': gate_w, 'gate_b': gate_b, 'W1': W1, 'b1': b1, 'W2': W2, 'b2': b2}
    _L2_ffn_all = _L2_ffn_setup()
    _L2_ffn_in = {k: v for k, v in _L2_ffn_all.items() if k in ('gate_w', 'gate_b', 'W1', 'b1', 'W2', 'b2')}
    del _L2_ffn_all

    def _L3_gnn_setup():
        import jax, jax.numpy as jnp
        import numpy as np
        N_NODES = 3125
        D = 256
        N_LAYERS = 3
        N_EDGES = 100000
        BN_EPS = 1e-05

        def _bn_train(x, gamma, beta):
            m = jnp.mean(x, axis=0)
            v = jnp.var(x, axis=0)
            return gamma * (x - m) * jax.lax.rsqrt(v + BN_EPS) + beta
        key = jax.random.key(seed)
        ks = jax.random.split(key, 16)
        s = 1.0 / np.sqrt(D)
        inp = {'x': jax.random.normal(ks[0], (N_NODES, D), dtype=jnp.float32), 'edge_index': jax.random.randint(ks[1], (2, N_EDGES), 0, N_NODES, dtype=jnp.int64 if jax.config.jax_enable_x64 else jnp.int32), 'edge_weight': jax.random.uniform(ks[2], (N_EDGES,), dtype=jnp.float32), 'W_in': jax.random.uniform(ks[3], (D, D), jnp.float32, -s, s), 'b_in': jax.random.uniform(ks[4], (D,), jnp.float32, -s, s), 'W1': jax.random.uniform(ks[5], (N_LAYERS, D, D), jnp.float32, -s, s), 'b1': jax.random.uniform(ks[6], (N_LAYERS, D), jnp.float32, -s, s), 'g1': jnp.ones((N_LAYERS, D), jnp.float32), 'be1': jnp.zeros((N_LAYERS, D), jnp.float32), 'W2': jax.random.uniform(ks[7], (N_LAYERS, D, D), jnp.float32, -s, s), 'b2': jax.random.uniform(ks[8], (N_LAYERS, D), jnp.float32, -s, s), 'g_out': jnp.ones((N_LAYERS, D), jnp.float32), 'b_out': jnp.zeros((N_LAYERS, D), jnp.float32)}
        return inp
    _L3_gnn_all = _L3_gnn_setup()
    _L3_gnn_in = {k: v for k, v in _L3_gnn_all.items() if k in ('W_in', 'b_in', 'W1', 'b1', 'g1', 'be1', 'W2', 'b2', 'g_out', 'b_out')}
    del _L3_gnn_all

    def _L3_ffn_setup():
        import jax, jax.numpy as jnp
        import numpy as np
        B, K, D = (512, 16, 256)
        E = 32
        H = int(D * 0.25)
        key = jax.random.key(seed)
        ks = jax.random.split(key, 7)
        d_rs = D ** (-0.5)
        h_rs = H ** (-0.5)
        x = jax.random.normal(ks[0], (B, K, D), dtype=jnp.float32)
        router_w = jax.random.uniform(ks[1], (E, D), jnp.float32, -d_rs, d_rs)
        router_b = jax.random.uniform(ks[2], (E,), jnp.float32, -d_rs, d_rs)
        W1 = jax.random.uniform(ks[3], (E, D, H), jnp.float32, -h_rs, h_rs)
        b1 = jax.random.uniform(ks[4], (E, H), jnp.float32, -h_rs, h_rs)
        W2 = jax.random.uniform(ks[5], (E, H, D), jnp.float32, -d_rs, d_rs)
        b2 = jax.random.uniform(ks[6], (E, D), jnp.float32, -d_rs, d_rs)
        return {'x': x, 'router_w': router_w, 'router_b': router_b, 'W1': W1, 'b1': b1, 'W2': W2, 'b2': b2}
    _L3_ffn_all = _L3_ffn_setup()
    _L3_ffn_in = {k: v for k, v in _L3_ffn_all.items() if k in ('router_w', 'router_b', 'W1', 'b1', 'W2', 'b2')}
    del _L3_ffn_all
    return {'x': x, 'src': src, 'dst': dst, 'edge_weight': edge_weight, 'L0_gnn_weight': _L0_gnn_in['weight'], 'L0_ffn_gate_w': _L0_ffn_in['gate_w'], 'L0_ffn_gate_b': _L0_ffn_in['gate_b'], 'L0_ffn_w1': _L0_ffn_in['w1'], 'L0_ffn_b1': _L0_ffn_in['b1'], 'L0_ffn_w2': _L0_ffn_in['w2'], 'L0_ffn_b2': _L0_ffn_in['b2'], 'L0_ffn_gamma': _L0_ffn_in['gamma'], 'L0_ffn_beta': _L0_ffn_in['beta'], 'L1_gnn_weight': _L1_gnn_in['weight'], 'L1_gnn_bias': _L1_gnn_in['bias'], 'L1_ffn_Wg': _L1_ffn_in['Wg'], 'L1_ffn_bg': _L1_ffn_in['bg'], 'L1_ffn_W1': _L1_ffn_in['W1'], 'L1_ffn_b1': _L1_ffn_in['b1'], 'L1_ffn_W2': _L1_ffn_in['W2'], 'L1_ffn_b2': _L1_ffn_in['b2'], 'L2_gnn_Wq': _L2_gnn_in['Wq'], 'L2_gnn_Wk': _L2_gnn_in['Wk'], 'L2_gnn_Wv': _L2_gnn_in['Wv'], 'L2_gnn_Wo': _L2_gnn_in['Wo'], 'L2_gnn_ln_g': _L2_gnn_in['ln_g'], 'L2_gnn_ln_b': _L2_gnn_in['ln_b'], 'L2_gnn_w1': _L2_gnn_in['w1'], 'L2_gnn_b1': _L2_gnn_in['b1'], 'L2_gnn_w2': _L2_gnn_in['w2'], 'L2_gnn_b2': _L2_gnn_in['b2'], 'L2_ffn_gate_w': _L2_ffn_in['gate_w'], 'L2_ffn_gate_b': _L2_ffn_in['gate_b'], 'L2_ffn_W1': _L2_ffn_in['W1'], 'L2_ffn_b1': _L2_ffn_in['b1'], 'L2_ffn_W2': _L2_ffn_in['W2'], 'L2_ffn_b2': _L2_ffn_in['b2'], 'L3_gnn_W_in': _L3_gnn_in['W_in'], 'L3_gnn_b_in': _L3_gnn_in['b_in'], 'L3_gnn_W1': _L3_gnn_in['W1'], 'L3_gnn_b1': _L3_gnn_in['b1'], 'L3_gnn_g1': _L3_gnn_in['g1'], 'L3_gnn_be1': _L3_gnn_in['be1'], 'L3_gnn_W2': _L3_gnn_in['W2'], 'L3_gnn_b2': _L3_gnn_in['b2'], 'L3_gnn_g_out': _L3_gnn_in['g_out'], 'L3_gnn_b_out': _L3_gnn_in['b_out'], 'L3_ffn_router_w': _L3_ffn_in['router_w'], 'L3_ffn_router_b': _L3_ffn_in['router_b'], 'L3_ffn_W1': _L3_ffn_in['W1'], 'L3_ffn_b1': _L3_ffn_in['b1'], 'L3_ffn_W2': _L3_ffn_in['W2'], 'L3_ffn_b2': _L3_ffn_in['b2']}

def reference(x, src, dst, edge_weight, L0_gnn_weight, L0_ffn_gate_w, L0_ffn_gate_b, L0_ffn_w1, L0_ffn_b1, L0_ffn_w2, L0_ffn_b2, L0_ffn_gamma, L0_ffn_beta, L1_gnn_weight, L1_gnn_bias, L1_ffn_Wg, L1_ffn_bg, L1_ffn_W1, L1_ffn_b1, L1_ffn_W2, L1_ffn_b2, L2_gnn_Wq, L2_gnn_Wk, L2_gnn_Wv, L2_gnn_Wo, L2_gnn_ln_g, L2_gnn_ln_b, L2_gnn_w1, L2_gnn_b1, L2_gnn_w2, L2_gnn_b2, L2_ffn_gate_w, L2_ffn_gate_b, L2_ffn_W1, L2_ffn_b1, L2_ffn_W2, L2_ffn_b2, L3_gnn_W_in, L3_gnn_b_in, L3_gnn_W1, L3_gnn_b1, L3_gnn_g1, L3_gnn_be1, L3_gnn_W2, L3_gnn_b2, L3_gnn_g_out, L3_gnn_b_out, L3_ffn_router_w, L3_ffn_router_b, L3_ffn_W1, L3_ffn_b1, L3_ffn_W2, L3_ffn_b2):
    import jax
    import jax.numpy as jnp

    def _L0_gnn_ref(x, edge_row, edge_col, edge_val, weight):
        import jax, jax.numpy as jnp
        import numpy as np
        N_NODES = 3125
        N_EDGES = 100000
        D_IN = 256
        D_OUT = 256
        gathered = edge_val[:, None] * x[edge_col]
        support = jax.ops.segment_sum(gathered, edge_row, num_segments=N_NODES)
        out = jax.nn.relu(support @ weight)
        return out

    def _L0_ffn_ref(x, gate_w, gate_b, w1, b1, w2, b2, gamma, beta):
        import jax, jax.numpy as jnp
        import numpy as np
        B, S, H, F, E, K = (8, 128, 256, 512, 16, 2)
        EPS = 1e-05
        gate_logits = x @ gate_w + gate_b
        topk_vals, topk_idx = jax.lax.top_k(gate_logits, K)
        topk_w = jax.nn.softmax(topk_vals, axis=-1)
        h = jax.nn.relu(jnp.einsum('bsh,ehf->bsef', x, w1) + b1)
        expert_out = jnp.einsum('bsef,efh->bseh', h, w2) + b2
        sel = jnp.take_along_axis(expert_out, topk_idx[:, :, :, None], axis=2)
        moe = jnp.sum(topk_w[..., None] * sel, axis=2)
        y = x + moe
        mu = jnp.mean(y, axis=-1, keepdims=True)
        var = jnp.var(y, axis=-1, keepdims=True)
        return (y - mu) / jnp.sqrt(var + EPS) * gamma + beta

    def _L1_gnn_ref(x, edge_row, edge_col, edge_weight, weight, bias):
        import jax, jax.numpy as jnp
        import numpy as np
        N_NODES = 3125
        N_EDGES = 100000
        D_IN = 256
        D_OUT = 256
        gathered = edge_weight[:, None] * x[edge_col]
        neigh = jax.ops.segment_sum(gathered, edge_row, num_segments=N_NODES)
        w_self, w_neigh = (weight[:D_IN], weight[D_IN:])
        out = x @ w_self + neigh @ w_neigh + bias
        return out

    def _L1_ffn_ref(x, Wg, bg, W1, b1, W2, b2):
        import jax, jax.numpy as jnp
        import numpy as np
        B, S, D, E, H, K = (4, 128, 256, 8, 512, 2)
        Bv, Sv, Dv = x.shape
        gate_scores = x @ Wg + bg
        _, idx = jax.lax.top_k(gate_scores, K)
        mask = jax.nn.one_hot(idx, E, dtype=x.dtype).sum(axis=-2)
        xf = x.reshape(-1, Dv)
        mf = mask.reshape(-1, E)
        h = jax.nn.gelu(jnp.einsum('td,edh->teh', xf, W1) + b1[None], approximate=False)
        y = jnp.einsum('teh,ehd->ted', h, W2) + b2[None]
        out = jnp.einsum('ted,te->td', y, mf)
        return out.reshape(Bv, Sv, Dv)

    def _L2_gnn_ref(h, src, dst, Wq, Wk, Wv, Wo, ln_g, ln_b, w1, b1, w2, b2):
        import jax, jax.numpy as jnp
        import numpy as np
        N, E, D, H, DK, DV, L, HUS = (625, 10000, 256, 8, 32, 32, 2, 1024)

        def _layer_norm(x, g, b, eps=1e-05):
            mu = jnp.mean(x, axis=-1, keepdims=True)
            var = jnp.mean((x - mu) ** 2, axis=-1, keepdims=True)
            return (x - mu) * jax.lax.rsqrt(var + eps) * g + b

        def _ga_layer(h, src, dst, Wq, Wk, Wv, Wo, g, b):
            n = h.shape[0]
            q = (h @ Wq).reshape(n, H, DK)
            k = (h @ Wk).reshape(n, H, DK)
            v = (h @ Wv).reshape(n, H, DV)
            e = jnp.sum(q[dst] * k[src], axis=-1) / np.sqrt(DK).astype(np.float32)
            m = jax.ops.segment_max(e, dst, num_segments=n)
            a = jnp.exp(e - m[dst])
            z = jax.ops.segment_sum(a, dst, num_segments=n)
            alpha = a / (z[dst] + 1e-09)
            msg = v[src] * alpha[:, :, None]
            agg = jax.ops.segment_sum(msg, dst, num_segments=n).reshape(n, H * DV)
            out = agg @ Wo
            return _layer_norm(out + h, g, b)
        for l in range(Wq.shape[0]):
            h = _ga_layer(h, src, dst, Wq[l], Wk[l], Wv[l], Wo[l], ln_g[l], ln_b[l])
        return jax.nn.relu(h @ w1 + b1) @ w2 + b2

    def _L2_ffn_ref(x, gate_w, gate_b, W1, b1, W2, b2):
        import jax, jax.numpy as jnp
        import numpy as np
        B, T, D, H, E = (16, 128, 256, 512, 8)
        Bb, Tt, Dd = x.shape
        Ee = gate_w.shape[1]
        xf = x.reshape(-1, Dd)
        N = xf.shape[0]
        logits = xf @ gate_w + gate_b
        probs = jax.nn.softmax(logits, axis=-1)
        top2_vals, top2_idx = jax.lax.top_k(probs, 2)
        cw = jnp.zeros((N, Ee), dtype=xf.dtype).at[jnp.arange(N)[:, None], top2_idx].add(top2_vals)

        def step(acc, params):
            w1, bb1, w2, bb2, we = params
            h = jax.nn.gelu(xf @ w1 + bb1, approximate=False)
            y = h @ w2 + bb2
            return (acc + we[:, None] * y, None)
        out, _ = jax.lax.scan(step, jnp.zeros_like(xf), (W1, b1, W2, b2, cw.T))
        return out.reshape(Bb, Tt, Dd)

    def _L3_gnn_ref(x, edge_index, edge_weight, W_in, b_in, W1, b1, g1, be1, W2, b2, g_out, b_out):
        import jax, jax.numpy as jnp
        import numpy as np
        N_NODES = 3125
        D = 256
        N_LAYERS = 3
        N_EDGES = 100000
        BN_EPS = 1e-05

        def _bn_train(x, gamma, beta):
            m = jnp.mean(x, axis=0)
            v = jnp.var(x, axis=0)
            return gamma * (x - m) * jax.lax.rsqrt(v + BN_EPS) + beta
        row, col = (edge_index[0], edge_index[1])
        h = x @ W_in + b_in
        for l in range(N_LAYERS):
            msgs = edge_weight[:, None] * h[col]
            pooled = jax.ops.segment_sum(msgs, row, num_segments=N_NODES) + h
            hid = jax.nn.relu(_bn_train(pooled @ W1[l] + b1[l], g1[l], be1[l]))
            rep = hid @ W2[l] + b2[l]
            h = jax.nn.relu(_bn_train(rep, g_out[l], b_out[l]))
        return h

    def _L3_ffn_ref(x, router_w, router_b, W1, b1, W2, b2):
        import jax, jax.numpy as jnp
        import numpy as np
        B, K, D = (512, 16, 256)
        E = 32
        H = int(D * 0.25)
        xf = x.reshape(-1, D)
        logits = xf @ router_w.T + router_b
        idx = jnp.argmax(logits, axis=-1)
        w1t = jnp.take(W1, idx, axis=0)
        h = jnp.einsum('nd,ndh->nh', xf, w1t) + jnp.take(b1, idx, axis=0)
        h = jax.nn.relu(h)
        w2t = jnp.take(W2, idx, axis=0)
        out = jnp.einsum('nh,nhd->nd', h, w2t) + jnp.take(b2, idx, axis=0)
        out = jax.nn.relu(out)
        return out.reshape(x.shape)
    edge_index = jnp.stack([src, dst])
    x = x + _L0_gnn_ref(_layernorm(x, axis=-1), src, dst, edge_weight, L0_gnn_weight)
    x = x + _L0_ffn_ref(_layernorm(x, axis=-1)[None], L0_ffn_gate_w, L0_ffn_gate_b, L0_ffn_w1, L0_ffn_b1, L0_ffn_w2, L0_ffn_b2, L0_ffn_gamma, L0_ffn_beta)[0]
    x = x + _L1_gnn_ref(_layernorm(x, axis=-1), src, dst, edge_weight, L1_gnn_weight, L1_gnn_bias)
    x = x + _L1_ffn_ref(_layernorm(x, axis=-1)[None], L1_ffn_Wg, L1_ffn_bg, L1_ffn_W1, L1_ffn_b1, L1_ffn_W2, L1_ffn_b2)[0]
    x = x + _L2_gnn_ref(_layernorm(x, axis=-1), src, dst, L2_gnn_Wq, L2_gnn_Wk, L2_gnn_Wv, L2_gnn_Wo, L2_gnn_ln_g, L2_gnn_ln_b, L2_gnn_w1, L2_gnn_b1, L2_gnn_w2, L2_gnn_b2)
    x = x + _L2_ffn_ref(_layernorm(x, axis=-1)[None], L2_ffn_gate_w, L2_ffn_gate_b, L2_ffn_W1, L2_ffn_b1, L2_ffn_W2, L2_ffn_b2)[0]
    x = x + _L3_gnn_ref(_layernorm(x, axis=-1), edge_index, edge_weight, L3_gnn_W_in, L3_gnn_b_in, L3_gnn_W1, L3_gnn_b1, L3_gnn_g1, L3_gnn_be1, L3_gnn_W2, L3_gnn_b2, L3_gnn_g_out, L3_gnn_b_out)
    x = x + _L3_ffn_ref(_layernorm(x, axis=-1)[None], L3_ffn_router_w, L3_ffn_router_b, L3_ffn_W1, L3_ffn_b1, L3_ffn_W2, L3_ffn_b2)[0]
    return x

_drawn_inputs = setup_inputs


def setup_inputs(seed=0):
    import zlib

    import numpy as np

    out = dict(_drawn_inputs(seed))
    spreads = {'L0_ffn_gate_b': (0.0, 0.1),
     'L0_ffn_b1': (0.0, 0.369),
     'L0_ffn_b2': (0.0, 0.1),
     'L0_ffn_gamma': (1.0, 0.2),
     'L0_ffn_beta': (0.0, 0.1),
     'L1_ffn_bg': (0.0, 0.1),
     'L1_ffn_b1': (0.0, 0.329),
     'L1_ffn_b2': (0.0, 0.1),
     'L2_gnn_ln_g': (1.0, 0.565),
     'L2_gnn_ln_b': (0.0, 0.62),
     'L2_gnn_b1': (0.0, 0.316),
     'L2_gnn_b2': (0.0, 0.1),
     'L2_ffn_gate_b': (0.0, 0.579),
     'L2_ffn_b1': (0.0, 0.8),
     'L2_ffn_b2': (0.0, 0.451),
     'L3_gnn_g1': (1.0, 0.2),
     'L3_gnn_be1': (0.0, 0.1),
     'L3_gnn_g_out': (1.0, 0.2),
     'L3_gnn_b_out': (0.0, 0.1)}
    factors = {'L2_gnn_Wq': 8.0,
     'L2_gnn_Wk': 8.0,
     'L2_gnn_Wv': 8.0,
     'L2_gnn_Wo': 8.0,
     'L2_ffn_gate_w': 3.004,
     'L2_ffn_W1': 4.016,
     'L2_ffn_W2': 3.759,
     'L3_gnn_b_in': 8.0,
     'L3_gnn_b1': 8.0,
     'L3_gnn_b2': 8.0,
     'L3_ffn_router_b': 2.904,
     'L3_ffn_b1': 8.0,
     'L3_ffn_b2': 5.145}
    for name, (base, spread) in spreads.items():
        noise = np.random.default_rng([zlib.crc32(name.encode()), seed]).standard_normal(out[name].shape)
        drawn = base * np.exp(spread * noise) if base else spread * noise
        out[name] = jnp.asarray(drawn.astype(out[name].dtype))
    for name, factor in factors.items():
        out[name] = (out[name] * factor).astype(out[name].dtype)
    return out
```

```python
import concourse.bass as bass
from concourse import mybir
from contextlib import ExitStack, contextmanager

FP = mybir.dt.float32
BF = mybir.dt.bfloat16
I32 = mybir.dt.int32
U32 = mybir.dt.uint32
ALU = mybir.AluOpType
ACT = mybir.ActivationFunctionType
AX = mybir.AxisListType

P = 128
D = 256
KD = D // P
NODES = 3125
NT = (NODES + P - 1) // P
NPAD = NT * P
LAST = NODES - (NT - 1) * P
EDGES = 50000
EP = 125
EC = EDGES // EP
EU = 16
CHUNKS = -(-((EDGES + NT * (P - 1)) // P) // EU) * EU
HEADS = 8
DH = D // HEADS
EPS = 1e-5
BIG = float(2.0 ** 99)


def token_chunks(picks, experts):
    return (picks * NPAD + experts * (P - 1)) // P


def steps(eng, n, unroll, lag, step):
    for i in range(unroll):
        step(i, i, 0)
    with eng.Fori(1, n // unroll) as k:
        for j in range(unroll):
            step(unroll * k + j, j, k)
    for i in range(n // unroll * unroll, n + lag):
        step(i, i % unroll, i // unroll)


def runs(c, n):
    return not isinstance(c, int) or 0 <= c < n


def wait_count(eng, sem, count):
    if not isinstance(count, int) or count > 0:
        eng.wait_ge(sem, count)


def wait_staged(pool, sem, count, passed):
    pool.wait_ge(sem, count)
    pool.sem_inc(passed, 1)


def linker(eng, sem):
    n = [0]

    def link(ins):
        n[0] += 1
        ins.then_inc(sem, 1)
        eng.wait_ge(sem, n[0])

    return link


class Stage:

    def __init__(self, nc, stack):
        self.nc, self.stack, self.sems = nc, stack, []

    def sem(self, name):
        self.sems.append(self.nc.alloc_semaphore(f"{name}_{self.nc.next_id()}"))
        return self.sems[-1]

    def sb(self, name, shape, dt=FP):
        return self.stack.enter_context(self.nc.sbuf_tensor(f"{name}_{self.nc.next_id()}", shape, dt))


@contextmanager
def stage(nc):
    with ExitStack() as stack:
        st = Stage(nc, stack)
        yield st
        if st.sems:
            nc.clear_and_free_semaphores(st.sems)
            nc.all_engine_barrier(sem_only=True)


class Edges:

    def __init__(self, st, name):
        self.idx = st.sb(name + "_idx", [P, CHUNKS], I32)
        self.pay = st.sb(name + "_pay", [P, CHUNKS * 3])
        self.bin = st.sb(name + "_bin", [1, CHUNKS], I32)


class Routing:

    def __init__(self, st, picks, experts, weighted):
        self.chunks = token_chunks(picks, experts)
        self.bin = st.sb("bin", [1, self.chunks], I32)
        self.idx = st.sb("idx", [P, self.chunks], I32)
        self.slots = [st.sb(f"slots{p}", [P, NT], I32) for p in range(picks)]
        self.weights = [st.sb(f"weight{p}", [P, NT]) for p in range(picks)] if weighted else None


class Core:

    def __init__(self, nc, st):
        self.iota = st.sb("iota", [P, CHUNKS])
        self.ident = st.sb("ident", [P, P])
        self.ident8 = st.sb("ident8", [P, HEADS * P], BF)
        self.ones = st.sb("ones", [P, P])
        self.before = st.sb("before", [P, P])
        self.ps = [st.stack.enter_context(nc.psum_tensor(f"bank{i}", [P, 512], FP)) for i in range(8)]
        self.table = nc.dram_tensor("table", (NPAD, D), FP, kind="Internal").ap()
        self.table2 = nc.dram_tensor("table2", (NPAD, D), FP, kind="Internal").ap()
        self.slot_rows = nc.dram_tensor("slot_rows", (token_chunks(2, 16) * P, D), FP, kind="Internal").ap()
        self.slot_table = nc.dram_tensor("slot_table", (CHUNKS * P * 3,), FP, kind="Internal").ap()
        self.by_src = Edges(st, "by_src")
        self.by_dst = Edges(st, "by_dst")


def tile_of(buf, t, width=D):
    return buf[:, bass.ds(t * width, width)]


def tile_rows(table, t):
    return table[bass.ds(t * P, P), :]


def make_constants(nc, K):
    with stage(nc) as st:
        ii = st.sb("ii", [P, CHUNKS], I32)
        made, ready, chain = st.sem("made"), st.sem("ready"), st.sem("chain")
        with nc.Block() as block:

            @block.gpsimd
            def _(pool):
                nc.gpsimd.iota(ii[:, :], pattern=[[1, CHUNKS]], base=0, channel_multiplier=0).then_inc(made, 1)
                nc.gpsimd.memset(K.ident[:, :], 0.0).then_inc(chain, 1)
                nc.gpsimd.memset(K.ones[:, :], 1.0).then_inc(chain, 1)
                pool.wait_ge(chain, 2)
                nc.gpsimd.affine_select(out=K.ident[:, :], in_=K.ident[:, :], compare_op=ALU.not_equal, fill=1.0,
                                        base=0, pattern=[[-1, P]], channel_multiplier=1).then_inc(made, 1)
                nc.gpsimd.affine_select(out=K.before[:, :], in_=K.ones[:, :], compare_op=ALU.is_ge, fill=0.0,
                                        base=-1, pattern=[[1, P]], channel_multiplier=-1).then_inc(made, 1)

            @block.vector
            def _(dve):
                dve.wait_ge(made, 3)
                nc.vector.tensor_copy(K.iota[:, :], ii[:, :])
                for h in range(HEADS):
                    last = nc.vector.tensor_copy(K.ident8[:, h * P:(h + 1) * P], K.ident[:, :])
                last.then_inc(ready, 1)


def load_nodes(nc, K, x):
    with stage(nc) as st:
        zeroed, loaded = st.sem("zeroed"), st.sem("loaded")
        with nc.Block() as block:

            @block.vector
            def _(dve):
                nc.vector.memset(tile_of(K.x, NT - 1), 0.0).then_inc(zeroed, 1)

            @block.sync
            def _(sp):
                sp.dma_start(K.x[:, 0:(NT - 1) * D].rearrange("p (t d) -> p t d", d=D),
                             x[0:(NT - 1) * P, :].rearrange("(t p) d -> p t d", p=P)).then_inc(loaded, 16)
                sp.wait_ge(zeroed, 1)
                sp.dma_start(K.x[0:LAST, (NT - 1) * D:NT * D], x[(NT - 1) * P:NODES, :]).then_inc(loaded, 16)
                sp.wait_ge(loaded, 32)


def store_nodes(nc, K, out):
    with stage(nc) as st:
        stored = st.sem("stored")
        with nc.Block() as block:

            @block.sync
            def _(sp):
                sp.dma_start(out[0:(NT - 1) * P, :].rearrange("(t p) d -> p t d", p=P),
                             K.x[:, 0:(NT - 1) * D].rearrange("p (t d) -> p t d", d=D)).then_inc(stored, 16)
                sp.dma_start(out[(NT - 1) * P:NODES, :], K.x[0:LAST, (NT - 1) * D:NT * D]).then_inc(stored, 16)
                sp.wait_ge(stored, 32)


def place(nc, K, total, picks, parts, bins, cols, slots, chunk_bin):
    with stage(nc) as st:
        S = st.sb("S", [parts, bins * cols])
        T = st.sb("T", [parts, bins * cols]) if len(picks) > 1 else S
        G = st.sb("G", [parts, bins])
        rc = st.sb("rc", [parts, bins])
        ci = st.sb("ci", [P, bins], I32)
        ni = st.sb("ni", [P, bins], I32)
        nf = st.sb("nf", [P, bins])
        ce = st.sb("ce", [P, bins])
        start = st.sb("start", [P, bins])
        base = st.sb("base", [parts, bins])
        pos = st.sb("pos", [parts, cols])
        posi = st.sb("posi", [parts, cols], I32)
        lane = st.sb("lane", [parts, cols], I32)
        chunk = st.sb("chunk", [parts, cols], I32)
        cb = st.sb("cb", [1, slots])
        S3 = S[:, :].rearrange("p (b c) -> p b c", c=cols)
        T3 = T[:, :].rearrange("p (b c) -> p b c", c=cols)
        chain, rows, counted = st.sem("chain"), st.sem("rows_counted"), st.sem("all_counted")
        with nc.Block() as block:

            @block.tensor
            def _(pe):
                pe.wait_ge(rows, 1)
                nc.tensor.matmul(K.ps[0][:, 0:bins], K.ones[0:parts, :], rc[:, :], start=True, stop=True)
                nc.tensor.matmul(K.ps[1][0:parts, 0:bins], K.before[0:parts, 0:parts], rc[:, :],
                                 start=True, stop=True).then_inc(counted, 1)

            @block.vector
            def _(dve):
                link = linker(dve, chain)
                V = nc.vector
                link(V.tensor_tensor_scan(S[:, :], total, total, 0.0, ALU.add, ALU.max))
                link(V.tensor_copy(G[:, :], S3[:, :, cols - 1]))
                link(V.tensor_copy(rc[:, :], G[:, :]))
                V.tensor_tensor(rc[:, 1:bins], G[:, 1:bins], G[:, 0:bins - 1], ALU.subtract).then_inc(rows, 1)
                dve.wait_ge(counted, 1)
                link(V.tensor_scalar(ci[:, :], K.ps[0][:, 0:bins], float(P - 1), None, ALU.add))
                link(V.tensor_scalar(ni[:, :], ci[:, :], 7, None, ALU.logical_shift_right))
                link(V.tensor_copy(nf[:, :], ni[:, :]))
                link(V.tensor_tensor_scan(ce[:, :], nf[:, :], nf[:, :], 0.0, ALU.add, ALU.max))
                link(V.tensor_tensor(start[:, :], ce[:, :], nf[:, :], ALU.subtract))
                link(V.scalar_tensor_tensor(base[:, :], start[0:parts, :], float(P), K.ps[1][0:parts, 0:bins],
                                            ALU.mult, ALU.add))
                link(V.tensor_scalar(base[:, :], base[:, :], -1.0, None, ALU.add))
                link(V.tensor_tensor(base[:, 1:bins], base[:, 1:bins], G[:, 0:bins - 1], ALU.subtract))
                for mask, row, slot in picks:
                    m3 = mask.rearrange("p (b c) -> p b c", c=cols)
                    for b in range(bins):
                        last = V.scalar_tensor_tensor(T3[:, b, :], S3[:, b, :], base[:, b:b + 1], m3[:, b, :],
                                                      ALU.add, ALU.mult)
                    link(last)
                    link(V.tensor_reduce(pos[:, :], T3.rearrange("p b c -> p c b"), AX.X, ALU.add))
                    link(V.tensor_copy(posi[:, :], pos[:, :]))
                    if slot is not None:
                        link(V.tensor_copy(slot, posi[:, :]))
                    V.tensor_scalar(lane[:, :], posi[:, :], P - 1, None, ALU.bitwise_and)
                    link(V.tensor_scalar(chunk[:, :], posi[:, :], 7, None, ALU.logical_shift_right))
                    link(V.scalar_tensor_tensor(row, lane[:, :], float(slots), chunk[:, :], ALU.mult, ALU.add))
                link(V.memset(cb[:, :], 0.0))
                for b in range(bins - 1):
                    link(V.scalar_tensor_tensor(cb[:, :], K.iota[0:1, 0:slots], ce[0:1, b:b + 1], cb[:, :],
                                                ALU.is_ge, ALU.add))
                link(V.tensor_copy(chunk_bin, cb[:, :]))


def scatter_items(nc, K, picks, parts, cols, unroll, halves, words, slots, fill, out):
    with stage(nc) as st:
        blank = st.sb("blank", [P, slots * words])
        rowr = st.sb("rowr", [parts, halves * unroll], I32)
        payr = st.sb("payr", [parts, halves * unroll * words])
        table = K.slot_table[0:P * slots * words].rearrange("(r w) -> r w", w=words)
        whole = K.slot_table[0:P * slots * words].rearrange("(p f) -> p f", p=P)
        blanked, filled, staged, passed, back = (st.sem(x) for x in ("blanked", "filled", "staged", "passed", "back"))
        landed = [st.sem(f"landed{h}") for h in range(halves)]
        rounds = cols // (unroll * halves)
        with nc.Block() as block:

            @block.vector
            def _(dve):
                for w in range(words):
                    last = nc.vector.memset(blank[:, :].rearrange("p (s w) -> p s w", w=words)[:, :, w], fill[w])
                last.then_inc(blanked, 1)

            @block.gpsimd
            def _(pool):
                pool.wait_ge(filled, 16)
                for n, (row, pay) in enumerate(picks):
                    with pool.Fori(0, rounds) as k:
                        for h in range(halves):
                            pool.wait_ge(landed[h], unroll * 16 * (n * rounds + k))
                            r = slice(h * unroll, (h + 1) * unroll)
                            w = slice(h * unroll * words, (h + 1) * unroll * words)
                            nc.gpsimd.tensor_copy(rowr[:, r], row[:, bass.ds((k * halves + h) * unroll, unroll)])
                            nc.gpsimd.tensor_copy(payr[:, w], pay[:, bass.ds((k * halves + h) * unroll * words,
                                                                            unroll * words)]).then_inc(staged, 1)
                            wait_staged(pool, staged, n * rounds * halves + k * halves + h + 1, passed)
                            for j in range(h * unroll, (h + 1) * unroll):
                                nc.gpsimd.indirect_dma_start(
                                    table, bass.IndirectOffsetOnAxis(ap=rowr[:, j:j + 1], axis=0),
                                    payr[:, j * words:(j + 1) * words], None).then_inc(landed[h], 16)

            @block.sync
            def _(sp):
                sp.wait_ge(blanked, 1)
                sp.dma_start(whole, blank[:, :]).then_inc(filled, 16)
                for h in range(halves):
                    sp.wait_ge(landed[h], unroll * 16 * rounds * len(picks))
                sp.dma_start(out, whole).then_inc(back, 16)
                sp.wait_ge(back, 16)


def sort_edges(nc, K, key, other, weight, to):
    with stage(nc) as st:
        ki = st.sb("ki", [EP, EC], I32)
        oi = st.sb("oi", [EP, EC], I32)
        wf = st.sb("wf", [EP, EC])
        ti = st.sb("ti", [EP, EC], I32)
        li = st.sb("li", [EP, EC], I32)
        tf = st.sb("tf", [EP, EC])
        mask = st.sb("mask", [EP, NT * EC])
        pay = st.sb("pay", [EP, EC * 3])
        row = st.sb("row", [EP, EC], I32)
        pay3 = pay[:, :].rearrange("p (c w) -> p c w", w=3)
        loaded, chain = st.sem("loaded"), st.sem("chain")
        with nc.Block() as block:

            @block.sync
            def _(sp):
                for a, b in ((ki, key), (oi, other), (wf, weight)):
                    sp.dma_start(a[:, :], b.rearrange("(p c) -> p c", c=EC)).then_inc(loaded, 16)

            @block.vector
            def _(dve):
                link = linker(dve, chain)
                V = nc.vector
                dve.wait_ge(loaded, 48)
                V.tensor_scalar(ti[:, :], ki[:, :], 7, None, ALU.logical_shift_right)
                link(V.tensor_scalar(li[:, :], ki[:, :], P - 1, None, ALU.bitwise_and))
                V.tensor_copy(pay3[:, :, 0], oi[:, :])
                V.tensor_copy(pay3[:, :, 1], li[:, :])
                V.tensor_copy(pay3[:, :, 2], wf[:, :])
                link(V.tensor_copy(tf[:, :], ti[:, :]))
                for b in range(NT):
                    last = V.tensor_scalar(mask[:, b * EC:(b + 1) * EC], tf[:, :], float(b), None, ALU.is_equal)
                link(last)

        place(nc, K, mask[:, :], [(mask[:, :], row[:, :], None)], EP, NT, EC, CHUNKS, to.bin[:, :])
        scatter_items(nc, K, [(row, pay)], EP, EC, 8, 2, 3, CHUNKS, (0.0, -1.0, 0.0), to.pay[:, :])
    with stage(nc) as st:
        done = st.sem("done")
        with nc.Block() as block:

            @block.vector
            def _(dve):
                nc.vector.tensor_copy(to.idx[:, :], to.pay[:, :].rearrange("p (c w) -> p c w", w=3)[:, :, 0])\
                    .then_inc(done, 1)


def spmm(nc, K, edges, table, out):
    GR, HALF, R = 16, 8, 4
    with stage(nc) as st:
        idxr = st.sb("idxr", [P, GR], I32)
        rows = st.sb("rows", [P, GR, D])
        pick = st.sb("pick", [P, R, P])
        gathered = [st.sem(f"gathered{j}") for j in range(GR)]
        staged, passed, picked, summed, added, cleared = (
            st.sem(n) for n in ("staged", "passed", "picked", "summed", "added", "cleared"))
        with nc.Block() as block:

            @block.gpsimd
            def _(pool):
                def step(i, j, k):
                    h = j
                    wait_count(pool, summed, HALF * i - GR + HALF)
                    nc.gpsimd.tensor_copy(idxr[:, h * HALF:(h + 1) * HALF],
                                          edges.idx[:, bass.ds(i * HALF, HALF)]).then_inc(staged, 1)
                    wait_staged(pool, staged, i + 1, passed)
                    for g in range(h * HALF, (h + 1) * HALF):
                        nc.gpsimd.indirect_dma_start(
                            rows[:, g, :], None, table,
                            bass.IndirectOffsetOnAxis(ap=idxr[:, g:g + 1], axis=0)).then_inc(gathered[g], 16)

                steps(pool, CHUNKS // HALF, 2, 0, step)

            @block.vector
            def _(dve):
                nc.vector.memset(out[:, :], 0.0).then_inc(cleared, 1)

                def step(i, j, k):
                    if runs(i - R, CHUNKS):
                        c = i - R
                        t = dve.value_load(edges.bin[0:1, bass.ds(c, 1)], min_val=0, max_val=NT - 1)
                        dve.wait_ge(summed, c + 1)
                        dve.wait_ge(added if not isinstance(c, int) or c else cleared, c if not isinstance(c, int) or c else 1)
                        nc.vector.tensor_tensor(tile_of(out, t), tile_of(out, t), K.ps[j][:, 0:D],
                                                ALU.add).then_inc(added, 1)
                    if runs(i, CHUNKS):
                        wait_count(dve, summed, i - R + 1)
                        nc.vector.tensor_scalar(pick[:, j, :], K.iota[:, 0:P], edges.pay[:, bass.ds(3 * i + 1, 1)],
                                                edges.pay[:, bass.ds(3 * i + 2, 1)], ALU.is_equal,
                                                ALU.mult).then_inc(picked, 1)

                steps(dve, CHUNKS, R, R, step)

            @block.tensor
            def _(pe):
                def step(i, j, k):
                    pe.wait_ge(gathered[j], 16 * k + 16)
                    pe.wait_ge(picked, i + 1)
                    wait_count(pe, added, i - R + 1)
                    nc.tensor.matmul(K.ps[j % R][:, 0:D], pick[:, j % R, :], rows[:, j, :],
                                     start=True, stop=True).then_inc(summed, 1)

                steps(pe, CHUNKS, GR, 0, step)


def vector_work(nc, *ops):
    with stage(nc) as st:
        chain = st.sem("chain")
        with nc.Block() as block:

            @block.vector
            def _(dve):
                link = linker(dve, chain)
                for op in ops:
                    link(op())


def layer_norm(nc, K, src, dst, affine=None, table=None, residual=False):
    with stage(nc) as st:
        stats = st.sb("stats", [P, NT * 6])
        mv = st.sb("mv", [P, NT * 2])
        rstd = st.sb("rstd", [P, NT])
        gb = st.sb("gb", [P, 2, D]) if affine else None
        var = mv[:, :].rearrange("p (t s) -> p t s", s=2)[:, :, 1]
        loaded, chain, stat, aggr, var_ok, root, normed, stored = (
            st.sem(n) for n in ("loaded", "chain", "stat", "aggr", "var_ok", "root", "normed", "stored"))
        with nc.Block() as block:

            @block.sync
            def _(sp):
                if affine:
                    for a in range(2):
                        sp.dma_start(gb[:, a, :], affine[a].partition_broadcast(P)).then_inc(loaded, 16)
                if table is not None:
                    def step(t, j, k):
                        sp.wait_ge(normed, t + 1)
                        sp.dma_start(tile_rows(table, t), tile_of(dst, t)).then_inc(stored, 16)

                    steps(sp, NT, 2, 0, step)
                    sp.wait_ge(stored, 16 * NT)

            @block.scalar
            def _(act):
                act.wait_ge(var_ok, 1)
                nc.scalar.activation(rstd[:, :], rstd[:, :], ACT.Sqrt).then_inc(root, 1)

            @block.vector
            def _(dve):
                link = linker(dve, chain)

                def statistics(t, j, k):
                    nc.vector.bn_stats(stats[:, bass.ds(t * 6, 6)], tile_of(src, t)).then_inc(stat, 1)

                steps(dve, NT, 5, 0, statistics)
                dve.wait_ge(stat, NT)
                for t in range(NT):
                    last = nc.vector.bn_aggr(mv[:, 2 * t:2 * t + 2], stats[:, 6 * t:6 * t + 6])
                link(last)
                nc.vector.tensor_scalar(rstd[:, :], var, EPS, None, ALU.add).then_inc(var_ok, 1)
                dve.wait_ge(root, 1)
                link(nc.vector.reciprocal(rstd[:, :], rstd[:, :]))
                if affine:
                    dve.wait_ge(loaded, 32)
                per = 1 + 2 * bool(affine) + bool(residual)

                def normalise(t, j, k):
                    n = per * t
                    ops = [lambda: nc.vector.tensor_scalar(tile_of(dst, t), tile_of(src, t), mv[:, bass.ds(2 * t, 1)],
                                                           rstd[:, bass.ds(t, 1)], ALU.subtract, ALU.mult)]
                    if affine:
                        ops += [lambda: nc.vector.tensor_tensor(tile_of(dst, t), tile_of(dst, t), gb[:, 0, :], ALU.mult),
                                lambda: nc.vector.tensor_tensor(tile_of(dst, t), tile_of(dst, t), gb[:, 1, :], ALU.add)]
                    if residual:
                        ops += [lambda: nc.vector.tensor_tensor(tile_of(K.x, t), tile_of(K.x, t), tile_of(dst, t), ALU.add)]
                    for m, op in enumerate(ops):
                        if m:
                            dve.wait_ge(aggr, n + m)
                        ins = op()
                        if per > 1:
                            ins.then_inc(aggr, 1)
                        else:
                            ins.then_inc(normed, 1)

                steps(dve, NT, 5, 0, normalise)


def dense(nc, K, sources, weights, bias, outs):
    width = sum(o[0] for o in outs)
    nsrc = len(sources)
    tables = [o for o in outs if o[1] in ("table", "both")]
    with stage(nc) as st:
        w = st.sb("w", [P, nsrc * KD, width])
        b = st.sb("b", [1, width]) if bias is not None else None
        raw = st.sb("raw", [P, 2, nsrc * D])
        xT = st.sb("xT", [P, 2, nsrc * D])
        ring = st.sb("ring", [P, 2, len(tables) or 1, D])
        loaded = st.sem("loaded")
        staged, turned, copied, summed, written = (st.sem(n) for n in ("staged", "turned", "copied", "summed", "written"))
        stored = [st.sem(f"stored{j}") for j in range(2)]
        with nc.Block() as block:

            @block.sync
            def _(sp):
                for s in range(nsrc):
                    at = 0
                    for part in weights[s]:
                        n = part.shape[1]
                        for c in range(KD):
                            sp.dma_start(w[:, s * KD + c, at:at + n], part[c * P:(c + 1) * P, :]).then_inc(loaded, 16)
                        at += n
                if b is not None:
                    sp.dma_start(b[:, :], bias).then_inc(loaded, 16)

                def step(t, j, k):
                    sp.wait_ge(written, t + 1)
                    for n, (wd, kind, target, _f) in enumerate(tables):
                        tab, src = (target, ring[:, j, n, 0:wd]) if kind == "table" else (target[1], tile_of(target[0], t, wd))
                        sp.dma_start(tile_rows(tab, t), src).then_inc(stored[j], 16)

                if tables:
                    steps(sp, NT, 2, 0, step)
                    for j in range(2):
                        sp.wait_ge(stored[j], 16 * len(tables) * ((NT + 1 - j) // 2))

            @block.scalar
            def _(act):
                def step(i, j, k):
                    if runs(i, NT):
                        wait_count(act, turned, i - 1)
                        for s, src in enumerate(sources):
                            last = nc.scalar.activation(raw[:, j, s * D:(s + 1) * D], tile_of(src, i), ACT.Copy)
                        last.then_inc(staged, 1)
                    if runs(i - 1, NT):
                        act.wait_ge(turned, i)
                        wait_count(act, summed, i - 2)
                        nc.scalar.activation(xT[:, 1 - j, :], K.ps[1 - j][:, 0:nsrc * D], ACT.Copy).then_inc(copied, 1)

                steps(act, NT, 2, 1, step)

            @block.tensor
            def _(pe):
                pe.wait_ge(loaded, 16 * (KD * sum(len(x) for x in weights) + (b is not None)))

                def step(i, j, k):
                    if runs(i, NT):
                        pe.wait_ge(staged, i + 1)
                        wait_count(pe, copied, i - 1)
                        for s in range(nsrc * KD):
                            last = nc.tensor.transpose(K.ps[j][:, s * P:(s + 1) * P], raw[:, j, s * P:(s + 1) * P],
                                                       K.ident[:, :])
                        last.then_inc(turned, 1)
                    if runs(i - 1, NT):
                        pe.wait_ge(copied, i)
                        wait_count(pe, written, i - 2)
                        at = 0
                        for g, o in enumerate(outs):
                            bank = K.ps[2 + 3 * (1 - j) + g][:, 0:o[0]]
                            for s in range(nsrc * KD):
                                last = nc.tensor.matmul(bank, xT[:, 1 - j, s * P:(s + 1) * P], w[:, s, at:at + o[0]],
                                                        start=(s == 0), stop=(s == nsrc * KD - 1 and b is None))
                            if b is not None:
                                last = nc.tensor.matmul(bank, K.ones[0:1, :], b[0:1, at:at + o[0]], start=False, stop=True)
                            at += o[0]
                        last.then_inc(summed, 1)

                steps(pe, NT, 2, 1, step)

            @block.vector
            def _(dve):
                def step(t, j, k):
                    dve.wait_ge(summed, t + 1)
                    if any(o[1] == "table" for o in outs):
                        wait_count(dve, stored[j], 16 * len(tables) * k)
                    n = 0
                    for g, (wd, kind, target, factor) in enumerate(outs):
                        bank = K.ps[2 + 3 * j + g][:, 0:wd]
                        if kind == "add":
                            last = nc.vector.tensor_tensor(tile_of(K.x, t), tile_of(K.x, t), bank, ALU.add)
                        elif kind == "relu_add":
                            last = nc.vector.scalar_tensor_tensor(tile_of(K.x, t), bank, 0.0, tile_of(K.x, t),
                                                                  ALU.max, ALU.add)
                        else:
                            to = ring[:, j, n, 0:wd] if kind == "table" else tile_of(target if kind == "sb" else target[0], t, wd)
                            if factor is None:
                                last = nc.vector.tensor_copy(to, bank)
                            else:
                                last = nc.vector.tensor_scalar(to, bank, factor, None, ALU.mult)
                        n += kind in ("table", "both")
                    last.then_inc(written, 1)

                steps(dve, NT, 2, 0, step)


def routed_ffn(nc, K, r, w1, b1, w2, b2, func, relu_out):
    experts, _, hid = w1.shape
    hm = min(P, hid)
    nh = hid // hm
    n = r.chunks
    R = 4
    with stage(nc) as st:
        b1T = st.sb("b1T", [hm, experts * nh])
        w1r = st.sb("w1r", [P, R, KD, hid])
        w2r = st.sb("w2r", [hm, R, nh, D])
        b2r = st.sb("b2r", [1, R, D])
        idxr = st.sb("idxr", [P, R], I32)
        rows = st.sb("rows", [P, R, D])
        xT = st.sb("xT", [P, 2, D])
        hT = st.sb("hT", [hm, 2, nh * P])
        yr = st.sb("yr", [P, R, D])
        fetched = [st.sem(f"fetched{j}") for j in range(R)]
        gathered = [st.sem(f"gathered{j}") for j in range(R)]
        stored = [st.sem(f"stored{j}") for j in range(R)]
        biased, staged, passed, turned, copied, hidden, acted, summed, written = (
            st.sem(x) for x in ("biased", "staged", "passed", "turned", "copied", "hidden", "acted", "summed", "written"))
        w1v = w1.rearrange("e (k p) h -> p e k h", p=P)
        w2v = w2.rearrange("e (c p) d -> p e c d", p=hm)
        b2v = b2.rearrange("(o e) d -> o e d", o=1)
        with nc.Block() as block:

            @block.sync
            def _(sp):
                def step(i, j, k):
                    if runs(i, n):
                        e = sp.value_load(r.bin[0:1, bass.ds(i, 1)], min_val=0, max_val=experts - 1)
                        wait_count(sp, summed, i - R + 1)
                        sp.dma_start(w1r[:, j, :, :], w1v[:, bass.ds(e, 1), :, :].rearrange("p e k h -> p (e k) h")).then_inc(fetched[j], 16)
                        sp.dma_start(w2r[:, j, :, :], w2v[:, bass.ds(e, 1), :, :].rearrange("p e c d -> p (e c) d")).then_inc(fetched[j], 16)
                        sp.dma_start(b2r[:, j, :], b2v[:, bass.ds(e, 1), :].rearrange("o e d -> o (e d)")).then_inc(fetched[j], 16)
                    if runs(i - R, n):
                        sp.wait_ge(written, i - R + 1)
                        sp.dma_start(tile_rows(K.slot_rows, i - R), yr[:, j, :]).then_inc(stored[j], 16)

                steps(sp, n, R, R, step)
                for j in range(R):
                    sp.wait_ge(stored[j], 16 * ((n + R - 1 - j) // R))

            @block.gpsimd
            def _(pool):
                def step(i, j, k):
                    wait_count(pool, turned, i - R + 1)
                    nc.gpsimd.tensor_copy(idxr[:, j:j + 1], r.idx[:, bass.ds(i, 1)]).then_inc(staged, 1)
                    wait_staged(pool, staged, i + 1, passed)
                    nc.gpsimd.indirect_dma_start(rows[:, j, :], None, K.table,
                                                 bass.IndirectOffsetOnAxis(ap=idxr[:, j:j + 1], axis=0))\
                        .then_inc(gathered[j], 16)

                steps(pool, n, R, 0, step)

            @block.tensor
            def _(pe):
                def step(i, j, k):
                    if runs(i, n):
                        pe.wait_ge(gathered[j], 16 * k + 16)
                        wait_count(pe, copied, i - 1)
                        for s in range(KD):
                            last = nc.tensor.transpose(K.ps[j % 2][:, s * P:(s + 1) * P], rows[:, j, s * P:(s + 1) * P],
                                                       K.ident[:, :])
                        last.then_inc(turned, 1)
                    if runs(i - 1, n):
                        c = i - 1
                        jj = (j - 1) % R
                        pe.wait_ge(copied, c + 1)
                        pe.wait_ge(fetched[jj], 48 * ((k if j else k - 1) + 1))
                        wait_count(pe, acted, c - 1)
                        for h in range(nh):
                            for s in range(KD):
                                last = nc.tensor.matmul(K.ps[2 + jj % 2][0:hm, h * P:(h + 1) * P],
                                                        w1r[:, jj, s, h * hm:(h + 1) * hm],
                                                        xT[:, jj % 2, s * P:(s + 1) * P],
                                                        start=(s == 0), stop=(s == KD - 1))
                        last.then_inc(hidden, 1)
                    if runs(i - 2, n):
                        c = i - 2
                        jj = (j - 2) % R
                        pe.wait_ge(acted, c + 1)
                        wait_count(pe, written, c - 1)
                        bank = K.ps[4 + jj % 2][:, 0:D]
                        for h in range(nh):
                            nc.tensor.matmul(bank, hT[:, jj % 2, h * P:(h + 1) * P], w2r[:, jj, h, :],
                                             start=(h == 0), stop=False)
                        nc.tensor.matmul(bank, K.ones[0:1, :], b2r[0:1, jj, :], start=False, stop=True)\
                            .then_inc(summed, 1)

                steps(pe, n, R, 2, step)

            @block.scalar
            def _(act):
                act.dma_start(b1T[:, :], b1.rearrange("e (c p) -> p (e c)", p=hm)).then_inc(biased, 16)
                act.wait_ge(biased, 16)

                def step(i, j, k):
                    e = act.value_load(r.bin[0:1, bass.ds(i, 1)], min_val=0, max_val=experts - 1)
                    act.wait_ge(hidden, i + 1)
                    wait_count(act, summed, i - 1)
                    for h in range(nh):
                        last = nc.scalar.activation(hT[:, j % 2, h * P:(h + 1) * P],
                                                    K.ps[2 + j % 2][0:hm, h * P:(h + 1) * P], func,
                                                    bias=b1T[:, bass.ds(e * nh + h, 1)])
                    last.then_inc(acted, 1)

                steps(act, n, R, 0, step)

            @block.vector
            def _(dve):
                def step(i, j, k):
                    if runs(i, n):
                        dve.wait_ge(turned, i + 1)
                        wait_count(dve, hidden, i - 1)
                        nc.vector.tensor_copy(xT[:, j % 2, :], K.ps[j % 2][:, 0:D]).then_inc(copied, 1)
                    if runs(i - 2, n):
                        jj = (j - 2) % R
                        dve.wait_ge(summed, i - 1)
                        wait_count(dve, stored[jj], 16 * (k if j >= 2 else k - 1))
                        if relu_out:
                            ins = nc.vector.tensor_scalar(yr[:, jj, :], K.ps[4 + jj % 2][:, 0:D], 0.0, None, ALU.max)
                        else:
                            ins = nc.vector.tensor_copy(yr[:, jj, :], K.ps[4 + jj % 2][:, 0:D])
                        ins.then_inc(written, 1)

                steps(dve, n, R, 2, step)


def combine(nc, K, slots, weights, first, dst):
    picks = len(slots)
    R = 2
    with stage(nc) as st:
        idxr = st.sb("idxr", [P, R * picks], I32)
        rows = st.sb("rows", [P, R * picks, D])
        gathered = [st.sem(f"gathered{j}") for j in range(R)]
        staged, passed, added = st.sem("staged"), st.sem("passed"), st.sem("added")
        with nc.Block() as block:

            @block.gpsimd
            def _(pool):
                def step(t, j, k):
                    wait_count(pool, added, picks * (t - 1))
                    for p in range(picks):
                        last = nc.gpsimd.tensor_copy(idxr[:, j * picks + p:j * picks + p + 1],
                                                     slots[p][:, bass.ds(t, 1)])
                    last.then_inc(staged, 1)
                    wait_staged(pool, staged, t + 1, passed)
                    for p in range(j * picks, (j + 1) * picks):
                        nc.gpsimd.indirect_dma_start(rows[:, p, :], None, K.slot_rows,
                                                     bass.IndirectOffsetOnAxis(ap=idxr[:, p:p + 1], axis=0))\
                            .then_inc(gathered[j], 16)

                steps(pool, NT, R, 0, step)

            @block.vector
            def _(dve):
                def step(t, j, k):
                    dve.wait_ge(gathered[j], 16 * picks * (k + 1))
                    for p in range(picks):
                        row = rows[:, j * picks + p, :]
                        onto = first if p == 0 else dst
                        if p:
                            dve.wait_ge(added, picks * t + p)
                        if weights is None:
                            ins = nc.vector.tensor_tensor(tile_of(dst, t), tile_of(onto, t), row, ALU.add)
                        else:
                            ins = nc.vector.scalar_tensor_tensor(tile_of(dst, t), row, weights[p][:, bass.ds(t, 1)],
                                                                 tile_of(onto, t), ALU.mult, ALU.add)
                        ins.then_inc(added, 1)

                steps(dve, NT, R, 0, step)


def route(nc, K, r, gate, experts, picks, mode):
    gate_w, gate_b = gate
    with stage(nc) as big:
        logits = big.sb("logits", [P, NT * experts])
        masks = [big.sb(f"mask{p}", [P, experts * NT]) for p in range(picks)]
        total = big.sb("total", [P, experts * NT]) if picks > 1 else masks[0]
        rows = [big.sb(f"rows{p}", [P, NT], I32) for p in range(picks)]
        token = big.sb("token", [P, NT])
        found = big.sb("found", [P, NT])
        found_i = big.sb("found_i", [P, NT], I32)
        dense(nc, K, [K.xn], [[gate_w]], gate_b.rearrange("(o n) -> o n", o=1), [(experts, "sb", logits, None)])
        with stage(nc) as st:
            top = st.sb("top", [P, NT * 8])
            at = st.sb("at", [P, NT * 8], U32)
            atf = st.sb("atf", [P, NT * 8])
            m = st.sb("m", [P, NT])
            z = st.sb("z", [P, NT])
            chain, asked, answered, numbered = (st.sem(x) for x in ("chain", "asked", "answered", "numbered"))
            top3 = top[:, :].rearrange("p (t e) -> p t e", e=8)
            atf3 = atf[:, :].rearrange("p (t e) -> p t e", e=8)
            lg3 = logits[:, :].rearrange("p (t e) -> p t e", e=experts)
            with nc.Block() as block:

                @block.gpsimd
                def _(pool):
                    nc.gpsimd.iota(found_i[:, :], pattern=[[P, NT]], base=0, channel_multiplier=1).then_inc(numbered, 1)

                @block.scalar
                def _(act):
                    if mode == "top_of_softmax":
                        act.wait_ge(asked, 1)
                        nc.scalar.activation(logits[:, :], logits[:, :], ACT.Exp).then_inc(answered, 1)
                    if mode == "softmax_of_top":
                        act.wait_ge(asked, 1)
                        nc.scalar.activation(m[:, :], m[:, :], ACT.Exp).then_inc(answered, 1)

                @block.vector
                def _(dve):
                    link = linker(dve, chain)
                    V = nc.vector
                    dve.wait_ge(numbered, 1)
                    link(V.tensor_copy(token[:, :], found_i[:, :]))
                    if mode == "top_of_softmax":
                        link(V.tensor_reduce(m[:, :], lg3, AX.X, ALU.max))
                        V.tensor_tensor(lg3, lg3, m[:, :].unsqueeze(2).broadcast_to([P, NT, experts]),
                                        ALU.subtract).then_inc(asked, 1)
                        dve.wait_ge(answered, 1)
                        link(V.tensor_reduce(z[:, :], lg3, AX.X, ALU.add))
                        link(V.reciprocal(z[:, :], z[:, :]))
                        link(V.tensor_tensor(lg3, lg3, z[:, :].unsqueeze(2).broadcast_to([P, NT, experts]), ALU.mult))
                    for t in range(NT):
                        last = V.max(top3[:, t, :], lg3[:, t, :])
                    link(last)
                    for t in range(NT):
                        last = V.max_index(at[:, 8 * t:8 * t + 8], top3[:, t, :], lg3[:, t, :])
                    link(last)
                    link(V.tensor_copy(atf[:, :], at[:, :]))
                    for p in range(picks):
                        for e in range(experts):
                            last = V.tensor_scalar(masks[p][:, e * NT:(e + 1) * NT], atf3[:, :, p], float(e), None,
                                                   ALU.is_equal)
                    link(last)
                    if picks > 1:
                        link(V.tensor_tensor(total[:, :], masks[0][:, :], masks[1][:, :], ALU.add))
                    if mode == "top_of_softmax":
                        V.tensor_copy(r.weights[0][:, :], top3[:, :, 0])
                        link(V.tensor_copy(r.weights[1][:, :], top3[:, :, 1]))
                    if mode == "softmax_of_top":
                        V.tensor_tensor(m[:, :], top3[:, :, 1], top3[:, :, 0], ALU.subtract).then_inc(asked, 1)
                        dve.wait_ge(answered, 1)
                        link(V.tensor_scalar(z[:, :], m[:, :], 1.0, None, ALU.add))
                        link(V.reciprocal(r.weights[0][:, :], z[:, :]))
                        link(V.tensor_tensor(r.weights[1][:, :], r.weights[0][:, :], m[:, :], ALU.mult))

        place(nc, K, total[:, :], [(masks[p][:, :], rows[p][:, :], r.slots[p][:, :]) for p in range(picks)],
              P, experts, NT, r.chunks, r.bin[:, 0:r.chunks])
        with stage(nc) as st2:
            back = st2.sb("back", [P, r.chunks])
            scatter_items(nc, K, [(rows[p], token) for p in range(picks)], P, NT, 5, 1, 1, r.chunks, (0.0,), back[:, :])
            vector_work(nc, lambda: nc.vector.tensor_copy(r.idx[:, 0:r.chunks], back[:, :]))


def moe(nc, K, gate, w1, b1, w2, b2, picks, mode, func, relu_out=False, after=None):
    experts = w1.shape[0]
    with stage(nc) as st:
        r = Routing(st, picks, experts, mode is not None)
        layer_norm(nc, K, K.x, K.xn, table=K.table)
        route(nc, K, r, gate, experts, picks, mode)
        routed_ffn(nc, K, r, w1, b1, w2, b2, func, relu_out)
        if after is None:
            combine(nc, K, r.slots, r.weights, K.x, K.x)
        else:
            combine(nc, K, r.slots, r.weights, K.xn, K.agg)
            layer_norm(nc, K, K.agg, K.agg, affine=after, residual=True)


def gather_rows(nc, pool, edges, table, rows, idxr, gathered, staged, passed, used, half):
    def step(i, j, k):
        wait_count(pool, used, half * (i - 1))
        nc.gpsimd.tensor_copy(idxr[:, j * half:(j + 1) * half], edges.idx[:, bass.ds(i * half, half)]).then_inc(staged, 1)
        wait_staged(pool, staged, i + 1, passed)
        for g in range(j * half, (j + 1) * half):
            nc.gpsimd.indirect_dma_start(rows[:, g, :], None, table,
                                         bass.IndirectOffsetOnAxis(ap=idxr[:, g:g + 1], axis=0)).then_inc(gathered[g], 16)

    steps(pool, CHUNKS // half, 2, 0, step)


def attention_scores(nc, K, edges, q, k_table, scores, m):
    R, G = 4, 8
    with stage(nc) as st:
        idxr = st.sb("idxr", [P, G], I32)
        rows = st.sb("rows", [P, G, D])
        hot = st.sb("hot", [P, R, P])
        cold = st.sb("cold", [P, R, P], BF)
        hotT = st.sb("hotT", [P, 2, P])
        prod = st.sb("prod", [P, 2, D])
        sc = st.sb("sc", [P, R, HEADS])
        mc = st.sb("mc", [P, 2, HEADS])
        gathered = [st.sem(f"gathered{j}") for j in range(G)]
        staged, passed, onehot, turned, copied, queried, product, scored, kept, masked, peak, merged, cleared = (
            st.sem(x) for x in ("staged", "passed", "onehot", "turned", "copied", "queried", "product", "scored", "kept",
                                "masked", "peak", "merged", "cleared"))
        with nc.Block() as block:

            @block.gpsimd
            def _(pool):
                gather_rows(nc, pool, edges, k_table, rows, idxr, gathered, staged, passed, scored, G // 2)

            @block.vector
            def _(dve):
                nc.vector.memset(m[:, :], -BIG).then_inc(cleared, 1)
                dve.wait_ge(cleared, 1)

                def step(i, j, k):
                    if runs(i, CHUNKS):
                        wait_count(dve, masked, i - R + 1)
                        at = edges.pay[:, bass.ds(3 * i + 1, 1)]
                        nc.vector.tensor_scalar(hot[:, j % R, :], K.iota[:, 0:P], at, None, ALU.is_equal)
                        nc.vector.tensor_scalar(cold[:, j % R, :], K.iota[:, 0:P], at, -BIG, ALU.not_equal,
                                                ALU.mult).then_inc(onehot, 1)
                    if runs(i - 2, CHUNKS):
                        c, jj = i - 2, (j - 2) % G
                        dve.wait_ge(queried, c + 1)
                        dve.wait_ge(gathered[jj], 16 * ((k if j >= 2 else k - 1) + 1))
                        nc.vector.tensor_tensor(prod[:, jj % 2, :], K.ps[2 + jj % 2][:, 0:D], rows[:, jj, :],
                                                ALU.mult).then_inc(product, 1)
                        dve.wait_ge(product, c + 1)
                        wait_count(dve, kept, c - R + 1)
                        nc.vector.tensor_reduce(sc[:, jj % R, :], prod[:, jj % 2, :].rearrange("p (h d) -> p h d", h=HEADS),
                                                AX.X, ALU.add).then_inc(scored, 1)
                    if runs(i - 4, CHUNKS):
                        c, jj = i - 4, (j - 4) % G
                        t = dve.value_load(edges.bin[0:1, bass.ds(c, 1)], min_val=0, max_val=NT - 1)
                        dve.wait_ge(masked, c + 1)
                        b = 4 + 2 * (jj % 2)
                        for hh in range(2):
                            last = nc.vector.tensor_reduce(mc[:, jj % 2, hh * 4:hh * 4 + 4],
                                                           K.ps[b + hh][:, :].rearrange("p (h e) -> p h e", h=4),
                                                           AX.X, ALU.max)
                        last.then_inc(peak, 1)
                        dve.wait_ge(peak, c + 1)
                        wait_count(dve, merged, c)
                        nc.vector.tensor_tensor(tile_of(m, t, HEADS), tile_of(m, t, HEADS), mc[:, jj % 2, :],
                                                ALU.max).then_inc(merged, 1)

                steps(dve, CHUNKS, G, 4, step)

            @block.tensor
            def _(pe):
                def step(i, j, k):
                    if runs(i, CHUNKS):
                        pe.wait_ge(onehot, i + 1)
                        wait_count(pe, copied, i - 1)
                        nc.tensor.transpose(K.ps[j % 2][:, 0:P], hot[:, j, :], K.ident[:, :]).then_inc(turned, 1)
                    if runs(i - 1, CHUNKS):
                        c, jj = i - 1, (j - 1) % R
                        t = pe.value_load(edges.bin[0:1, bass.ds(c, 1)], min_val=0, max_val=NT - 1)
                        pe.wait_ge(copied, c + 1)
                        wait_count(pe, product, c - 1)
                        nc.tensor.matmul(K.ps[2 + jj % 2][:, 0:D], hotT[:, jj % 2, :], tile_of(q, t),
                                         start=True, stop=True).then_inc(queried, 1)
                    if runs(i - 3, CHUNKS):
                        c, jj = i - 3, (j - 3) % R
                        pe.wait_ge(scored, c + 1)
                        wait_count(pe, peak, c - 1)
                        b = 4 + 2 * (jj % 2)
                        for hh in range(2):
                            nc.tensor.matmul(K.ps[b + hh][:, :], cold[:, jj, :], K.ident8[:, hh * 512:hh * 512 + 512],
                                             start=True, stop=False)
                            for h in range(4):
                                last = nc.tensor.matmul(K.ps[b + hh][:, h * P:(h + 1) * P],
                                                        sc[:, jj, hh * 4 + h:hh * 4 + h + 1].broadcast_to([P, P]),
                                                        K.ident[:, :], start=False, stop=(h == 3))
                        last.then_inc(masked, 1)

                steps(pe, CHUNKS, R, 3, step)

            @block.scalar
            def _(act):
                def step(i, j, k):
                    if runs(i, CHUNKS):
                        act.wait_ge(turned, i + 1)
                        wait_count(act, queried, i - 1)
                        nc.scalar.activation(hotT[:, j % 2, :], K.ps[j % 2][:, 0:P], ACT.Copy).then_inc(copied, 1)
                    if runs(i - 2, CHUNKS):
                        c, jj = i - 2, (j - 2) % R
                        act.wait_ge(scored, c + 1)
                        nc.scalar.activation(scores[:, bass.ds(c * HEADS, HEADS)], sc[:, jj, :], ACT.Copy).then_inc(kept, 1)

                steps(act, CHUNKS, R, 2, step)


def attention_values(nc, K, edges, v_table, scores, m, acc):
    R, G, W = 4, 8, D + HEADS
    with stage(nc) as st:
        idxr = st.sb("idxr", [P, G], I32)
        rows = st.sb("rows", [P, G, D])
        hot = st.sb("hot", [P, R, P])
        hotT = st.sb("hotT", [P, 2, P])
        diff = st.sb("diff", [P, 2, HEADS])
        msg = st.sb("msg", [P, R, W])
        gathered = [st.sem(f"gathered{j}") for j in range(G)]
        staged, passed, onehot, turned, copied, peaked, shifted, raised, weighed, summed, added, cleared = (
            st.sem(x) for x in ("staged", "passed", "onehot", "turned", "copied", "peaked", "shifted", "raised", "weighed",
                                "summed", "added", "cleared"))
        with nc.Block() as block:

            @block.gpsimd
            def _(pool):
                gather_rows(nc, pool, edges, v_table, rows, idxr, gathered, staged, passed, weighed, G // 2)

            @block.vector
            def _(dve):
                nc.vector.memset(acc[:, :], 0.0).then_inc(cleared, 1)
                dve.wait_ge(cleared, 1)

                def step(i, j, k):
                    if runs(i, CHUNKS):
                        wait_count(dve, summed, i - R + 1)
                        nc.vector.tensor_scalar(hot[:, j % R, :], K.iota[:, 0:P], edges.pay[:, bass.ds(3 * i + 1, 1)],
                                                None, ALU.is_equal).then_inc(onehot, 1)
                    if runs(i - 2, CHUNKS):
                        c, jj = i - 2, (j - 2) % G
                        dve.wait_ge(peaked, c + 1)
                        wait_count(dve, raised, c - 1)
                        nc.vector.tensor_tensor(diff[:, jj % 2, :], scores[:, bass.ds(c * HEADS, HEADS)],
                                                K.ps[2 + jj % 2][:, 0:HEADS], ALU.subtract).then_inc(shifted, 1)
                    if runs(i - 3, CHUNKS):
                        c, jj = i - 3, (j - 3) % G
                        dve.wait_ge(raised, c + 1)
                        dve.wait_ge(gathered[jj], 16 * ((k if j >= 3 else k - 1) + 1))
                        nc.vector.tensor_tensor(msg[:, jj % R, 0:D].rearrange("p (h d) -> p h d", h=HEADS),
                                                rows[:, jj, :].rearrange("p (h d) -> p h d", h=HEADS),
                                                msg[:, jj % R, D:W].unsqueeze(2).broadcast_to([P, HEADS, DH]),
                                                ALU.mult).then_inc(weighed, 1)
                    if runs(i - 4, CHUNKS):
                        c, jj = i - 4, (j - 4) % G
                        t = dve.value_load(edges.bin[0:1, bass.ds(c, 1)], min_val=0, max_val=NT - 1)
                        dve.wait_ge(summed, c + 1)
                        wait_count(dve, added, c)
                        nc.vector.tensor_tensor(tile_of(acc, t, W), tile_of(acc, t, W), K.ps[4 + jj % 2][:, 0:W],
                                                ALU.add).then_inc(added, 1)

                steps(dve, CHUNKS, G, 4, step)

            @block.tensor
            def _(pe):
                def step(i, j, k):
                    if runs(i, CHUNKS):
                        pe.wait_ge(onehot, i + 1)
                        wait_count(pe, copied, i - 1)
                        nc.tensor.transpose(K.ps[j % 2][:, 0:P], hot[:, j, :], K.ident[:, :]).then_inc(turned, 1)
                    if runs(i - 1, CHUNKS):
                        c, jj = i - 1, (j - 1) % R
                        t = pe.value_load(edges.bin[0:1, bass.ds(c, 1)], min_val=0, max_val=NT - 1)
                        pe.wait_ge(copied, c + 1)
                        wait_count(pe, shifted, c - 1)
                        nc.tensor.matmul(K.ps[2 + jj % 2][:, 0:HEADS], hotT[:, jj % 2, :], tile_of(m, t, HEADS),
                                         start=True, stop=True).then_inc(peaked, 1)
                    if runs(i - 3, CHUNKS):
                        c, jj = i - 3, (j - 3) % R
                        pe.wait_ge(weighed, c + 1)
                        wait_count(pe, added, c - 1)
                        nc.tensor.matmul(K.ps[4 + jj % 2][:, 0:W], hot[:, jj, :], msg[:, jj, :],
                                         start=True, stop=True).then_inc(summed, 1)

                steps(pe, CHUNKS, R, 3, step)

            @block.scalar
            def _(act):
                def step(i, j, k):
                    if runs(i, CHUNKS):
                        act.wait_ge(turned, i + 1)
                        wait_count(act, peaked, i - 1)
                        nc.scalar.activation(hotT[:, j % 2, :], K.ps[j % 2][:, 0:P], ACT.Copy).then_inc(copied, 1)
                    if runs(i - 2, CHUNKS):
                        c, jj = i - 2, (j - 2) % G
                        act.wait_ge(shifted, c + 1)
                        wait_count(act, summed, c - R + 1)
                        nc.scalar.activation(msg[:, jj % R, D:W], diff[:, jj % 2, :], ACT.Exp).then_inc(raised, 1)

                steps(act, CHUNKS, G, 2, step)


def node_mlp(nc, K, src, w1, b1, w2, b2):
    hid = w1.shape[1]
    nh = hid // P
    with stage(nc) as st:
        w1s = st.sb("w1s", [P, KD, hid])
        w2s = st.sb("w2s", [P, nh, D])
        b1T = st.sb("b1T", [P, nh])
        b2s = st.sb("b2s", [1, D])
        raw = st.sb("raw", [P, 2, D])
        xT = st.sb("xT", [P, 2, D])
        hT = st.sb("hT", [P, 2, hid])
        loaded, staged, turned, copied, hidden, acted, summed, added = (
            st.sem(x) for x in ("loaded", "staged", "turned", "copied", "hidden", "acted", "summed", "added"))
        with nc.Block() as block:

            @block.sync
            def _(sp):
                sp.dma_start(w1s[:, :, :], w1.rearrange("(k p) h -> p k h", p=P)).then_inc(loaded, 16)
                sp.dma_start(w2s[:, :, :], w2.rearrange("(c p) d -> p c d", p=P)).then_inc(loaded, 16)
                sp.dma_start(b1T[:, :], b1.rearrange("(c p) -> p c", p=P)).then_inc(loaded, 16)
                sp.dma_start(b2s[:, :], b2.rearrange("(o d) -> o d", o=1)).then_inc(loaded, 16)

            @block.scalar
            def _(act):
                act.wait_ge(loaded, 64)

                def step(i, j, k):
                    act.wait_ge(hidden, i + 1)
                    wait_count(act, summed, i - 1)
                    for h in range(nh):
                        last = nc.scalar.activation(hT[:, j, h * P:(h + 1) * P],
                                                    K.ps[2 + 2 * j + h // 4][:, h % 4 * P:(h % 4 + 1) * P], ACT.Relu,
                                                    bias=b1T[:, h:h + 1])
                    last.then_inc(acted, 1)

                steps(act, NT, 2, 0, step)

            @block.tensor
            def _(pe):
                pe.wait_ge(loaded, 64)

                def step(i, j4, k):
                    j = j4 % 2
                    if runs(i, NT):
                        pe.wait_ge(staged, i + 1)
                        wait_count(pe, copied, i)
                        for s in range(KD):
                            last = nc.tensor.transpose(K.ps[0][:, s * P:(s + 1) * P], raw[:, j, s * P:(s + 1) * P],
                                                       K.ident[:, :])
                        last.then_inc(turned, 1)
                    if runs(i - 1, NT):
                        c, jj = i - 1, 1 - j
                        pe.wait_ge(copied, c + 1)
                        wait_count(pe, acted, c - 1)
                        for h in range(nh):
                            for s in range(KD):
                                last = nc.tensor.matmul(K.ps[2 + 2 * jj + h // 4][:, h % 4 * P:(h % 4 + 1) * P],
                                                        w1s[:, s, h * P:(h + 1) * P], xT[:, jj, s * P:(s + 1) * P],
                                                        start=(s == 0), stop=(s == KD - 1))
                        last.then_inc(hidden, 1)
                    if runs(i - 2, NT):
                        c, jj = i - 2, j
                        pe.wait_ge(acted, c + 1)
                        wait_count(pe, added, c - 1)
                        bank = K.ps[6 + jj][:, 0:D]
                        for h in range(nh):
                            nc.tensor.matmul(bank, hT[:, jj, h * P:(h + 1) * P], w2s[:, h, :], start=(h == 0), stop=False)
                        nc.tensor.matmul(bank, K.ones[0:1, :], b2s[0:1, :], start=False, stop=True).then_inc(summed, 1)

                steps(pe, NT, 4, 2, step)

            @block.vector
            def _(dve):
                def step(i, j4, k):
                    j = j4 % 2
                    if runs(i, NT):
                        wait_count(dve, turned, i - 1)
                        nc.vector.tensor_copy(raw[:, j, :], tile_of(src, i)).then_inc(staged, 1)
                    if runs(i - 1, NT):
                        dve.wait_ge(turned, i)
                        wait_count(dve, hidden, i - 2)
                        nc.vector.tensor_copy(xT[:, 1 - j, :], K.ps[0][:, 0:D]).then_inc(copied, 1)
                    if runs(i - 3, NT):
                        dve.wait_ge(summed, i - 2)
                        nc.vector.tensor_tensor(tile_of(K.x, i - 3), tile_of(K.x, i - 3), K.ps[6 + (1 - j)][:, 0:D],
                                                ALU.add).then_inc(added, 1)

                steps(dve, NT, 4, 3, step)


def node_to_feature(nc, K, src, w, b, dst):
    with stage(nc) as st:
        ws = st.sb("ws", [P, KD, D])
        bs = st.sb("bs", [P, KD])
        raw = st.sb("raw", [P, 2, D])
        xT = st.sb("xT", [P, 2, D])
        loaded, staged, turned, copied, summed, written = (
            st.sem(x) for x in ("loaded", "staged", "turned", "copied", "summed", "written"))
        with nc.Block() as block:

            @block.sync
            def _(sp):
                sp.dma_start(ws[:, :, :], w.rearrange("(k p) n -> p k n", p=P)).then_inc(loaded, 16)
                sp.dma_start(bs[:, :], b.rearrange("(k p) -> p k", p=P)).then_inc(loaded, 16)

            @block.scalar
            def _(act):
                def step(i, j, k):
                    if runs(i, NT):
                        wait_count(act, turned, i - 1)
                        nc.scalar.activation(raw[:, j, :], tile_of(src, i), ACT.Copy).then_inc(staged, 1)
                    if runs(i - 1, NT):
                        act.wait_ge(turned, i)
                        wait_count(act, summed, i - 2)
                        nc.scalar.activation(xT[:, 1 - j, :], K.ps[1 - j][:, 0:D], ACT.Copy).then_inc(copied, 1)

                steps(act, NT, 2, 1, step)

            @block.tensor
            def _(pe):
                pe.wait_ge(loaded, 32)

                def step(i, j, k):
                    if runs(i, NT):
                        pe.wait_ge(staged, i + 1)
                        wait_count(pe, copied, i - 1)
                        for s in range(KD):
                            last = nc.tensor.transpose(K.ps[j][:, s * P:(s + 1) * P], raw[:, j, s * P:(s + 1) * P],
                                                       K.ident[:, :])
                        last.then_inc(turned, 1)
                    if runs(i - 1, NT):
                        pe.wait_ge(copied, i)
                        wait_count(pe, written, i - 2)
                        for o in range(KD):
                            for s in range(KD):
                                last = nc.tensor.matmul(K.ps[2 + 2 * (1 - j) + o][:, 0:P], ws[:, s, o * P:(o + 1) * P],
                                                        xT[:, 1 - j, s * P:(s + 1) * P], start=(s == 0), stop=(s == KD - 1))
                        last.then_inc(summed, 1)

                steps(pe, NT, 2, 1, step)

            @block.vector
            def _(dve):
                dve.wait_ge(loaded, 32)

                def step(t, j, k):
                    dve.wait_ge(summed, t + 1)
                    for o in range(KD):
                        last = nc.vector.tensor_scalar(dst[:, bass.ds(t * P + o * NPAD, P)], K.ps[2 + 2 * j + o][:, 0:P],
                                                       bs[:, o:o + 1], None, ALU.add)
                    last.then_inc(written, 1)

                steps(dve, NT, 2, 0, step)


def feature_to_feature(nc, K, src, w, b, dst):
    with stage(nc) as st:
        ws = st.sb("ws", [P, KD, D])
        bs = st.sb("bs", [P, KD])
        loaded, summed, written = (st.sem(x) for x in ("loaded", "summed", "written"))
        with nc.Block() as block:

            @block.sync
            def _(sp):
                sp.dma_start(ws[:, :, :], w.rearrange("(k p) n -> p k n", p=P)).then_inc(loaded, 16)
                sp.dma_start(bs[:, :], b.rearrange("(k p) -> p k", p=P)).then_inc(loaded, 16)

            @block.tensor
            def _(pe):
                pe.wait_ge(loaded, 32)

                def step(t, j, k):
                    wait_count(pe, written, t - 1)
                    for o in range(KD):
                        for s in range(KD):
                            last = nc.tensor.matmul(K.ps[2 * j + o][:, 0:P], ws[:, s, o * P:(o + 1) * P],
                                                    src[:, bass.ds(t * P + s * NPAD, P)], start=(s == 0), stop=(s == KD - 1))
                    last.then_inc(summed, 1)

                steps(pe, NT, 2, 0, step)

            @block.vector
            def _(dve):
                dve.wait_ge(loaded, 32)

                def step(t, j, k):
                    dve.wait_ge(summed, t + 1)
                    for o in range(KD):
                        last = nc.vector.tensor_scalar(dst[:, bass.ds(t * P + o * NPAD, P)], K.ps[2 * j + o][:, 0:P],
                                                       bs[:, o:o + 1], None, ALU.add)
                    last.then_inc(written, 1)

                steps(dve, NT, 2, 0, step)


def batch_norm_scale(nc, K, src, gamma, beta, scale, shift):
    CH = 512
    spans = [(a, min(CH, NODES - a)) for a in range(0, NODES, CH)]
    with stage(nc) as st:
        stats = st.sb("stats", [P, KD, len(spans) * 6])
        mv = st.sb("mv", [P, KD, 2])
        gb = st.sb("gb", [P, 2, KD])
        rstd = st.sb("rstd", [P, KD])
        tmp = st.sb("tmp", [P, KD])
        loaded, chain, asked, root = (st.sem(x) for x in ("loaded", "chain", "asked", "root"))
        with nc.Block() as block:

            @block.sync
            def _(sp):
                sp.dma_start(gb[:, 0, :], gamma.rearrange("(k p) -> p k", p=P)).then_inc(loaded, 16)
                sp.dma_start(gb[:, 1, :], beta.rearrange("(k p) -> p k", p=P)).then_inc(loaded, 16)

            @block.scalar
            def _(act):
                act.wait_ge(asked, 1)
                nc.scalar.activation(rstd[:, :], rstd[:, :], ACT.Sqrt).then_inc(root, 1)

            @block.vector
            def _(dve):
                link = linker(dve, chain)
                V = nc.vector
                for o in range(KD):
                    for n, (a, w) in enumerate(spans):
                        last = V.bn_stats(stats[:, o, 6 * n:6 * n + 6], src[:, o * NPAD + a:o * NPAD + a + w])
                link(last)
                for o in range(KD):
                    last = V.bn_aggr(mv[:, o, :], stats[:, o, :])
                link(last)
                V.tensor_scalar(rstd[:, :], mv[:, :, 1], EPS, None, ALU.add).then_inc(asked, 1)
                dve.wait_ge(root, 1)
                dve.wait_ge(loaded, 32)
                link(V.reciprocal(rstd[:, :], rstd[:, :]))
                link(V.tensor_tensor(scale[:, :], rstd[:, :], gb[:, 0, :], ALU.mult))
                link(V.tensor_tensor(tmp[:, :], scale[:, :], mv[:, :, 0], ALU.mult))
                link(V.tensor_tensor(shift[:, :], gb[:, 1, :], tmp[:, :], ALU.subtract))


def batch_norm_relu(nc, K, buf, scale, shift):
    with stage(nc) as st:
        done = st.sem("done")
        with nc.Block() as block:

            @block.scalar
            def _(act):
                for o in range(KD):
                    nc.scalar.activation(buf[:, o * NPAD:(o + 1) * NPAD], buf[:, o * NPAD:(o + 1) * NPAD], ACT.Relu,
                                         bias=shift[:, o:o + 1], scale=scale[:, o:o + 1]).then_inc(done, 1)


def batch_norm_relu_to_nodes(nc, K, src, scale, shift, h, table):
    with stage(nc) as st:
        raw = st.sb("raw", [P, 2, D])
        normed, turned, written, stored = (st.sem(x) for x in ("normed", "turned", "written", "stored"))
        with nc.Block() as block:

            @block.scalar
            def _(act):
                def step(t, j, k):
                    wait_count(act, turned, t - 1)
                    for o in range(KD):
                        last = nc.scalar.activation(raw[:, j, o * P:(o + 1) * P], src[:, bass.ds(t * P + o * NPAD, P)],
                                                    ACT.Relu, bias=shift[:, o:o + 1], scale=scale[:, o:o + 1])
                    last.then_inc(normed, 1)

                steps(act, NT, 2, 0, step)

            @block.tensor
            def _(pe):
                def step(t, j, k):
                    pe.wait_ge(normed, t + 1)
                    wait_count(pe, written, t - 1)
                    for o in range(KD):
                        last = nc.tensor.transpose(K.ps[j][:, o * P:(o + 1) * P], raw[:, j, o * P:(o + 1) * P], K.ident[:, :])
                    last.then_inc(turned, 1)

                steps(pe, NT, 2, 0, step)

            @block.vector
            def _(dve):
                def step(t, j, k):
                    dve.wait_ge(turned, t + 1)
                    if h is None:
                        ins = nc.vector.tensor_tensor(tile_of(K.x, t), tile_of(K.x, t), K.ps[j][:, 0:D], ALU.add)
                    else:
                        ins = nc.vector.tensor_copy(tile_of(h, t), K.ps[j][:, 0:D])
                    ins.then_inc(written, 1)

                steps(dve, NT, 2, 0, step)

            @block.sync
            def _(sp):
                if h is not None:
                    def step(t, j, k):
                        sp.wait_ge(written, t + 1)
                        sp.dma_start(tile_rows(table, t), tile_of(h, t)).then_inc(stored, 16)

                    steps(sp, NT, 2, 0, step)
                    sp.wait_ge(stored, 16 * NT)


def layer0_gnn(nc, K, A):
    layer_norm(nc, K, K.x, K.xn, table=K.table)
    spmm(nc, K, K.by_src, K.table, K.agg)
    dense(nc, K, [K.agg], [[A["L0_gnn_weight"]]], None, [(D, "relu_add", None, None)])


def layer1_gnn(nc, K, A):
    layer_norm(nc, K, K.x, K.xn, table=K.table)
    spmm(nc, K, K.by_src, K.table, K.agg)
    dense(nc, K, [K.xn, K.agg], [[A["L1_gnn_weight"][0:D, :]], [A["L1_gnn_weight"][D:2 * D, :]]],
          A["L1_gnn_bias"].rearrange("(o n) -> o n", o=1), [(D, "add", None, None)])


def layer2_gnn(nc, K, A):
    layer_norm(nc, K, K.x, K.xn)
    W = D + HEADS
    with stage(nc) as st:
        q = st.sb("q", [P, NT * D])
        scores = st.sb("scores", [P, CHUNKS * HEADS])
        m = st.sb("m", [P, NT * HEADS])
        acc = st.sb("acc", [P, NT * W])
        acc4 = acc[:, :].rearrange("p (t w) -> p t w", w=W)
        z = st.sb("z", [P, NT * HEADS])
        z3 = z[:, :].rearrange("p (t h) -> p t h", h=HEADS)
        agg4 = K.agg[:, :].rearrange("p (t h d) -> p t h d", t=NT, h=HEADS)
        for l in range(2):
            dense(nc, K, [K.xn], [[A["L2_gnn_Wq"][l], A["L2_gnn_Wk"][l], A["L2_gnn_Wv"][l]]], None,
                  [(D, "sb", q, float(DH) ** -0.5), (D, "table", K.table, None), (D, "table", K.table2, None)])
            attention_scores(nc, K, K.by_dst, q, K.table, scores, m)
            attention_values(nc, K, K.by_dst, K.table2, scores, m, acc)
            vector_work(
                nc,
                lambda: nc.vector.tensor_scalar(z3, acc4[:, :, D:W], 1e-9, None, ALU.add),
                lambda: nc.vector.reciprocal(z[:, :], z[:, :]),
                lambda: nc.vector.tensor_tensor(agg4, acc4[:, :, 0:D].rearrange("p t (h d) -> p t h d", h=HEADS),
                                                z3.unsqueeze(3).broadcast_to([P, NT, HEADS, DH]), ALU.mult))
            dense(nc, K, [K.agg], [[A["L2_gnn_Wo"][l]]], None, [(D, "sb", q, None)])
            vector_work(nc, lambda: nc.vector.tensor_tensor(K.xn[:, :], K.xn[:, :], q[:, :], ALU.add))
            layer_norm(nc, K, K.xn, K.xn, affine=(A["L2_gnn_ln_g"][l], A["L2_gnn_ln_b"][l]))
    node_mlp(nc, K, K.xn, A["L2_gnn_w1"], A["L2_gnn_b1"], A["L2_gnn_w2"], A["L2_gnn_b2"])


def layer3_gnn(nc, K, A):
    layer_norm(nc, K, K.x, K.xn)
    with stage(nc) as st:
        yT = st.sb("yT", [P, KD * NPAD])
        scale = st.sb("scale", [P, KD])
        shift = st.sb("shift", [P, KD])
        dense(nc, K, [K.xn], [[A["L3_gnn_W_in"]]], A["L3_gnn_b_in"].rearrange("(o n) -> o n", o=1),
              [(D, "both", (K.xn, K.table), None)])
        layers = A["L3_gnn_W1"].shape[0]
        for l in range(layers):
            spmm(nc, K, K.by_src, K.table, K.agg)
            vector_work(nc, lambda: nc.vector.tensor_tensor(K.agg[:, :], K.agg[:, :], K.xn[:, :], ALU.add))
            node_to_feature(nc, K, K.agg, A["L3_gnn_W1"][l], A["L3_gnn_b1"][l], yT)
            batch_norm_scale(nc, K, yT, A["L3_gnn_g1"][l], A["L3_gnn_be1"][l], scale, shift)
            batch_norm_relu(nc, K, yT, scale, shift)
            feature_to_feature(nc, K, yT, A["L3_gnn_W2"][l], A["L3_gnn_b2"][l], K.agg)
            batch_norm_scale(nc, K, K.agg, A["L3_gnn_g_out"][l], A["L3_gnn_b_out"][l], scale, shift)
            last = l == layers - 1
            batch_norm_relu_to_nodes(nc, K, K.agg, scale, shift, None if last else K.xn, K.table)


def build(nc, A, out, upto=99):
    with stage(nc) as st:
        st.stack.enter_context(nc.allow_non_contiguous_dma(reason="short rows of biases and of the L3 router"))
        K = Core(nc, st)
        make_constants(nc, K)
        sort_edges(nc, K, A["src"], A["dst"], A["edge_weight"], K.by_src)
        sort_edges(nc, K, A["dst"], A["src"], A["edge_weight"], K.by_dst)
        K.x, K.xn, K.agg = (st.sb(n, [P, NT * D]) for n in ("x", "xn", "agg"))
        load_nodes(nc, K, A["x"])
        layers = [
            lambda: layer0_gnn(nc, K, A),
            lambda: moe(nc, K, (A["L0_ffn_gate_w"], A["L0_ffn_gate_b"]), A["L0_ffn_w1"], A["L0_ffn_b1"], A["L0_ffn_w2"], A["L0_ffn_b2"],
                        2, "softmax_of_top", ACT.Relu, after=(A["L0_ffn_gamma"], A["L0_ffn_beta"])),
            lambda: layer1_gnn(nc, K, A),
            lambda: moe(nc, K, (A["L1_ffn_Wg"], A["L1_ffn_bg"]), A["L1_ffn_W1"], A["L1_ffn_b1"], A["L1_ffn_W2"], A["L1_ffn_b2"],
                        2, None, ACT.Gelu),
            lambda: layer2_gnn(nc, K, A),
            lambda: moe(nc, K, (A["L2_ffn_gate_w"], A["L2_ffn_gate_b"]), A["L2_ffn_W1"], A["L2_ffn_b1"], A["L2_ffn_W2"], A["L2_ffn_b2"],
                        2, "top_of_softmax", ACT.Gelu),
            lambda: layer3_gnn(nc, K, A),
            lambda: moe(nc, K, (A["L3_ffn_router_w"].rearrange("e d -> d e"), A["L3_ffn_router_b"]), A["L3_ffn_W1"], A["L3_ffn_b1"],
                        A["L3_ffn_W2"], A["L3_ffn_b2"], 1, None, ACT.Relu, relu_out=True),
        ]
        for layer in layers[:upto]:
            layer()
        store_nodes(nc, K, out)


def kernel(**inputs):
    import numpy as np
    import concourse.bacc as bacc
    from concourse.bass_utils import run_bass_kernel_spmd

    nc = bacc.Bacc("TRN2", target_bir_lowering=False, num_devices=1)
    arrays, A = {}, {}
    for name, value in inputs.items():
        a = np.ascontiguousarray(value)
        arrays[f"in_{name}"] = a
        A[name] = nc.dram_tensor(f"in_{name}", a.shape, mybir.dt.from_np(a.dtype), kind="ExternalInput").ap()
    out = nc.dram_tensor("out", (NODES, D), FP, kind="ExternalOutput").ap()
    build(nc, A, out)
    r = run_bass_kernel_spmd(nc, [arrays], core_ids=[0])
    return r.results[0]["out"]
```

```python
import concourse.bass as bass
from concourse import mybir
from contextlib import ExitStack, contextmanager

FP = mybir.dt.float32
BF = mybir.dt.bfloat16
I32 = mybir.dt.int32
U32 = mybir.dt.uint32
ALU = mybir.AluOpType
ACT = mybir.ActivationFunctionType
AX = mybir.AxisListType

P = 128
D = 256
KD = D // P
NODES = 3125
NT = (NODES + P - 1) // P
NPAD = NT * P
LAST = NODES - (NT - 1) * P
EDGES = 50000
EP = 125
EC = EDGES // EP
EU = 16
CHUNKS = -(-((EDGES + NT * (P - 1)) // P) // EU) * EU
HEADS = 8
DH = D // HEADS
EPS = 1e-5
BIG = float(2.0 ** 99)
BLOCKS = P // HEADS
PER = -(-CHUNKS // BLOCKS)
SPAN = PER * P
RUNS = 4
GS = 4


def token_chunks(picks, experts):
    return (picks * NPAD + experts * (P - 1)) // P


def steps(eng, n, unroll, lag, step):
    for i in range(unroll):
        step(i, i, 0)
    with eng.Fori(1, n // unroll) as k:
        for j in range(unroll):
            step(unroll * k + j, j, k)
    for i in range(n // unroll * unroll, n + lag):
        step(i, i % unroll, i // unroll)


def runs(c, n):
    return not isinstance(c, int) or 0 <= c < n


def wait_count(eng, sem, count):
    if not isinstance(count, int) or count > 0:
        eng.wait_ge(sem, count)


def wait_staged(pool, sem, count, passed):
    pool.wait_ge(sem, count)
    pool.sem_inc(passed, 1)


def linker(eng, sem):
    n = [0]

    def link(ins):
        n[0] += 1
        ins.then_inc(sem, 1)
        eng.wait_ge(sem, n[0])

    return link


class Stage:

    def __init__(self, nc, stack):
        self.nc, self.stack, self.sems = nc, stack, []

    def sem(self, name):
        self.sems.append(self.nc.alloc_semaphore(f"{name}_{self.nc.next_id()}"))
        return self.sems[-1]

    def sb(self, name, shape, dt=FP):
        return self.stack.enter_context(self.nc.sbuf_tensor(f"{name}_{self.nc.next_id()}", shape, dt))


@contextmanager
def stage(nc):
    with ExitStack() as stack:
        st = Stage(nc, stack)
        yield st
        if st.sems:
            nc.clear_and_free_semaphores(st.sems)
            nc.all_engine_barrier(sem_only=True)


class Edges:

    def __init__(self, st, name):
        self.idx = st.sb(name + "_idx", [P, CHUNKS], I32)
        self.same = st.sb(name + "_same", [P, CHUNKS])
        self.pay = st.sb(name + "_pay", [P, CHUNKS * 3])
        self.bin = st.sb(name + "_bin", [1, CHUNKS], I32)


class Routing:

    def __init__(self, st, picks, experts, weighted):
        self.chunks = token_chunks(picks, experts)
        self.bin = st.sb("bin", [1, self.chunks], I32)
        self.idx = st.sb("idx", [P, self.chunks], I32)
        self.slots = [st.sb(f"slots{p}", [P, NT], I32) for p in range(picks)]
        self.weights = [st.sb(f"weight{p}", [P, NT]) for p in range(picks)] if weighted else None


class Core:

    def __init__(self, nc, st):
        self.iota = st.sb("iota", [P, CHUNKS])
        self.ident = st.sb("ident", [P, P])
        self.ident_bf = st.sb("ident_bf", [P, P], BF)
        self.ones = st.sb("ones", [P, P])
        self.before = st.sb("before", [P, P])
        self.ps = [st.stack.enter_context(nc.psum_tensor(f"bank{i}", [P, 512], FP)) for i in range(8)]
        self.table = nc.dram_tensor("table", (NPAD, D), FP, kind="Internal").ap()
        self.table2 = nc.dram_tensor("table2", (NPAD, D), FP, kind="Internal").ap()
        self.slot_rows = nc.dram_tensor("slot_rows", (token_chunks(2, 16) * P, D), FP, kind="Internal").ap()
        self.slot_table = nc.dram_tensor("slot_table", (CHUNKS * P * 3,), FP, kind="Internal").ap()
        self.by_src = Edges(st, "by_src")
        self.by_dst = Edges(st, "by_dst")


def tile_of(buf, t, width=D):
    return buf[:, bass.ds(t * width, width)]


def tile_rows(table, t):
    return table[bass.ds(t * P, P), :]


def make_constants(nc, K):
    with stage(nc) as st:
        ii = st.sb("ii", [P, CHUNKS], I32)
        made, ready, chain = st.sem("made"), st.sem("ready"), st.sem("chain")
        with nc.Block() as block:

            @block.gpsimd
            def _(pool):
                nc.gpsimd.iota(ii[:, :], pattern=[[1, CHUNKS]], base=0, channel_multiplier=0).then_inc(made, 1)
                nc.gpsimd.memset(K.ident[:, :], 0.0).then_inc(chain, 1)
                nc.gpsimd.memset(K.ones[:, :], 1.0).then_inc(chain, 1)
                pool.wait_ge(chain, 2)
                nc.gpsimd.affine_select(out=K.ident[:, :], in_=K.ident[:, :], compare_op=ALU.not_equal, fill=1.0,
                                        base=0, pattern=[[-1, P]], channel_multiplier=1).then_inc(made, 1)
                nc.gpsimd.affine_select(out=K.before[:, :], in_=K.ones[:, :], compare_op=ALU.is_ge, fill=0.0,
                                        base=-1, pattern=[[1, P]], channel_multiplier=-1).then_inc(made, 1)

            @block.vector
            def _(dve):
                dve.wait_ge(made, 3)
                nc.vector.tensor_copy(K.iota[:, :], ii[:, :])
                nc.vector.tensor_copy(K.ident_bf[:, :], K.ident[:, :]).then_inc(ready, 1)


def load_nodes(nc, K, x):
    with stage(nc) as st:
        zeroed, loaded = st.sem("zeroed"), st.sem("loaded")
        with nc.Block() as block:

            @block.vector
            def _(dve):
                nc.vector.memset(tile_of(K.x, NT - 1), 0.0).then_inc(zeroed, 1)

            @block.sync
            def _(sp):
                sp.dma_start(K.x[:, 0:(NT - 1) * D].rearrange("p (t d) -> p t d", d=D),
                             x[0:(NT - 1) * P, :].rearrange("(t p) d -> p t d", p=P)).then_inc(loaded, 16)
                sp.wait_ge(zeroed, 1)
                sp.dma_start(K.x[0:LAST, (NT - 1) * D:NT * D], x[(NT - 1) * P:NODES, :]).then_inc(loaded, 16)
                sp.wait_ge(loaded, 32)


def store_nodes(nc, K, out):
    with stage(nc) as st:
        stored = st.sem("stored")
        with nc.Block() as block:

            @block.sync
            def _(sp):
                sp.dma_start(out[0:(NT - 1) * P, :].rearrange("(t p) d -> p t d", p=P),
                             K.x[:, 0:(NT - 1) * D].rearrange("p (t d) -> p t d", d=D)).then_inc(stored, 16)
                sp.dma_start(out[(NT - 1) * P:NODES, :], K.x[0:LAST, (NT - 1) * D:NT * D]).then_inc(stored, 16)
                sp.wait_ge(stored, 32)


def start_buffers(st, S, parts, bins, slots):
    G, rc, base = (st.sb(x, [parts, bins]) for x in ("G", "rc", "base"))
    ci, ni = (st.sb(x, [P, bins], I32) for x in ("ci", "ni"))
    nf, ce, start = (st.sb(x, [P, bins]) for x in ("nf", "ce", "start"))
    return (S, G, rc, ci, ni, nf, ce, start, base), base, ce, st.sb("cb", [1, slots])


def count_products(nc, K, bufs, parts, bins):
    rc = bufs[2]
    nc.tensor.matmul(K.ps[0][:, 0:bins], K.ones[0:parts, :], rc[:, :], start=True, stop=True)
    return nc.tensor.matmul(K.ps[1][0:parts, 0:bins], K.before[0:parts, 0:parts], rc[:, :], start=True, stop=True)


def bin_starts(nc, K, dve, link, total, cols, bufs, rows, counted):
    S, G, rc, ci, ni, nf, ce, start, base = bufs
    V = nc.vector
    parts, bins = G.shape
    link(V.tensor_tensor_scan(S[:, :], total, total, 0.0, ALU.add, ALU.max))
    link(V.tensor_copy(G[:, :], S[:, :].rearrange("p (b c) -> p b c", c=cols)[:, :, cols - 1]))
    link(V.tensor_copy(rc[:, :], G[:, :]))
    V.tensor_tensor(rc[:, 1:bins], G[:, 1:bins], G[:, 0:bins - 1], ALU.subtract).then_inc(rows, 1)
    dve.wait_ge(counted, 1)
    link(V.tensor_scalar(ci[:, :], K.ps[0][:, 0:bins], float(P - 1), None, ALU.add))
    link(V.tensor_scalar(ni[:, :], ci[:, :], 7, None, ALU.logical_shift_right))
    link(V.tensor_copy(nf[:, :], ni[:, :]))
    link(V.tensor_tensor_scan(ce[:, :], nf[:, :], nf[:, :], 0.0, ALU.add, ALU.max))
    link(V.tensor_tensor(start[:, :], ce[:, :], nf[:, :], ALU.subtract))
    link(V.scalar_tensor_tensor(base[:, :], start[0:parts, :], float(P), K.ps[1][0:parts, 0:bins],
                                ALU.mult, ALU.add))
    link(V.tensor_tensor(base[:, 1:bins], base[:, 1:bins], G[:, 0:bins - 1], ALU.subtract))


def chunk_bins(nc, K, link, ce, cb, chunk_bin):
    bins, slots = ce.shape[1], cb.shape[1]
    link(nc.vector.memset(cb[:, :], 0.0))
    for b in range(bins - 1):
        link(nc.vector.scalar_tensor_tensor(cb[:, :], K.iota[0:1, 0:slots], ce[0:1, b:b + 1], cb[:, :],
                                            ALU.is_ge, ALU.add))
    link(nc.vector.tensor_copy(chunk_bin, cb[:, :]))


def place(nc, K, total, picks, parts, bins, cols, slots, chunk_bin):
    with stage(nc) as st:
        S = st.sb("S", [parts, bins * cols])
        T = st.sb("T", [parts, bins * cols]) if len(picks) > 1 else S
        st_bufs, base, ce, cb = start_buffers(st, S, parts, bins, slots)
        pos = st.sb("pos", [parts, cols])
        posi = st.sb("posi", [parts, cols], I32)
        lane = st.sb("lane", [parts, cols], I32)
        chunk = st.sb("chunk", [parts, cols], I32)
        S3 = S[:, :].rearrange("p (b c) -> p b c", c=cols)
        T3 = T[:, :].rearrange("p (b c) -> p b c", c=cols)
        chain, rows, counted = st.sem("chain"), st.sem("rows_counted"), st.sem("all_counted")
        with nc.Block() as block:

            @block.tensor
            def _(pe):
                pe.wait_ge(rows, 1)
                count_products(nc, K, st_bufs, parts, bins).then_inc(counted, 1)

            @block.vector
            def _(dve):
                link = linker(dve, chain)
                V = nc.vector
                bin_starts(nc, K, dve, link, total, cols, st_bufs, rows, counted)
                link(V.tensor_scalar(base[:, :], base[:, :], -1.0, None, ALU.add))
                for mask, row, slot in picks:
                    m3 = mask.rearrange("p (b c) -> p b c", c=cols)
                    for b in range(bins):
                        last = V.scalar_tensor_tensor(T3[:, b, :], S3[:, b, :], base[:, b:b + 1], m3[:, b, :],
                                                      ALU.add, ALU.mult)
                    link(last)
                    link(V.tensor_reduce(pos[:, :], T3.rearrange("p b c -> p c b"), AX.X, ALU.add))
                    link(V.tensor_copy(posi[:, :], pos[:, :]))
                    if slot is not None:
                        link(V.tensor_copy(slot, posi[:, :]))
                    V.tensor_scalar(lane[:, :], posi[:, :], P - 1, None, ALU.bitwise_and)
                    link(V.tensor_scalar(chunk[:, :], posi[:, :], 7, None, ALU.logical_shift_right))
                    link(V.scalar_tensor_tensor(row, lane[:, :], float(slots), chunk[:, :], ALU.mult, ALU.add))
                chunk_bins(nc, K, link, ce, cb, chunk_bin)


def scatter_items(nc, K, picks, parts, cols, unroll, halves, words, slots, fill, out):
    with stage(nc) as st:
        blank = st.sb("blank", [P, slots * words])
        rowr = st.sb("rowr", [parts, halves * unroll], I32)
        payr = st.sb("payr", [parts, halves * unroll * words])
        table = K.slot_table[0:P * slots * words].rearrange("(r w) -> r w", w=words)
        whole = K.slot_table[0:P * slots * words].rearrange("(p f) -> p f", p=P)
        blanked, filled, staged, passed, back = (st.sem(x) for x in ("blanked", "filled", "staged", "passed", "back"))
        landed = [st.sem(f"landed{h}") for h in range(halves)]
        rounds = cols // (unroll * halves)
        with nc.Block() as block:

            @block.vector
            def _(dve):
                for w in range(words):
                    last = nc.vector.memset(blank[:, :].rearrange("p (s w) -> p s w", w=words)[:, :, w], fill[w])
                last.then_inc(blanked, 1)

            @block.gpsimd
            def _(pool):
                pool.wait_ge(filled, 16)
                for n, (row, pay) in enumerate(picks):
                    with pool.Fori(0, rounds) as k:
                        for h in range(halves):
                            pool.wait_ge(landed[h], unroll * 16 * (n * rounds + k))
                            r = slice(h * unroll, (h + 1) * unroll)
                            w = slice(h * unroll * words, (h + 1) * unroll * words)
                            nc.gpsimd.tensor_copy(rowr[:, r], row[:, bass.ds((k * halves + h) * unroll, unroll)])
                            nc.gpsimd.tensor_copy(payr[:, w], pay[:, bass.ds((k * halves + h) * unroll * words,
                                                                            unroll * words)]).then_inc(staged, 1)
                            wait_staged(pool, staged, n * rounds * halves + k * halves + h + 1, passed)
                            for j in range(h * unroll, (h + 1) * unroll):
                                nc.gpsimd.indirect_dma_start(
                                    table, bass.IndirectOffsetOnAxis(ap=rowr[:, j:j + 1], axis=0),
                                    payr[:, j * words:(j + 1) * words], None).then_inc(landed[h], 16)

            @block.sync
            def _(sp):
                sp.wait_ge(blanked, 1)
                sp.dma_start(whole, blank[:, :]).then_inc(filled, 16)
                for h in range(halves):
                    sp.wait_ge(landed[h], unroll * 16 * rounds * len(picks))
                sp.dma_start(out, whole).then_inc(back, 16)
                sp.wait_ge(back, 16)


def place_by_node(nc, K, node_row, tile, row, chunk_bin):
    W = 20
    U = 4
    with stage(nc) as st:
        tiles = st.sb("tiles", [EP, EC * NT], BF)
        counts = st.sb("counts", [P, NT * EC], BF)
        S = st.sb("S", [P, NT * EC])
        first = st.sb("first", [P, EC * NT])
        tiles3 = tiles[:, :].rearrange("p (c t) -> p c t", t=NT)
        counts3 = counts[:, :].rearrange("p (t c) -> p t c", c=EC)
        S3 = S[:, :].rearrange("p (t c) -> p t c", c=EC)
        first3 = first[:, :].rearrange("p (c t) -> p c t", t=NT)
        with stage(nc) as st1:
            hot = st1.sb("hot", [EP, 2, W, P], BF)
            tiled, made, counted, kept = (st1.sem(x) for x in ("tiled", "made", "counted", "kept"))
            with nc.Block() as block:

                @block.vector
                def _(dve):
                    for t in range(NT):
                        last = nc.vector.tensor_scalar(tiles3[:, :, t], tile, float(t), None, ALU.is_equal)
                    last.then_inc(tiled, 1)

                    def step(i, j, k):
                        wait_count(dve, counted, i - 1)
                        nc.vector.tensor_tensor(hot[:, j, :, :],
                                                K.iota[0:EP, 0:P].unsqueeze(1).broadcast_to([EP, W, P]),
                                                node_row[:, bass.ds(i * W, W)].unsqueeze(2).broadcast_to([EP, W, P]),
                                                ALU.is_equal).then_inc(made, 1)

                    steps(dve, EC // W, 2, 0, step)

                @block.tensor
                def _(pe):
                    pe.wait_ge(tiled, 1)

                    def step(i, j, k):
                        pe.wait_ge(made, i + 1)
                        wait_count(pe, kept, i - 1)
                        for c in range(W):
                            last = nc.tensor.matmul(K.ps[j][:, c * NT:(c + 1) * NT], hot[:, j, c, :],
                                                    tiles[:, bass.ds(i * (W * NT) + c * NT, NT)], start=True, stop=True)
                        last.then_inc(counted, 1)

                    steps(pe, EC // W, 2, 0, step)

                @block.scalar
                def _(act):
                    def step(i, j, k):
                        act.wait_ge(counted, i + 1)
                        nc.scalar.activation(counts3[:, :, bass.ds(i * W, W)],
                                             K.ps[j][:, 0:W * NT].rearrange("p (c t) -> p t c", t=NT),
                                             ACT.Copy).then_inc(kept, 1)

                    steps(act, EC // W, 2, 0, step)

        with stage(nc) as st2:
            bufs, base, ce, cb = start_buffers(st2, S, P, NT, CHUNKS)
            chain, rows, counted = (st2.sem(x) for x in ("chain", "rows", "counted"))
            with nc.Block() as block:

                @block.tensor
                def _(pe):
                    pe.wait_ge(rows, 1)
                    count_products(nc, K, bufs, P, NT).then_inc(counted, 1)

                @block.vector
                def _(dve):
                    link = linker(dve, chain)
                    bin_starts(nc, K, dve, link, counts[:, :], EC, bufs, rows, counted)
                    for t in range(NT):
                        last = nc.vector.scalar_tensor_tensor(first3[:, :, t], S3[:, t, :], base[:, t:t + 1],
                                                              counts3[:, t, :], ALU.add, ALU.subtract)
                    link(last)
                    chunk_bins(nc, K, link, ce, cb, chunk_bin)

        with stage(nc) as st3:
            hot = st3.sb("hot", [EP, 2, U, P], BF)
            hotT = st3.sb("hotT", [P, 4, U * EP])
            twin = st3.sb("twin", [EP, 2, U, EP], BF)
            pos = st3.sb("pos", [EP, EC])
            posi, lane, chunk = (st3.sb(x, [EP, EC], I32) for x in ("posi", "lane", "chunk"))
            found = S[0:EP, :]
            made, turned, copied, paired, masked, looked, kept, chain = (
                st3.sem(x) for x in ("made", "turned", "copied", "paired", "masked", "looked", "kept", "chain"))
            with nc.Block() as block:

                @block.vector
                def _(dve):
                    def step(i, j, k):
                        if runs(i, EC // U):
                            wait_count(dve, turned, i - 1)
                            nc.vector.tensor_tensor(hot[:, j % 2, :, :],
                                                    K.iota[0:EP, 0:P].unsqueeze(1).broadcast_to([EP, U, P]),
                                                    node_row[:, bass.ds(i * U, U)].unsqueeze(2).broadcast_to([EP, U, P]),
                                                    ALU.is_equal).then_inc(made, 1)
                        if runs(i - 1, EC // U):
                            dve.wait_ge(paired, i)
                            wait_count(dve, looked, i - 2)
                            nc.vector.tensor_tensor(twin[:, (j - 1) % 2, :, :],
                                                    K.ps[2 + (j - 1) % 2][0:EP, 0:U * EP].rearrange("p (u e) -> p u e", u=U),
                                                    K.before[0:EP, 0:EP].unsqueeze(1).broadcast_to([EP, U, EP]),
                                                    ALU.mult).then_inc(masked, 1)

                    steps(dve, EC // U, 4, 1, step)
                    dve.wait_ge(kept, EC // U)
                    link = linker(dve, chain)
                    V = nc.vector
                    link(V.tensor_tensor(found, found, tiles[:, :], ALU.mult))
                    link(V.tensor_reduce(pos[:, :], found.rearrange("p (c t) -> p c t", t=NT), AX.X, ALU.add))
                    link(V.tensor_copy(posi[:, :], pos[:, :]))
                    V.tensor_scalar(lane[:, :], posi[:, :], P - 1, None, ALU.bitwise_and)
                    link(V.tensor_scalar(chunk[:, :], posi[:, :], 7, None, ALU.logical_shift_right))
                    link(V.scalar_tensor_tensor(row, lane[:, :], float(CHUNKS), chunk[:, :], ALU.mult, ALU.add))

                @block.tensor
                def _(pe):
                    def step(i, j, k):
                        if runs(i, EC // U):
                            pe.wait_ge(made, i + 1)
                            wait_count(pe, copied, i - 1)
                            for u in range(U):
                                last = nc.tensor.matmul(K.ps[j % 2][:, u * EP:(u + 1) * EP], hot[:, j % 2, u, :],
                                                        K.ident_bf[0:EP, 0:EP], start=True, stop=True)
                            last.then_inc(turned, 1)
                        if runs(i - 1, EC // U):
                            pe.wait_ge(copied, i)
                            wait_count(pe, masked, i - 2)
                            for u in range(U):
                                both = hotT[:, (j - 1) % 4, u * EP:(u + 1) * EP]
                                last = nc.tensor.matmul(K.ps[2 + (j - 1) % 2][0:EP, u * EP:(u + 1) * EP], both, both,
                                                        start=True, stop=True)
                            last.then_inc(paired, 1)
                        if runs(i - 2, EC // U):
                            c, jj = i - 2, (j - 2) % 4
                            pe.wait_ge(masked, c + 1)
                            wait_count(pe, kept, c - 1)
                            for u in range(U):
                                bank = K.ps[4 + jj % 2][0:EP, u * NT:(u + 1) * NT]
                                nc.tensor.matmul(bank, hotT[:, jj, u * EP:(u + 1) * EP],
                                                 first[:, bass.ds(c * (U * NT) + u * NT, NT)], start=True, stop=False)
                                last = nc.tensor.matmul(bank, twin[:, jj % 2, u, :],
                                                        tiles[:, bass.ds(c * (U * NT) + u * NT, NT)],
                                                        start=False, stop=True)
                            last.then_inc(looked, 1)

                    steps(pe, EC // U, 4, 2, step)

                @block.scalar
                def _(act):
                    def step(i, j, k):
                        if runs(i, EC // U):
                            act.wait_ge(turned, i + 1)
                            wait_count(act, looked, i - 3)
                            nc.scalar.activation(hotT[:, j, :], K.ps[j % 2][:, 0:U * EP], ACT.Copy).then_inc(copied, 1)
                        if runs(i - 2, EC // U):
                            c, jj = i - 2, (j - 2) % 4
                            act.wait_ge(looked, c + 1)
                            nc.scalar.activation(found[:, bass.ds(c * (U * NT), U * NT)], K.ps[4 + jj % 2][0:EP, 0:U * NT],
                                                 ACT.Copy).then_inc(kept, 1)

                    steps(act, EC // U, 4, 2, step)


def sort_edges(nc, K, key, other, weight, to, by_node):
    with stage(nc) as st:
        ki = st.sb("ki", [EP, EC], I32)
        oi = st.sb("oi", [EP, EC], I32)
        wf = st.sb("wf", [EP, EC])
        ti = st.sb("ti", [EP, EC], I32)
        li = st.sb("li", [EP, EC], I32)
        tf = st.sb("tf", [EP, EC])
        lf = st.sb("lf", [EP, EC])
        pay = st.sb("pay", [EP, EC * 3])
        row = st.sb("row", [EP, EC], I32)
        pay3 = pay[:, :].rearrange("p (c w) -> p c w", w=3)
        loaded, chain = st.sem("loaded"), st.sem("chain")
        with nc.Block() as block:

            @block.sync
            def _(sp):
                for a, b in ((ki, key), (oi, other), (wf, weight)):
                    sp.dma_start(a[:, :], b.rearrange("(p c) -> p c", c=EC)).then_inc(loaded, 16)

            @block.vector
            def _(dve):
                link = linker(dve, chain)
                V = nc.vector
                dve.wait_ge(loaded, 48)
                V.tensor_scalar(ti[:, :], ki[:, :], 7, None, ALU.logical_shift_right)
                link(V.tensor_scalar(li[:, :], ki[:, :], P - 1, None, ALU.bitwise_and))
                V.tensor_copy(pay3[:, :, 0], oi[:, :])
                V.tensor_copy(pay3[:, :, 1], li[:, :])
                V.tensor_copy(lf[:, :], li[:, :])
                V.tensor_copy(pay3[:, :, 2], ki[:, :] if by_node else wf[:, :])
                link(V.tensor_copy(tf[:, :], ti[:, :]))

        if by_node:
            place_by_node(nc, K, lf[:, :], tf[:, :], row[:, :], to.bin[:, :])
        else:
            with stage(nc) as st2:
                mask = st2.sb("mask", [EP, NT * EC])

                def masks():
                    for b in range(NT):
                        last = nc.vector.tensor_scalar(mask[:, b * EC:(b + 1) * EC], tf[:, :], float(b), None, ALU.is_equal)
                    return last

                vector_work(nc, masks)
                place(nc, K, mask[:, :], [(mask[:, :], row[:, :], None)], EP, NT, EC, CHUNKS, to.bin[:, :])
        scatter_items(nc, K, [(row, pay)], EP, EC, 8, 2, 3, CHUNKS, (0.0, -1.0, -1.0 if by_node else 0.0), to.pay[:, :])
    with stage(nc) as st:
        binf = st.sb("binf", [1, CHUNKS])
        bins = st.sb("bins", [P, CHUNKS])
        chain, numbered, spread = st.sem("chain"), st.sem("numbered"), st.sem("spread")
        with nc.Block() as block:

            @block.tensor
            def _(pe):
                pe.wait_ge(numbered, 1)
                nc.tensor.matmul(K.ps[0][:, 0:CHUNKS], K.ones[0:1, :], binf[:, :], start=True, stop=True).then_inc(spread, 1)

            @block.vector
            def _(dve):
                link = linker(dve, chain)
                nc.vector.tensor_copy(to.idx[:, :], to.pay[:, :].rearrange("p (c w) -> p c w", w=3)[:, :, 0])
                nc.vector.tensor_copy(binf[:, :], to.bin[:, :]).then_inc(numbered, 1)
                dve.wait_ge(spread, 1)
                link(nc.vector.tensor_copy(bins[:, :], K.ps[0][:, 0:CHUNKS]))
                nc.vector.memset(to.same[:, 0:1], 0.0)
                nc.vector.tensor_tensor(to.same[:, 1:CHUNKS], bins[:, 1:CHUNKS], bins[:, 0:CHUNKS - 1], ALU.is_equal)


def gather_rows(nc, pool, edges, table, rows, idxr, gathered, staged, passed, used, per):
    GR = rows.shape[1]
    half = GR // 2

    def step(i, j, k):
        wait_count(pool, used, half // per * (i - 1))
        nc.gpsimd.tensor_copy(idxr[:, j * half:(j + 1) * half], edges.idx[:, bass.ds(i * half, half)]).then_inc(staged, 1)
        wait_staged(pool, staged, i + 1, passed)
        for g in range(j * half, (j + 1) * half):
            nc.gpsimd.indirect_dma_start(rows[:, g, :], None, table,
                                         bass.IndirectOffsetOnAxis(ap=idxr[:, g:g + 1], axis=0))\
                .then_inc(gathered[g // per], 16)

    steps(pool, CHUNKS // half, 2, 0, step)


def carry(nc, dve, edges, run, bank, c, width, summed, kept, ran):
    dve.wait_ge(summed, c + 1)
    wait_count(dve, ran, c)
    wait_count(dve, kept, c - RUNS + 1)
    return nc.vector.scalar_tensor_tensor(run[1], run[0], edges.same[:, bass.ds(c, 1)], bank, ALU.mult,
                                          ALU.add).then_inc(ran, 1)


def keep(nc, act, edges, out, run, c, width, ran, kept):
    t = act.value_load(edges.bin[0:1, bass.ds(c, 1)], min_val=0, max_val=NT - 1)
    act.wait_ge(ran, c + 1)
    wait_count(act, kept, c)
    nc.scalar.activation(tile_of(out, t, width), run, ACT.Copy).then_inc(kept, 1)


def spmm(nc, K, edges, table, out):
    GR, R, LAG = 16, 8, 4
    with stage(nc) as st:
        idxr = st.sb("idxr", [P, GR], I32)
        rows = st.sb("rows", [P, GR, D])
        pick = st.sb("pick", [P, R, P])
        run = st.sb("run", [P, RUNS, D])
        gathered = [st.sem(f"gathered{j}") for j in range(GR)]
        staged, passed, picked, summed, ran, kept, cleared = (
            st.sem(n) for n in ("staged", "passed", "picked", "summed", "ran", "kept", "cleared"))
        with nc.Block() as block:

            @block.gpsimd
            def _(pool):
                gather_rows(nc, pool, edges, table, rows, idxr, gathered, staged, passed, summed, 1)

            @block.vector
            def _(dve):
                nc.vector.memset(out[:, :], 0.0)
                nc.vector.memset(run[:, RUNS - 1, :], 0.0).then_inc(cleared, 1)
                dve.wait_ge(cleared, 1)

                def step(i, j, k):
                    if runs(i - LAG, CHUNKS):
                        c, jj = i - LAG, (j - LAG) % R
                        carry(nc, dve, edges, (run[:, (jj - 1) % RUNS, :], run[:, jj % RUNS, :]), K.ps[jj][:, 0:D],
                              c, D, summed, kept, ran)
                    if runs(i, CHUNKS):
                        wait_count(dve, summed, i - R + 1)
                        nc.vector.tensor_scalar(pick[:, j, :], K.iota[:, 0:P], edges.pay[:, bass.ds(3 * i + 1, 1)],
                                                edges.pay[:, bass.ds(3 * i + 2, 1)], ALU.is_equal,
                                                ALU.mult).then_inc(picked, 1)

                steps(dve, CHUNKS, R, LAG, step)

            @block.tensor
            def _(pe):
                def step(i, j, k):
                    pe.wait_ge(gathered[j], 16 * k + 16)
                    pe.wait_ge(picked, i + 1)
                    wait_count(pe, ran, i - R + 1)
                    nc.tensor.matmul(K.ps[j % R][:, 0:D], pick[:, j % R, :], rows[:, j, :],
                                     start=True, stop=True).then_inc(summed, 1)

                steps(pe, CHUNKS, GR, 0, step)

            @block.scalar
            def _(act):
                act.wait_ge(cleared, 1)

                def step(i, j, k):
                    keep(nc, act, edges, out, run[:, j, :], i, D, ran, kept)

                steps(act, CHUNKS, RUNS, 0, step)


def vector_work(nc, *ops):
    with stage(nc) as st:
        chain = st.sem("chain")
        with nc.Block() as block:

            @block.vector
            def _(dve):
                link = linker(dve, chain)
                for op in ops:
                    link(op())


def layer_norm(nc, K, src, dst, affine=None, table=None, residual=False):
    with stage(nc) as st:
        stats = st.sb("stats", [P, NT * 6])
        mv = st.sb("mv", [P, NT * 2])
        rstd = st.sb("rstd", [P, NT])
        gb = st.sb("gb", [P, 2, D]) if affine else None
        var = mv[:, :].rearrange("p (t s) -> p t s", s=2)[:, :, 1]
        loaded, chain, stat, aggr, var_ok, root, normed, stored = (
            st.sem(n) for n in ("loaded", "chain", "stat", "aggr", "var_ok", "root", "normed", "stored"))
        with nc.Block() as block:

            @block.sync
            def _(sp):
                if affine:
                    for a in range(2):
                        sp.dma_start(gb[:, a, :], affine[a].partition_broadcast(P)).then_inc(loaded, 16)
                if table is not None:
                    def step(t, j, k):
                        sp.wait_ge(normed, t + 1)
                        sp.dma_start(tile_rows(table, t), tile_of(dst, t)).then_inc(stored, 16)

                    steps(sp, NT, 2, 0, step)
                    sp.wait_ge(stored, 16 * NT)

            @block.scalar
            def _(act):
                act.wait_ge(var_ok, 1)
                nc.scalar.activation(rstd[:, :], rstd[:, :], ACT.Sqrt).then_inc(root, 1)

            @block.vector
            def _(dve):
                link = linker(dve, chain)

                def statistics(t, j, k):
                    nc.vector.bn_stats(stats[:, bass.ds(t * 6, 6)], tile_of(src, t)).then_inc(stat, 1)

                steps(dve, NT, 5, 0, statistics)
                dve.wait_ge(stat, NT)
                for t in range(NT):
                    last = nc.vector.bn_aggr(mv[:, 2 * t:2 * t + 2], stats[:, 6 * t:6 * t + 6])
                link(last)
                nc.vector.tensor_scalar(rstd[:, :], var, EPS, None, ALU.add).then_inc(var_ok, 1)
                dve.wait_ge(root, 1)
                link(nc.vector.reciprocal(rstd[:, :], rstd[:, :]))
                if affine:
                    dve.wait_ge(loaded, 32)
                per = 1 + 2 * bool(affine) + bool(residual)

                def normalise(t, j, k):
                    n = per * t
                    ops = [lambda: nc.vector.tensor_scalar(tile_of(dst, t), tile_of(src, t), mv[:, bass.ds(2 * t, 1)],
                                                           rstd[:, bass.ds(t, 1)], ALU.subtract, ALU.mult)]
                    if affine:
                        ops += [lambda: nc.vector.tensor_tensor(tile_of(dst, t), tile_of(dst, t), gb[:, 0, :], ALU.mult),
                                lambda: nc.vector.tensor_tensor(tile_of(dst, t), tile_of(dst, t), gb[:, 1, :], ALU.add)]
                    if residual:
                        ops += [lambda: nc.vector.tensor_tensor(tile_of(K.x, t), tile_of(K.x, t), tile_of(dst, t), ALU.add)]
                    for m, op in enumerate(ops):
                        if m:
                            dve.wait_ge(aggr, n + m)
                        ins = op()
                        if per > 1:
                            ins.then_inc(aggr, 1)
                        else:
                            ins.then_inc(normed, 1)

                steps(dve, NT, 5, 0, normalise)


def dense(nc, K, sources, weights, bias, outs):
    width = sum(o[0] for o in outs)
    nsrc = len(sources)
    tables = [o for o in outs if o[1] in ("table", "both")]
    with stage(nc) as st:
        w = st.sb("w", [P, nsrc * KD, width])
        b = st.sb("b", [1, width]) if bias is not None else None
        raw = st.sb("raw", [P, 2, nsrc * D])
        xT = st.sb("xT", [P, 2, nsrc * D])
        ring = st.sb("ring", [P, 2, len(tables) or 1, D])
        loaded = st.sem("loaded")
        staged, turned, copied, summed, written = (st.sem(n) for n in ("staged", "turned", "copied", "summed", "written"))
        stored = [st.sem(f"stored{j}") for j in range(2)]
        with nc.Block() as block:

            @block.sync
            def _(sp):
                for s in range(nsrc):
                    at = 0
                    for part in weights[s]:
                        n = part.shape[1]
                        for c in range(KD):
                            sp.dma_start(w[:, s * KD + c, at:at + n], part[c * P:(c + 1) * P, :]).then_inc(loaded, 16)
                        at += n
                if b is not None:
                    sp.dma_start(b[:, :], bias).then_inc(loaded, 16)

                def step(t, j, k):
                    sp.wait_ge(written, t + 1)
                    for n, (wd, kind, target, _f) in enumerate(tables):
                        tab, src = (target, ring[:, j, n, 0:wd]) if kind == "table" else (target[1], tile_of(target[0], t, wd))
                        sp.dma_start(tile_rows(tab, t), src).then_inc(stored[j], 16)

                if tables:
                    steps(sp, NT, 2, 0, step)
                    for j in range(2):
                        sp.wait_ge(stored[j], 16 * len(tables) * ((NT + 1 - j) // 2))

            @block.scalar
            def _(act):
                def step(i, j, k):
                    if runs(i, NT):
                        wait_count(act, turned, i - 1)
                        for s, src in enumerate(sources):
                            last = nc.scalar.activation(raw[:, j, s * D:(s + 1) * D], tile_of(src, i), ACT.Copy)
                        last.then_inc(staged, 1)
                    if runs(i - 1, NT):
                        act.wait_ge(turned, i)
                        wait_count(act, summed, i - 2)
                        nc.scalar.activation(xT[:, 1 - j, :], K.ps[1 - j][:, 0:nsrc * D], ACT.Copy).then_inc(copied, 1)

                steps(act, NT, 2, 1, step)

            @block.tensor
            def _(pe):
                pe.wait_ge(loaded, 16 * (KD * sum(len(x) for x in weights) + (b is not None)))

                def step(i, j, k):
                    if runs(i, NT):
                        pe.wait_ge(staged, i + 1)
                        wait_count(pe, copied, i - 1)
                        for s in range(nsrc * KD):
                            last = nc.tensor.transpose(K.ps[j][:, s * P:(s + 1) * P], raw[:, j, s * P:(s + 1) * P],
                                                       K.ident[:, :])
                        last.then_inc(turned, 1)
                    if runs(i - 1, NT):
                        pe.wait_ge(copied, i)
                        wait_count(pe, written, i - 2)
                        at = 0
                        for g, o in enumerate(outs):
                            bank = K.ps[2 + 3 * (1 - j) + g][:, 0:o[0]]
                            for s in range(nsrc * KD):
                                last = nc.tensor.matmul(bank, xT[:, 1 - j, s * P:(s + 1) * P], w[:, s, at:at + o[0]],
                                                        start=(s == 0), stop=(s == nsrc * KD - 1 and b is None))
                            if b is not None:
                                last = nc.tensor.matmul(bank, K.ones[0:1, :], b[0:1, at:at + o[0]], start=False, stop=True)
                            at += o[0]
                        last.then_inc(summed, 1)

                steps(pe, NT, 2, 1, step)

            @block.vector
            def _(dve):
                def step(t, j, k):
                    dve.wait_ge(summed, t + 1)
                    if any(o[1] == "table" for o in outs):
                        wait_count(dve, stored[j], 16 * len(tables) * k)
                    n = 0
                    for g, (wd, kind, target, factor) in enumerate(outs):
                        bank = K.ps[2 + 3 * j + g][:, 0:wd]
                        if kind == "add":
                            last = nc.vector.tensor_tensor(tile_of(target, t), tile_of(target, t), bank, ALU.add)
                        elif kind == "relu_add":
                            last = nc.vector.scalar_tensor_tensor(tile_of(K.x, t), bank, 0.0, tile_of(K.x, t),
                                                                  ALU.max, ALU.add)
                        else:
                            to = ring[:, j, n, 0:wd] if kind == "table" else tile_of(target if kind == "sb" else target[0], t, wd)
                            if factor is None:
                                last = nc.vector.tensor_copy(to, bank)
                            else:
                                last = nc.vector.tensor_scalar(to, bank, factor, None, ALU.mult)
                        n += kind in ("table", "both")
                    last.then_inc(written, 1)

                steps(dve, NT, 2, 0, step)


def routed_ffn(nc, K, r, w1, b1, w2, b2, func, relu_out):
    experts, _, hid = w1.shape
    hm = min(P, hid)
    nh = hid // hm
    n = r.chunks
    R = 4
    with stage(nc) as st:
        b1T = st.sb("b1T", [hm, experts * nh])
        w1r = st.sb("w1r", [P, R, KD, hid])
        w2r = st.sb("w2r", [hm, R, nh, D])
        b2r = st.sb("b2r", [1, R, D])
        idxr = st.sb("idxr", [P, R], I32)
        rows = st.sb("rows", [P, R, D])
        xT = st.sb("xT", [P, 2, D])
        hT = st.sb("hT", [hm, 2, nh * P])
        yr = st.sb("yr", [P, R, D])
        fetched = [st.sem(f"fetched{j}") for j in range(R)]
        gathered = [st.sem(f"gathered{j}") for j in range(R)]
        stored = [st.sem(f"stored{j}") for j in range(R)]
        biased, staged, passed, turned, copied, hidden, acted, summed, written = (
            st.sem(x) for x in ("biased", "staged", "passed", "turned", "copied", "hidden", "acted", "summed", "written"))
        w1v = w1.rearrange("e (k p) h -> p e k h", p=P)
        w2v = w2.rearrange("e (c p) d -> p e c d", p=hm)
        b2v = b2.rearrange("(o e) d -> o e d", o=1)
        with nc.Block() as block:

            @block.sync
            def _(sp):
                def step(i, j, k):
                    if runs(i, n):
                        e = sp.value_load(r.bin[0:1, bass.ds(i, 1)], min_val=0, max_val=experts - 1)
                        wait_count(sp, summed, i - R + 1)
                        sp.dma_start(w1r[:, j, :, :], w1v[:, bass.ds(e, 1), :, :].rearrange("p e k h -> p (e k) h")).then_inc(fetched[j], 16)
                        sp.dma_start(w2r[:, j, :, :], w2v[:, bass.ds(e, 1), :, :].rearrange("p e c d -> p (e c) d")).then_inc(fetched[j], 16)
                        sp.dma_start(b2r[:, j, :], b2v[:, bass.ds(e, 1), :].rearrange("o e d -> o (e d)")).then_inc(fetched[j], 16)
                    if runs(i - R, n):
                        sp.wait_ge(written, i - R + 1)
                        sp.dma_start(tile_rows(K.slot_rows, i - R), yr[:, j, :]).then_inc(stored[j], 16)

                steps(sp, n, R, R, step)
                for j in range(R):
                    sp.wait_ge(stored[j], 16 * ((n + R - 1 - j) // R))

            @block.gpsimd
            def _(pool):
                def step(i, j, k):
                    wait_count(pool, turned, i - R + 1)
                    nc.gpsimd.tensor_copy(idxr[:, j:j + 1], r.idx[:, bass.ds(i, 1)]).then_inc(staged, 1)
                    wait_staged(pool, staged, i + 1, passed)
                    nc.gpsimd.indirect_dma_start(rows[:, j, :], None, K.table,
                                                 bass.IndirectOffsetOnAxis(ap=idxr[:, j:j + 1], axis=0))\
                        .then_inc(gathered[j], 16)

                steps(pool, n, R, 0, step)

            @block.tensor
            def _(pe):
                def step(i, j, k):
                    if runs(i, n):
                        pe.wait_ge(gathered[j], 16 * k + 16)
                        wait_count(pe, copied, i - 1)
                        for s in range(KD):
                            last = nc.tensor.transpose(K.ps[j % 2][:, s * P:(s + 1) * P], rows[:, j, s * P:(s + 1) * P],
                                                       K.ident[:, :])
                        last.then_inc(turned, 1)
                    if runs(i - 1, n):
                        c = i - 1
                        jj = (j - 1) % R
                        pe.wait_ge(copied, c + 1)
                        pe.wait_ge(fetched[jj], 48 * ((k if j else k - 1) + 1))
                        wait_count(pe, acted, c - 1)
                        for h in range(nh):
                            for s in range(KD):
                                last = nc.tensor.matmul(K.ps[2 + jj % 2][0:hm, h * P:(h + 1) * P],
                                                        w1r[:, jj, s, h * hm:(h + 1) * hm],
                                                        xT[:, jj % 2, s * P:(s + 1) * P],
                                                        start=(s == 0), stop=(s == KD - 1))
                        last.then_inc(hidden, 1)
                    if runs(i - 2, n):
                        c = i - 2
                        jj = (j - 2) % R
                        pe.wait_ge(acted, c + 1)
                        wait_count(pe, written, c - 1)
                        bank = K.ps[4 + jj % 2][:, 0:D]
                        for h in range(nh):
                            nc.tensor.matmul(bank, hT[:, jj % 2, h * P:(h + 1) * P], w2r[:, jj, h, :],
                                             start=(h == 0), stop=False)
                        nc.tensor.matmul(bank, K.ones[0:1, :], b2r[0:1, jj, :], start=False, stop=True)\
                            .then_inc(summed, 1)

                steps(pe, n, R, 2, step)

            @block.scalar
            def _(act):
                act.dma_start(b1T[:, :], b1.rearrange("e (c p) -> p (e c)", p=hm)).then_inc(biased, 16)
                act.wait_ge(biased, 16)

                def step(i, j, k):
                    e = act.value_load(r.bin[0:1, bass.ds(i, 1)], min_val=0, max_val=experts - 1)
                    act.wait_ge(hidden, i + 1)
                    wait_count(act, summed, i - 1)
                    for h in range(nh):
                        last = nc.scalar.activation(hT[:, j % 2, h * P:(h + 1) * P],
                                                    K.ps[2 + j % 2][0:hm, h * P:(h + 1) * P], func,
                                                    bias=b1T[:, bass.ds(e * nh + h, 1)])
                    last.then_inc(acted, 1)

                steps(act, n, R, 0, step)

            @block.vector
            def _(dve):
                def step(i, j, k):
                    if runs(i, n):
                        dve.wait_ge(turned, i + 1)
                        wait_count(dve, hidden, i - 1)
                        nc.vector.tensor_copy(xT[:, j % 2, :], K.ps[j % 2][:, 0:D]).then_inc(copied, 1)
                    if runs(i - 2, n):
                        jj = (j - 2) % R
                        dve.wait_ge(summed, i - 1)
                        wait_count(dve, stored[jj], 16 * (k if j >= 2 else k - 1))
                        if relu_out:
                            ins = nc.vector.tensor_scalar(yr[:, jj, :], K.ps[4 + jj % 2][:, 0:D], 0.0, None, ALU.max)
                        else:
                            ins = nc.vector.tensor_copy(yr[:, jj, :], K.ps[4 + jj % 2][:, 0:D])
                        ins.then_inc(written, 1)

                steps(dve, n, R, 2, step)


def combine(nc, K, slots, weights, first, dst):
    picks = len(slots)
    R = 2
    with stage(nc) as st:
        idxr = st.sb("idxr", [P, R * picks], I32)
        rows = st.sb("rows", [P, R * picks, D])
        gathered = [st.sem(f"gathered{j}") for j in range(R)]
        staged, passed, added = st.sem("staged"), st.sem("passed"), st.sem("added")
        with nc.Block() as block:

            @block.gpsimd
            def _(pool):
                def step(t, j, k):
                    wait_count(pool, added, picks * (t - 1))
                    for p in range(picks):
                        last = nc.gpsimd.tensor_copy(idxr[:, j * picks + p:j * picks + p + 1],
                                                     slots[p][:, bass.ds(t, 1)])
                    last.then_inc(staged, 1)
                    wait_staged(pool, staged, t + 1, passed)
                    for p in range(j * picks, (j + 1) * picks):
                        nc.gpsimd.indirect_dma_start(rows[:, p, :], None, K.slot_rows,
                                                     bass.IndirectOffsetOnAxis(ap=idxr[:, p:p + 1], axis=0))\
                            .then_inc(gathered[j], 16)

                steps(pool, NT, R, 0, step)

            @block.vector
            def _(dve):
                def step(t, j, k):
                    dve.wait_ge(gathered[j], 16 * picks * (k + 1))
                    for p in range(picks):
                        row = rows[:, j * picks + p, :]
                        onto = first if p == 0 else dst
                        if p:
                            dve.wait_ge(added, picks * t + p)
                        if weights is None:
                            ins = nc.vector.tensor_tensor(tile_of(dst, t), tile_of(onto, t), row, ALU.add)
                        else:
                            ins = nc.vector.scalar_tensor_tensor(tile_of(dst, t), row, weights[p][:, bass.ds(t, 1)],
                                                                 tile_of(onto, t), ALU.mult, ALU.add)
                        ins.then_inc(added, 1)

                steps(dve, NT, R, 0, step)


def route(nc, K, r, gate, experts, picks, mode):
    gate_w, gate_b = gate
    with stage(nc) as big:
        logits = big.sb("logits", [P, NT * experts])
        masks = [big.sb(f"mask{p}", [P, experts * NT]) for p in range(picks)]
        total = big.sb("total", [P, experts * NT]) if picks > 1 else masks[0]
        rows = [big.sb(f"rows{p}", [P, NT], I32) for p in range(picks)]
        token = big.sb("token", [P, NT])
        found = big.sb("found", [P, NT])
        found_i = big.sb("found_i", [P, NT], I32)
        dense(nc, K, [K.xn], [[gate_w]], gate_b.rearrange("(o n) -> o n", o=1), [(experts, "sb", logits, None)])
        with stage(nc) as st:
            top = st.sb("top", [P, NT * 8])
            at = st.sb("at", [P, NT * 8], U32)
            atf = st.sb("atf", [P, NT * 8])
            m = st.sb("m", [P, NT])
            z = st.sb("z", [P, NT])
            chain, asked, answered, numbered = (st.sem(x) for x in ("chain", "asked", "answered", "numbered"))
            top3 = top[:, :].rearrange("p (t e) -> p t e", e=8)
            atf3 = atf[:, :].rearrange("p (t e) -> p t e", e=8)
            lg3 = logits[:, :].rearrange("p (t e) -> p t e", e=experts)
            with nc.Block() as block:

                @block.gpsimd
                def _(pool):
                    nc.gpsimd.iota(found_i[:, :], pattern=[[P, NT]], base=0, channel_multiplier=1).then_inc(numbered, 1)

                @block.scalar
                def _(act):
                    if mode == "top_of_softmax":
                        act.wait_ge(asked, 1)
                        nc.scalar.activation(logits[:, :], logits[:, :], ACT.Exp).then_inc(answered, 1)
                    if mode == "softmax_of_top":
                        act.wait_ge(asked, 1)
                        nc.scalar.activation(m[:, :], m[:, :], ACT.Exp).then_inc(answered, 1)

                @block.vector
                def _(dve):
                    link = linker(dve, chain)
                    V = nc.vector
                    dve.wait_ge(numbered, 1)
                    link(V.tensor_copy(token[:, :], found_i[:, :]))
                    if mode == "top_of_softmax":
                        link(V.tensor_reduce(m[:, :], lg3, AX.X, ALU.max))
                        V.tensor_tensor(lg3, lg3, m[:, :].unsqueeze(2).broadcast_to([P, NT, experts]),
                                        ALU.subtract).then_inc(asked, 1)
                        dve.wait_ge(answered, 1)
                        link(V.tensor_reduce(z[:, :], lg3, AX.X, ALU.add))
                        link(V.reciprocal(z[:, :], z[:, :]))
                        link(V.tensor_tensor(lg3, lg3, z[:, :].unsqueeze(2).broadcast_to([P, NT, experts]), ALU.mult))
                    for t in range(NT):
                        last = V.max(top3[:, t, :], lg3[:, t, :])
                    link(last)
                    for t in range(NT):
                        last = V.max_index(at[:, 8 * t:8 * t + 8], top3[:, t, :], lg3[:, t, :])
                    link(last)
                    link(V.tensor_copy(atf[:, :], at[:, :]))
                    for p in range(picks):
                        for e in range(experts):
                            last = V.tensor_scalar(masks[p][:, e * NT:(e + 1) * NT], atf3[:, :, p], float(e), None,
                                                   ALU.is_equal)
                    link(last)
                    if picks > 1:
                        link(V.tensor_tensor(total[:, :], masks[0][:, :], masks[1][:, :], ALU.add))
                    if mode == "top_of_softmax":
                        V.tensor_copy(r.weights[0][:, :], top3[:, :, 0])
                        link(V.tensor_copy(r.weights[1][:, :], top3[:, :, 1]))
                    if mode == "softmax_of_top":
                        V.tensor_tensor(m[:, :], top3[:, :, 1], top3[:, :, 0], ALU.subtract).then_inc(asked, 1)
                        dve.wait_ge(answered, 1)
                        link(V.tensor_scalar(z[:, :], m[:, :], 1.0, None, ALU.add))
                        link(V.reciprocal(r.weights[0][:, :], z[:, :]))
                        link(V.tensor_tensor(r.weights[1][:, :], r.weights[0][:, :], m[:, :], ALU.mult))

        place(nc, K, total[:, :], [(masks[p][:, :], rows[p][:, :], r.slots[p][:, :]) for p in range(picks)],
              P, experts, NT, r.chunks, r.bin[:, 0:r.chunks])
        with stage(nc) as st2:
            back = st2.sb("back", [P, r.chunks])
            scatter_items(nc, K, [(rows[p], token) for p in range(picks)], P, NT, 5, 1, 1, r.chunks, (0.0,), back[:, :])
            vector_work(nc, lambda: nc.vector.tensor_copy(r.idx[:, 0:r.chunks], back[:, :]))


def moe(nc, K, gate, w1, b1, w2, b2, picks, mode, func, relu_out=False, after=None):
    experts = w1.shape[0]
    with stage(nc) as st:
        r = Routing(st, picks, experts, mode is not None)
        layer_norm(nc, K, K.x, K.xn, table=K.table)
        route(nc, K, r, gate, experts, picks, mode)
        routed_ffn(nc, K, r, w1, b1, w2, b2, func, relu_out)
        if after is None:
            combine(nc, K, r.slots, r.weights, K.x, K.x)
        else:
            combine(nc, K, r.slots, r.weights, K.xn, K.agg)
            layer_norm(nc, K, K.agg, K.agg, affine=after, residual=True)


def one_hot(nc, edges, K, hot, i):
    at = edges.pay[:, bass.ds(i * (3 * GS), 3 * GS)].rearrange("p (c w) -> p c w", w=3)[:, :, 1]
    return nc.vector.tensor_tensor(hot, K.iota[:, 0:P].unsqueeze(1).broadcast_to([P, GS, P]),
                                   at.unsqueeze(2).broadcast_to([P, GS, P]), ALU.is_equal)


def attention_scores(nc, K, edges, q, k_table, scores):
    GR = 4 * GS
    S = CHUNKS // GS
    with stage(nc) as st:
        idxr = st.sb("idxr", [P, GR], I32)
        rows = st.sb("rows", [P, GR, D])
        hot = st.sb("hot", [P, 2, GS, P])
        hotT = st.sb("hotT", [P, 2, GS * P])
        prod = st.sb("prod", [P, 2, GS * D])
        gathered = [st.sem(f"gathered{j}") for j in range(4)]
        staged, passed, onehot, turned, copied, queried, product, scored = (
            st.sem(x) for x in ("staged", "passed", "onehot", "turned", "copied", "queried", "product", "scored"))
        with nc.Block() as block:

            @block.gpsimd
            def _(pool):
                gather_rows(nc, pool, edges, k_table, rows, idxr, gathered, staged, passed, scored, GS)

            @block.vector
            def _(dve):
                def step(i, j, k):
                    if runs(i, S):
                        wait_count(dve, turned, i - 1)
                        one_hot(nc, edges, K, hot[:, j % 2, :, :], i).then_inc(onehot, 1)
                    if runs(i - 2, S):
                        c, jj = i - 2, (j - 2) % 4
                        dve.wait_ge(queried, c + 1)
                        dve.wait_ge(gathered[jj], 16 * GS * ((k if j >= 2 else k - 1) + 1))
                        wait_count(dve, scored, c - 1)
                        for hh in range(2):
                            last = nc.vector.tensor_tensor(
                                prod[:, jj % 2, hh * 2 * D:(hh + 1) * 2 * D].rearrange("p (c d) -> p c d", d=D),
                                K.ps[2 + 2 * (jj % 2) + hh][:, 0:2 * D].rearrange("p (c d) -> p c d", d=D),
                                rows[:, GS * jj + 2 * hh:GS * jj + 2 * hh + 2, :], ALU.mult)
                        last.then_inc(product, 1)
                        dve.wait_ge(product, c + 1)
                        nc.vector.tensor_reduce(scores[:, bass.ds(c * (GS * HEADS), GS * HEADS)],
                                                prod[:, jj % 2, :].rearrange("p (h d) -> p h d", d=DH),
                                                AX.X, ALU.add).then_inc(scored, 1)

                steps(dve, S, 4, 2, step)

            @block.tensor
            def _(pe):
                def step(i, j, k):
                    if runs(i, S):
                        pe.wait_ge(onehot, i + 1)
                        wait_count(pe, copied, i - 1)
                        for g in range(GS):
                            last = nc.tensor.transpose(K.ps[j % 2][:, g * P:(g + 1) * P], hot[:, j % 2, g, :], K.ident[:, :])
                        last.then_inc(turned, 1)
                    if runs(i - 1, S):
                        c, jj = i - 1, (j - 1) % 4
                        pe.wait_ge(copied, c + 1)
                        wait_count(pe, product, c - 1)
                        for g in range(GS):
                            t = pe.value_load(edges.bin[0:1, bass.ds(c * GS + g, 1)], min_val=0, max_val=NT - 1)
                            last = nc.tensor.matmul(K.ps[2 + 2 * (jj % 2) + g // 2][:, g % 2 * D:(g % 2 + 1) * D],
                                                    hotT[:, jj % 2, g * P:(g + 1) * P], tile_of(q, t),
                                                    start=True, stop=True)
                        last.then_inc(queried, 1)

                steps(pe, S, 4, 1, step)

            @block.scalar
            def _(act):
                def step(i, j, k):
                    act.wait_ge(turned, i + 1)
                    wait_count(act, queried, i - 1)
                    nc.scalar.activation(hotT[:, j % 2, :], K.ps[j % 2][:, :], ACT.Copy).then_inc(copied, 1)

                steps(act, S, 4, 0, step)


def turn(nc, K, src, dst):
    groups = [range(g, min(g + 4, PER)) for g in range(0, PER, 4)]
    with stage(nc) as st:
        turned = st.sem("turned")
        with nc.Block() as block:

            @block.tensor
            def _(pe):
                for g, group in enumerate(groups):
                    for o in group:
                        last = nc.tensor.transpose(K.ps[g][:, (o % 4) * P:(o % 4 + 1) * P], src[:, o * P:(o + 1) * P],
                                                   K.ident[:, :])
                    last.then_inc(turned, 1)

            def copies(parity, wait, copy):
                for g, group in enumerate(groups):
                    if g % 2 == parity:
                        wait(turned, g + 1)
                        for o in group:
                            view, shape = dst(o)
                            square = K.ps[g][:, (o % 4) * P:(o % 4 + 1) * P]
                            copy(view, square if shape is None else square.rearrange("p (b h) -> p b h", h=HEADS))

            @block.vector
            def _(dve):
                copies(0, dve.wait_ge, nc.vector.tensor_copy)

            @block.scalar
            def _(act):
                copies(1, act.wait_ge, lambda o, i: nc.scalar.activation(o, i, ACT.Copy))


class Segments:

    def __init__(self, st):
        self.reset = st.sb("reset", [P, SPAN + 1])
        self.of_block = st.sb("of_block", [P, BLOCKS])
        self.of_head = st.sb("of_head", [P, HEADS])
        self.of_headT = st.sb("of_headT", [HEADS, P])
        self.joint = st.sb("joint", [HEADS, BLOCKS])
        self.through_f = st.sb("through_f", [HEADS, BLOCKS])
        self.through_r = st.sb("through_r", [HEADS, BLOCKS])


def by_offset(buf, width):
    return buf.rearrange("p (b o w) -> p b o w", b=BLOCKS, w=width)


def find_segments(nc, K, edges, G):
    B = BLOCKS
    with stage(nc) as st:
        nodes = st.sb("nodes", [P, PER * P])
        nodesT = st.sb("nodesT", [P, SPAN])
        ends = st.sb("ends", [P, 3 * B])
        small = st.sb("small", [HEADS, 3 * B])
        low = st.sb("low", [P, 1])
        nodes4 = nodes[:, :].rearrange("p (o b h) -> p b o h", b=B, h=HEADS)
        node = by_offset(edges.pay[:, :], 3)[:, :, :, 2]
        vector_work(nc, *[lambda h=h: nc.vector.tensor_copy(nodes4[:, :, :, h], node) for h in range(HEADS)])
        turn(nc, K, nodes, lambda o: (nodesT[:, o * P:(o + 1) * P], None))
        chain, packed, moved = st.sem("chain"), st.sem("packed"), st.sem("moved")
        with nc.Block() as block:

            @block.tensor
            def _(pe):
                pe.wait_ge(packed, 1)
                nc.tensor.matmul(K.ps[0][0:HEADS, 0:3 * B], G.of_head[:, :], ends[:, :], start=True, stop=True).then_inc(moved, 1)

            @block.vector
            def _(dve):
                link = linker(dve, chain)
                V = nc.vector
                ident = K.ident[:, :]
                V.tensor_reduce(G.of_block[:, :], ident.rearrange("p (b h) -> p b h", h=HEADS), AX.X, ALU.add)
                V.tensor_reduce(G.of_head[:, :], ident.rearrange("p (b h) -> p h b", h=HEADS), AX.X, ALU.add)
                V.tensor_copy(G.of_headT[:, :].rearrange("g (b h) -> g b h", h=HEADS),
                              K.ident[0:HEADS, 0:HEADS].unsqueeze(1).broadcast_to([HEADS, B, HEADS]))
                link(V.memset(G.reset[:, :], 0.0))
                link(V.tensor_tensor(G.reset[:, 1:SPAN], nodesT[:, 1:SPAN], nodesT[:, 0:SPAN - 1], ALU.not_equal))
                link(V.tensor_scalar(G.reset[:, 1:SPAN], G.reset[:, 1:SPAN], -BIG, None, ALU.mult))
                link(V.tensor_reduce(low[:, :], G.reset[:, :], AX.X, ALU.min))
                for n, value in enumerate((nodesT[:, 0:1], nodesT[:, SPAN - 1:SPAN], low[:, 0:1])):
                    last = V.tensor_scalar(ends[:, n * B:(n + 1) * B], G.of_block[:, :], value, None, ALU.mult)
                last.then_inc(packed, 1)
                dve.wait_ge(moved, 1)
                link(V.tensor_copy(small[:, :], K.ps[0][0:HEADS, 0:3 * B]))
                link(V.memset(G.joint[:, :], -BIG))
                link(V.tensor_tensor(G.joint[:, 1:B], small[:, 1:B], small[:, B:2 * B - 1], ALU.not_equal))
                link(V.tensor_scalar(G.joint[:, 1:B], G.joint[:, 1:B], -BIG, None, ALU.mult))
                link(V.memset(G.through_r[:, :], -BIG))
                V.tensor_tensor(G.through_f[:, :], G.joint[:, :], small[:, 2 * B:3 * B], ALU.min)
                link(V.tensor_tensor(G.through_r[:, 0:B - 1], G.joint[:, 1:B], small[:, 2 * B:3 * B - 1], ALU.min))


def attention_weights(nc, K, G, scores):
    B = BLOCKS
    with stage(nc) as st:
        packed = st.sb("packed", [P, PER * P])
        scoresT = st.sb("scoresT", [P, SPAN])
        peak = st.sb("peak", [P, SPAN])
        ends = st.sb("ends", [P, B])
        small = st.sb("small", [HEADS, B])
        scan = st.sb("scan", [HEADS, B])
        past = st.sb("past", [HEADS, B])
        into = st.sb("into", [P, 1])
        scores4 = by_offset(scores[:, :], HEADS)
        packed4 = packed[:, :].rearrange("p (o b h) -> p b o h", b=B, h=HEADS)
        vector_work(nc, *[lambda b=b: nc.vector.tensor_copy(packed4[:, b, :, :], scores4[:, b, :, :]) for b in range(B)])
        turn(nc, K, packed, lambda o: (scoresT[:, o * P:(o + 1) * P], None))
        with stage(nc) as st2:
            chain, shifted, raised = (st2.sem(x) for x in ("chain", "shifted", "raised"))
            ended, moved, carried, spread = (st2.sem(x) for x in ("ended", "moved", "carried", "spread"))
            with nc.Block() as block:

                @block.tensor
                def _(pe):
                    for way in range(2):
                        pe.wait_ge(ended, way + 1)
                        nc.tensor.matmul(K.ps[0][0:HEADS, 0:B], G.of_head[:, :], ends[:, :], start=True,
                                         stop=True).then_inc(moved, 1)
                        pe.wait_ge(carried, way + 1)
                        nc.tensor.matmul(K.ps[1][:, 0:B], G.of_headT[:, :], past[:, :], start=True, stop=True).then_inc(spread, 1)

                @block.vector
                def _(dve):
                    link = linker(dve, chain)
                    V = nc.vector
                    for way, (reset, over, goal, last, through, at, fro, to) in enumerate((
                            (G.reset[:, 0:SPAN], scoresT[:, :], peak[:, :], peak[:, SPAN - 1:SPAN], G.through_f[:, :],
                             slice(0, B - 1), slice(1, B), 0),
                            (G.reset[:, 1:SPAN + 1], scoresT[:, :], packed[:, 0:SPAN], packed[:, 0:1], G.through_r[:, :],
                             slice(1, B), slice(0, B - 1), B - 1))):
                        flip = (lambda a: a) if way == 0 else (lambda a: a[:, ::-1])
                        link(V.tensor_tensor_scan(flip(goal), flip(reset), flip(over), -BIG, ALU.add, ALU.max))
                        V.tensor_scalar(ends[:, :], G.of_block[:, :], last, None, ALU.mult).then_inc(ended, 1)
                        dve.wait_ge(moved, way + 1)
                        link(V.tensor_copy(small[:, :], K.ps[0][0:HEADS, 0:B]))
                        link(V.tensor_tensor_scan(flip(scan[:, :]), flip(through), flip(small[:, :]), -BIG, ALU.add, ALU.max))
                        link(V.memset(past[:, :], -BIG))
                        V.tensor_tensor(past[:, fro], scan[:, at], G.joint[:, 1:B], ALU.add).then_inc(carried, 1)
                        dve.wait_ge(spread, way + 1)
                        link(V.tensor_tensor(ends[:, :], K.ps[1][:, 0:B], G.of_block[:, :], ALU.mult))
                        link(V.tensor_reduce(into[:, :], ends[:, :], AX.X, ALU.add))
                        if way == 0:
                            link(V.tensor_tensor_scan(goal, reset, over, into[:, 0:1], ALU.add, ALU.max))
                        else:
                            link(V.tensor_tensor_scan(flip(goal), flip(reset), flip(over), into[:, 0:1], ALU.add, ALU.max))
                    link(V.tensor_tensor(peak[:, :], peak[:, :], packed[:, 0:SPAN], ALU.max))
                    V.tensor_tensor(scoresT[:, :], scoresT[:, :], peak[:, :], ALU.subtract).then_inc(shifted, 1)

                @block.scalar
                def _(act):
                    act.wait_ge(shifted, 1)
                    nc.scalar.activation(scoresT[:, :], scoresT[:, :], ACT.Exp).then_inc(raised, 1)

        turn(nc, K, scoresT, lambda o: (scores4[:, :, o, :], True))


def attention_values(nc, K, edges, v_table, weights, acc):
    GR, W = 4 * GS, D + HEADS
    S = CHUNKS // GS
    with stage(nc) as st:
        idxr = st.sb("idxr", [P, GR], I32)
        rows = st.sb("rows", [P, GR, D])
        hot = st.sb("hot", [P, 2, GS, P])
        msg = st.sb("msg", [P, 2, GS, W])
        run = st.sb("run", [P, RUNS, W])
        gathered = [st.sem(f"gathered{j}") for j in range(4)]
        staged, passed, placed, weighed, summed, ran, kept, cleared = (
            st.sem(x) for x in ("staged", "passed", "placed", "weighed", "summed", "ran", "kept", "cleared"))
        with nc.Block() as block:

            @block.gpsimd
            def _(pool):
                gather_rows(nc, pool, edges, v_table, rows, idxr, gathered, staged, passed, weighed, GS)

            @block.vector
            def _(dve):
                nc.vector.memset(acc[:, :], 0.0)
                nc.vector.memset(run[:, RUNS - 1, :], 0.0).then_inc(cleared, 1)
                dve.wait_ge(cleared, 1)

                def step(i, j, k):
                    if runs(i - 2, S):
                        for g in range(GS):
                            carry(nc, dve, edges, (run[:, (g - 1) % RUNS, :], run[:, g, :]),
                                  K.ps[j % 2 * GS + g][:, 0:W], (i - 2) * GS + g, W, summed, kept, ran)
                    if runs(i, S):
                        one_hot(nc, edges, K, hot[:, j % 2, :, :], i)
                        dve.wait_ge(gathered[j], 16 * GS * (k + 1))
                        nc.vector.tensor_tensor(
                            msg[:, j % 2, :, 0:D].rearrange("p c (h d) -> p c h d", d=DH),
                            rows[:, GS * j:GS * (j + 1), :].rearrange("p c (h d) -> p c h d", d=DH),
                            weights[:, bass.ds(i * (GS * HEADS), GS * HEADS)].rearrange("p (c h) -> p c h", h=HEADS)
                            .unsqueeze(3).broadcast_to([P, GS, HEADS, DH]), ALU.mult).then_inc(weighed, 1)

                steps(dve, S, 4, 2, step)

            @block.tensor
            def _(pe):
                def step(i, j, k):
                    pe.wait_ge(weighed, i + 1)
                    pe.wait_ge(placed, i + 1)
                    for g in range(GS):
                        wait_count(pe, ran, (i - 2) * GS + g + 1)
                        nc.tensor.matmul(K.ps[j % 2 * GS + g][:, 0:W], hot[:, j % 2, g, :], msg[:, j % 2, g, :],
                                         start=True, stop=True).then_inc(summed, 1)

                steps(pe, S, 4, 0, step)

            @block.scalar
            def _(act):
                act.wait_ge(cleared, 1)

                def step(i, j, k):
                    if runs(i, S):
                        wait_count(act, summed, (i - 1) * GS)
                        nc.scalar.activation(msg[:, j % 2, :, D:W],
                                             weights[:, bass.ds(i * (GS * HEADS), GS * HEADS)]
                                             .rearrange("p (c h) -> p c h", h=HEADS), ACT.Copy).then_inc(placed, 1)
                    if runs(i - 2, S):
                        for g in range(GS):
                            keep(nc, act, edges, acc, run[:, g, :], (i - 2) * GS + g, W, ran, kept)

                steps(act, S, 4, 2, step)


def node_mlp(nc, K, src, w1, b1, w2, b2):
    hid = w1.shape[1]
    nh = hid // P
    with stage(nc) as st:
        w1s = st.sb("w1s", [P, KD, hid])
        w2s = st.sb("w2s", [P, nh, D])
        b1T = st.sb("b1T", [P, nh])
        b2s = st.sb("b2s", [1, D])
        raw = st.sb("raw", [P, 2, D])
        xT = st.sb("xT", [P, 2, D])
        hT = st.sb("hT", [P, 2, hid])
        loaded, staged, turned, copied, hidden, acted, summed, added = (
            st.sem(x) for x in ("loaded", "staged", "turned", "copied", "hidden", "acted", "summed", "added"))
        with nc.Block() as block:

            @block.sync
            def _(sp):
                sp.dma_start(w1s[:, :, :], w1.rearrange("(k p) h -> p k h", p=P)).then_inc(loaded, 16)
                sp.dma_start(w2s[:, :, :], w2.rearrange("(c p) d -> p c d", p=P)).then_inc(loaded, 16)
                sp.dma_start(b1T[:, :], b1.rearrange("(c p) -> p c", p=P)).then_inc(loaded, 16)
                sp.dma_start(b2s[:, :], b2.rearrange("(o d) -> o d", o=1)).then_inc(loaded, 16)

            @block.scalar
            def _(act):
                act.wait_ge(loaded, 64)

                def step(i, j, k):
                    act.wait_ge(hidden, i + 1)
                    wait_count(act, summed, i - 1)
                    for h in range(nh):
                        last = nc.scalar.activation(hT[:, j, h * P:(h + 1) * P],
                                                    K.ps[2 + 2 * j + h // 4][:, h % 4 * P:(h % 4 + 1) * P], ACT.Relu,
                                                    bias=b1T[:, h:h + 1])
                    last.then_inc(acted, 1)

                steps(act, NT, 2, 0, step)

            @block.tensor
            def _(pe):
                pe.wait_ge(loaded, 64)

                def step(i, j4, k):
                    j = j4 % 2
                    if runs(i, NT):
                        pe.wait_ge(staged, i + 1)
                        wait_count(pe, copied, i)
                        for s in range(KD):
                            last = nc.tensor.transpose(K.ps[0][:, s * P:(s + 1) * P], raw[:, j, s * P:(s + 1) * P],
                                                       K.ident[:, :])
                        last.then_inc(turned, 1)
                    if runs(i - 1, NT):
                        c, jj = i - 1, 1 - j
                        pe.wait_ge(copied, c + 1)
                        wait_count(pe, acted, c - 1)
                        for h in range(nh):
                            for s in range(KD):
                                last = nc.tensor.matmul(K.ps[2 + 2 * jj + h // 4][:, h % 4 * P:(h % 4 + 1) * P],
                                                        w1s[:, s, h * P:(h + 1) * P], xT[:, jj, s * P:(s + 1) * P],
                                                        start=(s == 0), stop=(s == KD - 1))
                        last.then_inc(hidden, 1)
                    if runs(i - 2, NT):
                        c, jj = i - 2, j
                        pe.wait_ge(acted, c + 1)
                        wait_count(pe, added, c - 1)
                        bank = K.ps[6 + jj][:, 0:D]
                        for h in range(nh):
                            nc.tensor.matmul(bank, hT[:, jj, h * P:(h + 1) * P], w2s[:, h, :], start=(h == 0), stop=False)
                        nc.tensor.matmul(bank, K.ones[0:1, :], b2s[0:1, :], start=False, stop=True).then_inc(summed, 1)

                steps(pe, NT, 4, 2, step)

            @block.vector
            def _(dve):
                def step(i, j4, k):
                    j = j4 % 2
                    if runs(i, NT):
                        wait_count(dve, turned, i - 1)
                        nc.vector.tensor_copy(raw[:, j, :], tile_of(src, i)).then_inc(staged, 1)
                    if runs(i - 1, NT):
                        dve.wait_ge(turned, i)
                        wait_count(dve, hidden, i - 2)
                        nc.vector.tensor_copy(xT[:, 1 - j, :], K.ps[0][:, 0:D]).then_inc(copied, 1)
                    if runs(i - 3, NT):
                        dve.wait_ge(summed, i - 2)
                        nc.vector.tensor_tensor(tile_of(K.x, i - 3), tile_of(K.x, i - 3), K.ps[6 + (1 - j)][:, 0:D],
                                                ALU.add).then_inc(added, 1)

                steps(dve, NT, 4, 3, step)


def node_to_feature(nc, K, src, w, b, dst):
    with stage(nc) as st:
        ws = st.sb("ws", [P, KD, D])
        bs = st.sb("bs", [P, KD])
        raw = st.sb("raw", [P, 2, D])
        xT = st.sb("xT", [P, 2, D])
        loaded, staged, turned, copied, summed, written = (
            st.sem(x) for x in ("loaded", "staged", "turned", "copied", "summed", "written"))
        with nc.Block() as block:

            @block.sync
            def _(sp):
                sp.dma_start(ws[:, :, :], w.rearrange("(k p) n -> p k n", p=P)).then_inc(loaded, 16)
                sp.dma_start(bs[:, :], b.rearrange("(k p) -> p k", p=P)).then_inc(loaded, 16)

            @block.scalar
            def _(act):
                def step(i, j, k):
                    if runs(i, NT):
                        wait_count(act, turned, i - 1)
                        nc.scalar.activation(raw[:, j, :], tile_of(src, i), ACT.Copy).then_inc(staged, 1)
                    if runs(i - 1, NT):
                        act.wait_ge(turned, i)
                        wait_count(act, summed, i - 2)
                        nc.scalar.activation(xT[:, 1 - j, :], K.ps[1 - j][:, 0:D], ACT.Copy).then_inc(copied, 1)

                steps(act, NT, 2, 1, step)

            @block.tensor
            def _(pe):
                pe.wait_ge(loaded, 32)

                def step(i, j, k):
                    if runs(i, NT):
                        pe.wait_ge(staged, i + 1)
                        wait_count(pe, copied, i - 1)
                        for s in range(KD):
                            last = nc.tensor.transpose(K.ps[j][:, s * P:(s + 1) * P], raw[:, j, s * P:(s + 1) * P],
                                                       K.ident[:, :])
                        last.then_inc(turned, 1)
                    if runs(i - 1, NT):
                        pe.wait_ge(copied, i)
                        wait_count(pe, written, i - 2)
                        for o in range(KD):
                            for s in range(KD):
                                last = nc.tensor.matmul(K.ps[2 + 2 * (1 - j) + o][:, 0:P], ws[:, s, o * P:(o + 1) * P],
                                                        xT[:, 1 - j, s * P:(s + 1) * P], start=(s == 0), stop=(s == KD - 1))
                        last.then_inc(summed, 1)

                steps(pe, NT, 2, 1, step)

            @block.vector
            def _(dve):
                dve.wait_ge(loaded, 32)

                def step(t, j, k):
                    dve.wait_ge(summed, t + 1)
                    for o in range(KD):
                        last = nc.vector.tensor_scalar(dst[:, bass.ds(t * P + o * NPAD, P)], K.ps[2 + 2 * j + o][:, 0:P],
                                                       bs[:, o:o + 1], None, ALU.add)
                    last.then_inc(written, 1)

                steps(dve, NT, 2, 0, step)


def feature_to_feature(nc, K, src, w, b, dst):
    with stage(nc) as st:
        ws = st.sb("ws", [P, KD, D])
        bs = st.sb("bs", [P, KD])
        loaded, summed, written = (st.sem(x) for x in ("loaded", "summed", "written"))
        with nc.Block() as block:

            @block.sync
            def _(sp):
                sp.dma_start(ws[:, :, :], w.rearrange("(k p) n -> p k n", p=P)).then_inc(loaded, 16)
                sp.dma_start(bs[:, :], b.rearrange("(k p) -> p k", p=P)).then_inc(loaded, 16)

            @block.tensor
            def _(pe):
                pe.wait_ge(loaded, 32)

                def step(t, j, k):
                    wait_count(pe, written, t - 1)
                    for o in range(KD):
                        for s in range(KD):
                            last = nc.tensor.matmul(K.ps[2 * j + o][:, 0:P], ws[:, s, o * P:(o + 1) * P],
                                                    src[:, bass.ds(t * P + s * NPAD, P)], start=(s == 0), stop=(s == KD - 1))
                    last.then_inc(summed, 1)

                steps(pe, NT, 2, 0, step)

            @block.vector
            def _(dve):
                dve.wait_ge(loaded, 32)

                def step(t, j, k):
                    dve.wait_ge(summed, t + 1)
                    for o in range(KD):
                        last = nc.vector.tensor_scalar(dst[:, bass.ds(t * P + o * NPAD, P)], K.ps[2 * j + o][:, 0:P],
                                                       bs[:, o:o + 1], None, ALU.add)
                    last.then_inc(written, 1)

                steps(dve, NT, 2, 0, step)


def batch_norm_scale(nc, K, src, gamma, beta, scale, shift):
    CH = 512
    spans = [(a, min(CH, NODES - a)) for a in range(0, NODES, CH)]
    with stage(nc) as st:
        stats = st.sb("stats", [P, KD, len(spans) * 6])
        mv = st.sb("mv", [P, KD, 2])
        gb = st.sb("gb", [P, 2, KD])
        rstd = st.sb("rstd", [P, KD])
        tmp = st.sb("tmp", [P, KD])
        loaded, chain, asked, root = (st.sem(x) for x in ("loaded", "chain", "asked", "root"))
        with nc.Block() as block:

            @block.sync
            def _(sp):
                sp.dma_start(gb[:, 0, :], gamma.rearrange("(k p) -> p k", p=P)).then_inc(loaded, 16)
                sp.dma_start(gb[:, 1, :], beta.rearrange("(k p) -> p k", p=P)).then_inc(loaded, 16)

            @block.scalar
            def _(act):
                act.wait_ge(asked, 1)
                nc.scalar.activation(rstd[:, :], rstd[:, :], ACT.Sqrt).then_inc(root, 1)

            @block.vector
            def _(dve):
                link = linker(dve, chain)
                V = nc.vector
                for o in range(KD):
                    for n, (a, w) in enumerate(spans):
                        last = V.bn_stats(stats[:, o, 6 * n:6 * n + 6], src[:, o * NPAD + a:o * NPAD + a + w])
                link(last)
                for o in range(KD):
                    last = V.bn_aggr(mv[:, o, :], stats[:, o, :])
                link(last)
                V.tensor_scalar(rstd[:, :], mv[:, :, 1], EPS, None, ALU.add).then_inc(asked, 1)
                dve.wait_ge(root, 1)
                dve.wait_ge(loaded, 32)
                link(V.reciprocal(rstd[:, :], rstd[:, :]))
                link(V.tensor_tensor(scale[:, :], rstd[:, :], gb[:, 0, :], ALU.mult))
                link(V.tensor_tensor(tmp[:, :], scale[:, :], mv[:, :, 0], ALU.mult))
                link(V.tensor_tensor(shift[:, :], gb[:, 1, :], tmp[:, :], ALU.subtract))


def batch_norm_relu(nc, K, buf, scale, shift):
    with stage(nc) as st:
        done = st.sem("done")
        with nc.Block() as block:

            @block.scalar
            def _(act):
                for o in range(KD):
                    nc.scalar.activation(buf[:, o * NPAD:(o + 1) * NPAD], buf[:, o * NPAD:(o + 1) * NPAD], ACT.Relu,
                                         bias=shift[:, o:o + 1], scale=scale[:, o:o + 1]).then_inc(done, 1)


def batch_norm_relu_to_nodes(nc, K, src, scale, shift, h, table):
    with stage(nc) as st:
        raw = st.sb("raw", [P, 2, D])
        normed, turned, written, stored = (st.sem(x) for x in ("normed", "turned", "written", "stored"))
        with nc.Block() as block:

            @block.scalar
            def _(act):
                def step(t, j, k):
                    wait_count(act, turned, t - 1)
                    for o in range(KD):
                        last = nc.scalar.activation(raw[:, j, o * P:(o + 1) * P], src[:, bass.ds(t * P + o * NPAD, P)],
                                                    ACT.Relu, bias=shift[:, o:o + 1], scale=scale[:, o:o + 1])
                    last.then_inc(normed, 1)

                steps(act, NT, 2, 0, step)

            @block.tensor
            def _(pe):
                def step(t, j, k):
                    pe.wait_ge(normed, t + 1)
                    wait_count(pe, written, t - 1)
                    for o in range(KD):
                        last = nc.tensor.transpose(K.ps[j][:, o * P:(o + 1) * P], raw[:, j, o * P:(o + 1) * P], K.ident[:, :])
                    last.then_inc(turned, 1)

                steps(pe, NT, 2, 0, step)

            @block.vector
            def _(dve):
                def step(t, j, k):
                    dve.wait_ge(turned, t + 1)
                    if h is None:
                        ins = nc.vector.tensor_tensor(tile_of(K.x, t), tile_of(K.x, t), K.ps[j][:, 0:D], ALU.add)
                    else:
                        ins = nc.vector.tensor_copy(tile_of(h, t), K.ps[j][:, 0:D])
                    ins.then_inc(written, 1)

                steps(dve, NT, 2, 0, step)

            @block.sync
            def _(sp):
                if h is not None:
                    def step(t, j, k):
                        sp.wait_ge(written, t + 1)
                        sp.dma_start(tile_rows(table, t), tile_of(h, t)).then_inc(stored, 16)

                    steps(sp, NT, 2, 0, step)
                    sp.wait_ge(stored, 16 * NT)


def layer0_gnn(nc, K, A):
    layer_norm(nc, K, K.x, K.xn, table=K.table)
    spmm(nc, K, K.by_src, K.table, K.agg)
    dense(nc, K, [K.agg], [[A["L0_gnn_weight"]]], None, [(D, "relu_add", None, None)])


def layer1_gnn(nc, K, A):
    layer_norm(nc, K, K.x, K.xn, table=K.table)
    spmm(nc, K, K.by_src, K.table, K.agg)
    dense(nc, K, [K.xn, K.agg], [[A["L1_gnn_weight"][0:D, :]], [A["L1_gnn_weight"][D:2 * D, :]]],
          A["L1_gnn_bias"].rearrange("(o n) -> o n", o=1), [(D, "add", K.x, None)])


def layer2_gnn(nc, K, A):
    layer_norm(nc, K, K.x, K.xn)
    W = D + HEADS
    q = K.agg
    with stage(nc) as st:
        G = Segments(st)
        find_segments(nc, K, K.by_dst, G)
        scores = st.sb("scores", [P, CHUNKS * HEADS])
        for l in range(2):
            dense(nc, K, [K.xn], [[A["L2_gnn_Wq"][l], A["L2_gnn_Wk"][l], A["L2_gnn_Wv"][l]]], None,
                  [(D, "sb", q, float(DH) ** -0.5), (D, "table", K.table, None), (D, "table", K.table2, None)])
            attention_scores(nc, K, K.by_dst, q, K.table, scores)
            attention_weights(nc, K, G, scores)
            with stage(nc) as st2:
                acc = st2.sb("acc", [P, NT * W])
                z = st2.sb("z", [P, NT * HEADS])
                acc4 = acc[:, :].rearrange("p (t w) -> p t w", w=W)
                z3 = z[:, :].rearrange("p (t h) -> p t h", h=HEADS)
                agg4 = K.agg[:, :].rearrange("p (t h d) -> p t h d", t=NT, h=HEADS)
                attention_values(nc, K, K.by_dst, K.table2, scores, acc)
                vector_work(
                    nc,
                    lambda: nc.vector.tensor_scalar(z3, acc4[:, :, D:W], 1e-9, None, ALU.add),
                    lambda: nc.vector.reciprocal(z[:, :], z[:, :]),
                    lambda: nc.vector.tensor_tensor(agg4, acc4[:, :, 0:D].rearrange("p t (h d) -> p t h d", h=HEADS),
                                                    z3.unsqueeze(3).broadcast_to([P, NT, HEADS, DH]), ALU.mult))
            dense(nc, K, [K.agg], [[A["L2_gnn_Wo"][l]]], None, [(D, "add", K.xn, None)])
            layer_norm(nc, K, K.xn, K.xn, affine=(A["L2_gnn_ln_g"][l], A["L2_gnn_ln_b"][l]))
    node_mlp(nc, K, K.xn, A["L2_gnn_w1"], A["L2_gnn_b1"], A["L2_gnn_w2"], A["L2_gnn_b2"])


def layer3_gnn(nc, K, A):
    layer_norm(nc, K, K.x, K.xn)
    with stage(nc) as st:
        yT = st.sb("yT", [P, KD * NPAD])
        scale = st.sb("scale", [P, KD])
        shift = st.sb("shift", [P, KD])
        dense(nc, K, [K.xn], [[A["L3_gnn_W_in"]]], A["L3_gnn_b_in"].rearrange("(o n) -> o n", o=1),
              [(D, "both", (K.xn, K.table), None)])
        layers = A["L3_gnn_W1"].shape[0]
        for l in range(layers):
            spmm(nc, K, K.by_src, K.table, K.agg)
            vector_work(nc, lambda: nc.vector.tensor_tensor(K.agg[:, :], K.agg[:, :], K.xn[:, :], ALU.add))
            node_to_feature(nc, K, K.agg, A["L3_gnn_W1"][l], A["L3_gnn_b1"][l], yT)
            batch_norm_scale(nc, K, yT, A["L3_gnn_g1"][l], A["L3_gnn_be1"][l], scale, shift)
            batch_norm_relu(nc, K, yT, scale, shift)
            feature_to_feature(nc, K, yT, A["L3_gnn_W2"][l], A["L3_gnn_b2"][l], K.agg)
            batch_norm_scale(nc, K, K.agg, A["L3_gnn_g_out"][l], A["L3_gnn_b_out"][l], scale, shift)
            last = l == layers - 1
            batch_norm_relu_to_nodes(nc, K, K.agg, scale, shift, None if last else K.xn, K.table)


def build(nc, A, out, upto=99):
    with stage(nc) as st:
        st.stack.enter_context(nc.allow_non_contiguous_dma(reason="short rows of biases and of the L3 router"))
        K = Core(nc, st)
        make_constants(nc, K)
        sort_edges(nc, K, A["src"], A["dst"], A["edge_weight"], K.by_src, False)
        sort_edges(nc, K, A["dst"], A["src"], A["edge_weight"], K.by_dst, True)
        K.x, K.xn, K.agg = (st.sb(n, [P, NT * D]) for n in ("x", "xn", "agg"))
        load_nodes(nc, K, A["x"])
        layers = [
            lambda: layer0_gnn(nc, K, A),
            lambda: moe(nc, K, (A["L0_ffn_gate_w"], A["L0_ffn_gate_b"]), A["L0_ffn_w1"], A["L0_ffn_b1"], A["L0_ffn_w2"], A["L0_ffn_b2"],
                        2, "softmax_of_top", ACT.Relu, after=(A["L0_ffn_gamma"], A["L0_ffn_beta"])),
            lambda: layer1_gnn(nc, K, A),
            lambda: moe(nc, K, (A["L1_ffn_Wg"], A["L1_ffn_bg"]), A["L1_ffn_W1"], A["L1_ffn_b1"], A["L1_ffn_W2"], A["L1_ffn_b2"],
                        2, None, ACT.Gelu),
            lambda: layer2_gnn(nc, K, A),
            lambda: moe(nc, K, (A["L2_ffn_gate_w"], A["L2_ffn_gate_b"]), A["L2_ffn_W1"], A["L2_ffn_b1"], A["L2_ffn_W2"], A["L2_ffn_b2"],
                        2, "top_of_softmax", ACT.Gelu),
            lambda: layer3_gnn(nc, K, A),
            lambda: moe(nc, K, (A["L3_ffn_router_w"].rearrange("e d -> d e"), A["L3_ffn_router_b"]), A["L3_ffn_W1"], A["L3_ffn_b1"],
                        A["L3_ffn_W2"], A["L3_ffn_b2"], 1, None, ACT.Relu, relu_out=True),
        ]
        for layer in layers[:upto]:
            layer()
        store_nodes(nc, K, out)


def kernel(**inputs):
    import numpy as np
    import concourse.bacc as bacc
    from concourse.bass_utils import run_bass_kernel_spmd

    nc = bacc.Bacc("TRN2", target_bir_lowering=False, num_devices=1)
    arrays, A = {}, {}
    for name, value in inputs.items():
        a = np.ascontiguousarray(value)
        arrays[f"in_{name}"] = a
        A[name] = nc.dram_tensor(f"in_{name}", a.shape, mybir.dt.from_np(a.dtype), kind="ExternalInput").ap()
    out = nc.dram_tensor("out", (NODES, D), FP, kind="ExternalOutput").ap()
    build(nc, A, out)
    r = run_bass_kernel_spmd(nc, [arrays], core_ids=[0])
    return r.results[0]["out"]
```

```python
import concourse.bass as bass
from concourse import mybir
from contextlib import ExitStack, contextmanager

FP = mybir.dt.float32
BF = mybir.dt.bfloat16
I32 = mybir.dt.int32
U32 = mybir.dt.uint32
ALU = mybir.AluOpType
ACT = mybir.ActivationFunctionType
AX = mybir.AxisListType

P = 128
D = 256
KD = D // P
NODES = 3125
NT = (NODES + P - 1) // P
NPAD = NT * P
LAST = NODES - (NT - 1) * P
EDGES = 50000
EP = 125
EC = EDGES // EP
EU = 16
CHUNKS = -(-((EDGES + NT * (P - 1)) // P) // EU) * EU
HEADS = 8
DH = D // HEADS
EPS = 1e-5
BIG = float(2.0 ** 99)
BLOCKS = P // HEADS
PER = -(-CHUNKS // BLOCKS)
SPAN = PER * P
RUNS = 4
GS = 4


def token_chunks(picks, experts):
    return (picks * NPAD + experts * (P - 1)) // P


def steps(eng, n, unroll, lag, step):
    for i in range(unroll):
        step(i, i, 0)
    if n // unroll > 1:
        with eng.Fori(1, n // unroll) as k:
            for j in range(unroll):
                step(unroll * k + j, j, k)
    for i in range(n // unroll * unroll, n + lag):
        step(i, i % unroll, i // unroll)


def runs(c, n):
    return not isinstance(c, int) or 0 <= c < n


def wait_count(eng, sem, count):
    if not isinstance(count, int) or count > 0:
        eng.wait_ge(sem, count)


def wait_staged(pool, sem, count, passed):
    pool.wait_ge(sem, count)
    pool.sem_inc(passed, 1)


def linker(eng, sem):
    n = [0]

    def link(ins):
        n[0] += 1
        ins.then_inc(sem, 1)
        eng.wait_ge(sem, n[0])

    return link


class Stage:

    def __init__(self, nc, stack):
        self.nc, self.stack, self.sems = nc, stack, []

    def sem(self, name):
        self.sems.append(self.nc.alloc_semaphore(f"{name}_{self.nc.next_id()}"))
        return self.sems[-1]

    def sb(self, name, shape, dt=FP):
        return self.stack.enter_context(self.nc.sbuf_tensor(f"{name}_{self.nc.next_id()}", shape, dt))


@contextmanager
def stage(nc):
    with ExitStack() as stack:
        st = Stage(nc, stack)
        yield st
        if st.sems:
            nc.clear_and_free_semaphores(st.sems)
            nc.all_engine_barrier(sem_only=True)


class Edges:

    def __init__(self, st, name):
        self.idx = st.sb(name + "_idx", [P, CHUNKS], I32)
        self.same = st.sb(name + "_same", [P, CHUNKS])
        self.pay = st.sb(name + "_pay", [P, CHUNKS * 3])
        self.bin = st.sb(name + "_bin", [1, CHUNKS], I32)


class Routing:

    def __init__(self, st, picks, experts, weighted):
        self.chunks = token_chunks(picks, experts)
        self.bin = st.sb("bin", [1, self.chunks], I32)
        self.idx = st.sb("idx", [P, self.chunks], I32)
        self.slots = [st.sb(f"slots{p}", [P, NT], I32) for p in range(picks)]
        self.weights = [st.sb(f"weight{p}", [P, NT]) for p in range(picks)] if weighted else None


class Core:

    def __init__(self, nc, st):
        self.iota = st.sb("iota", [P, CHUNKS])
        self.ident = st.sb("ident", [P, P])
        self.ident_bf = st.sb("ident_bf", [P, P], BF)
        self.ones = st.sb("ones", [P, P])
        self.before = st.sb("before", [P, P])
        self.ps = [st.stack.enter_context(nc.psum_tensor(f"bank{i}", [P, 512], FP)) for i in range(8)]
        self.table = nc.dram_tensor("table", (NPAD, D), FP, kind="Internal").ap()
        self.table2 = nc.dram_tensor("table2", (NPAD, D), FP, kind="Internal").ap()
        self.slot_rows = nc.dram_tensor("slot_rows", (token_chunks(2, 16) * P, D), FP, kind="Internal").ap()
        self.src_table = nc.dram_tensor("src_table", (CHUNKS * P, 3), FP, kind="Internal").ap()
        self.dst_table = nc.dram_tensor("dst_table", (CHUNKS * P, 3), FP, kind="Internal").ap()
        self.by_src = Edges(st, "by_src")
        self.by_dst = Edges(st, "by_dst")


def tile_of(buf, t, width=D):
    return buf[:, bass.ds(t * width, width)]


def tile_rows(table, t):
    return table[bass.ds(t * P, P), :]


def make_constants(nc, K):
    with stage(nc) as st:
        ii = st.sb("ii", [P, CHUNKS], I32)
        made, ready, chain = st.sem("made"), st.sem("ready"), st.sem("chain")
        with nc.Block() as block:

            @block.gpsimd
            def _(pool):
                nc.gpsimd.iota(ii[:, :], pattern=[[1, CHUNKS]], base=0, channel_multiplier=0).then_inc(made, 1)
                nc.gpsimd.memset(K.ident[:, :], 0.0).then_inc(chain, 1)
                nc.gpsimd.memset(K.ones[:, :], 1.0).then_inc(chain, 1)
                pool.wait_ge(chain, 2)
                nc.gpsimd.affine_select(out=K.ident[:, :], in_=K.ident[:, :], compare_op=ALU.not_equal, fill=1.0,
                                        base=0, pattern=[[-1, P]], channel_multiplier=1).then_inc(made, 1)
                nc.gpsimd.affine_select(out=K.before[:, :], in_=K.ones[:, :], compare_op=ALU.is_ge, fill=0.0,
                                        base=-1, pattern=[[1, P]], channel_multiplier=-1).then_inc(made, 1)

            @block.vector
            def _(dve):
                dve.wait_ge(made, 3)
                nc.vector.tensor_copy(K.iota[:, :], ii[:, :])
                nc.vector.tensor_copy(K.ident_bf[:, :], K.ident[:, :]).then_inc(ready, 1)


def load_nodes(nc, K, x):
    with stage(nc) as st:
        zeroed, loaded = st.sem("zeroed"), st.sem("loaded")
        with nc.Block() as block:

            @block.vector
            def _(dve):
                nc.vector.memset(tile_of(K.x, NT - 1), 0.0).then_inc(zeroed, 1)

            @block.sync
            def _(sp):
                sp.dma_start(K.x[:, 0:(NT - 1) * D].rearrange("p (t d) -> p t d", d=D),
                             x[0:(NT - 1) * P, :].rearrange("(t p) d -> p t d", p=P)).then_inc(loaded, 16)
                sp.wait_ge(zeroed, 1)
                sp.dma_start(K.x[0:LAST, (NT - 1) * D:NT * D], x[(NT - 1) * P:NODES, :]).then_inc(loaded, 16)
                sp.wait_ge(loaded, 32)


def store_nodes(nc, K, out):
    with stage(nc) as st:
        stored = st.sem("stored")
        with nc.Block() as block:

            @block.sync
            def _(sp):
                sp.dma_start(out[0:(NT - 1) * P, :].rearrange("(t p) d -> p t d", p=P),
                             K.x[:, 0:(NT - 1) * D].rearrange("p (t d) -> p t d", d=D)).then_inc(stored, 16)
                sp.dma_start(out[(NT - 1) * P:NODES, :], K.x[0:LAST, (NT - 1) * D:NT * D]).then_inc(stored, 16)
                sp.wait_ge(stored, 32)


def start_buffers(st, S, parts, bins, slots):
    G, rc, base = (st.sb(x, [parts, bins]) for x in ("G", "rc", "base"))
    ci, ni = (st.sb(x, [P, bins], I32) for x in ("ci", "ni"))
    nf, ce, start = (st.sb(x, [P, bins]) for x in ("nf", "ce", "start"))
    return ((S, G, rc, ci, ni, nf, ce, start, base), base, ce, st.sb("ends", [bins, bins + 1]),
            st.sb("past", [bins, slots]))


def count_products(nc, K, bufs, parts, bins):
    rc = bufs[2]
    nc.tensor.matmul(K.ps[0][:, 0:bins], K.ones[0:parts, :], rc[:, :], start=True, stop=True)
    return nc.tensor.matmul(K.ps[1][0:parts, 0:bins], K.before[0:parts, 0:parts], rc[:, :], start=True, stop=True)


def bin_starts(nc, K, dve, link, total, cols, bufs, rows, counted):
    S, G, rc, ci, ni, nf, ce, start, base = bufs
    V = nc.vector
    parts, bins = G.shape
    link(V.tensor_tensor_scan(S[:, :], total, total, 0.0, ALU.add, ALU.max))
    link(V.tensor_copy(G[:, :], S[:, :].rearrange("p (b c) -> p b c", c=cols)[:, :, cols - 1]))
    link(V.tensor_copy(rc[:, :], G[:, :]))
    V.tensor_tensor(rc[:, 1:bins], G[:, 1:bins], G[:, 0:bins - 1], ALU.subtract).then_inc(rows, 1)
    dve.wait_ge(counted, 1)
    link(V.tensor_scalar(ci[:, :], K.ps[0][:, 0:bins], float(P - 1), None, ALU.add))
    link(V.tensor_scalar(ni[:, :], ci[:, :], 7, None, ALU.logical_shift_right))
    link(V.tensor_copy(nf[:, :], ni[:, :]))
    link(V.tensor_tensor_scan(ce[:, :], nf[:, :], nf[:, :], 0.0, ALU.add, ALU.max))
    link(V.tensor_tensor(start[:, :], ce[:, :], nf[:, :], ALU.subtract))
    link(V.scalar_tensor_tensor(base[:, :], start[0:parts, :], float(P), K.ps[1][0:parts, 0:bins],
                                ALU.mult, ALU.add))
    link(V.tensor_tensor(base[:, 1:bins], base[:, 1:bins], G[:, 0:bins - 1], ALU.subtract))


def chunk_bins(nc, K, dve, link, ce, ends, past, compared, chunk_bin):
    bins, slots = ce.shape[1], past.shape[1]
    link(nc.vector.tensor_tensor(ends[:, 0:bins], ce[0:bins, :], K.ident[0:bins, 0:bins], ALU.mult))
    link(nc.vector.tensor_reduce(ends[:, bins:bins + 1], ends[:, 0:bins], AX.X, ALU.add))
    nc.vector.tensor_scalar(past[:, :], K.iota[0:bins, 0:slots], ends[:, bins:bins + 1], None, ALU.is_ge)\
        .then_inc(compared[0], 1)
    dve.wait_ge(compared[1], 1)
    link(nc.vector.tensor_copy(chunk_bin, K.ps[2][0:1, 0:slots]))


def count_bins(nc, K, pe, past, compared):
    bins, slots = past.shape
    pe.wait_ge(compared[0], 1)
    nc.tensor.matmul(K.ps[2][:, 0:slots], K.ones[0:bins - 1, :], past[0:bins - 1, :], start=True, stop=True)\
        .then_inc(compared[1], 1)


def place(nc, K, total, picks, parts, bins, cols, slots, chunk_bin):
    with stage(nc) as st:
        S = st.sb("S", [parts, bins * cols])
        T = st.sb("T", [parts, bins * cols]) if len(picks) > 1 else S
        st_bufs, base, ce, ends, past = start_buffers(st, S, parts, bins, slots)
        pos = st.sb("pos", [parts, cols])
        posi = st.sb("posi", [parts, cols], I32)
        lane = st.sb("lane", [parts, cols], I32)
        chunk = st.sb("chunk", [parts, cols], I32)
        S3 = S[:, :].rearrange("p (b c) -> p b c", c=cols)
        T3 = T[:, :].rearrange("p (b c) -> p b c", c=cols)
        chain, rows, counted = st.sem("chain"), st.sem("rows_counted"), st.sem("all_counted")
        compared = [st.sem("compared"), st.sem("binned")]
        with nc.Block() as block:

            @block.tensor
            def _(pe):
                pe.wait_ge(rows, 1)
                count_products(nc, K, st_bufs, parts, bins).then_inc(counted, 1)
                count_bins(nc, K, pe, past, compared)

            @block.vector
            def _(dve):
                link = linker(dve, chain)
                V = nc.vector
                bin_starts(nc, K, dve, link, total, cols, st_bufs, rows, counted)
                link(V.tensor_scalar(base[:, :], base[:, :], -1.0, None, ALU.add))
                for mask, row, slot in picks:
                    m3 = mask.rearrange("p (b c) -> p b c", c=cols)
                    for b in range(bins):
                        last = V.scalar_tensor_tensor(T3[:, b, :], S3[:, b, :], base[:, b:b + 1], m3[:, b, :],
                                                      ALU.add, ALU.mult)
                    link(last)
                    link(V.tensor_reduce(pos[:, :], T3.rearrange("p b c -> p c b"), AX.X, ALU.add))
                    link(V.tensor_copy(posi[:, :], pos[:, :]))
                    if slot is not None:
                        link(V.tensor_copy(slot, posi[:, :]))
                    V.tensor_scalar(lane[:, :], posi[:, :], P - 1, None, ALU.bitwise_and)
                    link(V.tensor_scalar(chunk[:, :], posi[:, :], 7, None, ALU.logical_shift_right))
                    if slot is None:
                        link(V.scalar_tensor_tensor(row, lane[:, :], float(slots), chunk[:, :], ALU.mult, ALU.add))
                    else:
                        V.tensor_copy(row[0], lane[:, :])
                        link(V.tensor_copy(row[1], chunk[:, :]))
                chunk_bins(nc, K, dve, link, ce, ends, past, compared, chunk_bin)


def read_table(nc, table, out):
    with stage(nc) as st:
        back = st.sem("back")
        with nc.Block() as block:

            @block.sync
            def _(sp):
                sp.dma_start(out, table.rearrange("(p s) w -> p (s w)", p=P)).then_inc(back, 16)
                sp.wait_ge(back, 16)


class Scatter:

    def __init__(self, nc, st, table, row, pay, first, cols, unroll):
        assert cols % unroll == 0
        parts, words = row.shape[0], table.shape[1]
        self.nc, self.table, self.row, self.pay, self.words = nc, table, row, pay, words
        self.first, self.n, self.unroll = first, cols // unroll, unroll
        self.rowr = st.sb("rowr", [parts, 4 * unroll], I32)
        self.payr = st.sb("payr", [parts, 4 * unroll * words])
        self.staged, self.passed = st.sem("staged"), st.sem("passed")
        self.landed = [st.sem(f"landed{h}") for h in range(4)]

    def step(self, pool, i, j, k):
        U, W = self.unroll, self.words
        if runs(i, self.n):
            wait_count(pool, self.landed[j], U * 16 * k)
            self.nc.gpsimd.tensor_copy(self.rowr[:, j * U:(j + 1) * U], self.row[:, bass.ds(i * U + self.first, U)])
            self.nc.gpsimd.tensor_copy(self.payr[:, j * U * W:(j + 1) * U * W],
                                       self.pay[:, bass.ds(i * (U * W) + self.first * W, U * W)]).then_inc(self.staged, 1)
        if runs(i - 1, self.n):
            h = (j - 1) % 4
            wait_staged(pool, self.staged, i, self.passed)
            for n in range(h * U, (h + 1) * U):
                self.nc.gpsimd.indirect_dma_start(self.table, bass.IndirectOffsetOnAxis(ap=self.rowr[:, n:n + 1], axis=0),
                                                  self.payr[:, n * W:(n + 1) * W], None).then_inc(self.landed[h], 16)

    def end(self, pool):
        for h in range(4):
            pool.wait_ge(self.landed[h], 16 * self.unroll * ((self.n + 3 - h) // 4))

    def whole(self, pool):
        steps(pool, self.n, 4, 1, lambda i, j, k: self.step(pool, i, j % 4, k))
        self.end(pool)


def items_of_slots(nc, K, lane, chunk, item, out):
    n, chunks = lane.shape[1], out.shape[1]
    cols = item.shape[1]
    group = 5
    with stage(nc) as st:
        lanes = st.sb("lanes", [P, n, P])
        at = st.sb("at", [P, n, chunks])
        made, summed, done = st.sem("made"), st.sem("summed"), st.sem("done")
        with nc.Block() as block:

            @block.vector
            def _(dve):
                for a in range(0, n, group):
                    nc.vector.tensor_tensor(lanes[:, a:a + group, :],
                                            K.iota[:, 0:P].unsqueeze(1).broadcast_to([P, group, P]),
                                            lane[:, a:a + group].unsqueeze(2).broadcast_to([P, group, P]), ALU.is_equal)
                    for c in range(a, a + group):
                        last = nc.vector.tensor_scalar(at[:, c, :], K.iota[:, 0:chunks], chunk[:, c:c + 1],
                                                       item[:, c % cols:c % cols + 1], ALU.is_equal, ALU.mult)
                    last.then_inc(made, 1)
                dve.wait_ge(summed, 1)
                nc.vector.tensor_copy(out, K.ps[0][:, 0:chunks]).then_inc(done, 1)

            @block.tensor
            def _(pe):
                for c in range(n):
                    if c % group == 0:
                        pe.wait_ge(made, c // group + 1)
                    last = nc.tensor.matmul(K.ps[0][:, 0:chunks], lanes[:, c, :], at[:, c, :], start=(c == 0),
                                            stop=(c == n - 1))
                last.then_inc(summed, 1)


def place_by_node(nc, K, node_row, tile, row, chunk_bin, beside):
    W = 20
    U = 4
    with stage(nc) as st:
        tiles = st.sb("tiles", [EP, EC * NT], BF)
        counts = st.sb("counts", [P, NT * EC], BF)
        S = st.sb("S", [P, NT * EC])
        first = st.sb("first", [P, EC * NT])
        tiles3 = tiles[:, :].rearrange("p (c t) -> p c t", t=NT)
        counts3 = counts[:, :].rearrange("p (t c) -> p t c", c=EC)
        S3 = S[:, :].rearrange("p (t c) -> p t c", c=EC)
        first3 = first[:, :].rearrange("p (c t) -> p c t", t=NT)
        with stage(nc) as st1:
            hot = st1.sb("hot", [EP, 2, W, P], BF)
            tiled, made, counted, kept = (st1.sem(x) for x in ("tiled", "made", "counted", "kept"))
            scatter1 = beside(0, st1)
            with nc.Block() as block:

                @block.gpsimd
                def _(pool):
                    scatter1.whole(pool)

                @block.vector
                def _(dve):
                    for t in range(NT):
                        last = nc.vector.tensor_scalar(tiles3[:, :, t], tile, float(t), None, ALU.is_equal)
                    last.then_inc(tiled, 1)

                    def step(i, j, k):
                        wait_count(dve, counted, i - 1)
                        nc.vector.tensor_tensor(hot[:, j, :, :],
                                                K.iota[0:EP, 0:P].unsqueeze(1).broadcast_to([EP, W, P]),
                                                node_row[:, bass.ds(i * W, W)].unsqueeze(2).broadcast_to([EP, W, P]),
                                                ALU.is_equal).then_inc(made, 1)

                    steps(dve, EC // W, 2, 0, step)

                @block.tensor
                def _(pe):
                    pe.wait_ge(tiled, 1)

                    def step(i, j, k):
                        pe.wait_ge(made, i + 1)
                        wait_count(pe, kept, i - 1)
                        for c in range(W):
                            last = nc.tensor.matmul(K.ps[j][:, c * NT:(c + 1) * NT], hot[:, j, c, :],
                                                    tiles[:, bass.ds(i * (W * NT) + c * NT, NT)], start=True, stop=True)
                        last.then_inc(counted, 1)

                    steps(pe, EC // W, 2, 0, step)

                @block.scalar
                def _(act):
                    def step(i, j, k):
                        act.wait_ge(counted, i + 1)
                        nc.scalar.activation(counts3[:, :, bass.ds(i * W, W)],
                                             K.ps[j][:, 0:W * NT].rearrange("p (c t) -> p t c", t=NT),
                                             ACT.Copy).then_inc(kept, 1)

                    steps(act, EC // W, 2, 0, step)

        with stage(nc) as st2:
            bufs, base, ce, ends, past = start_buffers(st2, S, P, NT, CHUNKS)
            chain, rows, counted = (st2.sem(x) for x in ("chain", "rows", "counted"))
            compared = [st2.sem("compared"), st2.sem("binned")]
            scatter2 = beside(1, st2)
            with nc.Block() as block:

                @block.gpsimd
                def _(pool):
                    scatter2.whole(pool)

                @block.tensor
                def _(pe):
                    pe.wait_ge(rows, 1)
                    count_products(nc, K, bufs, P, NT).then_inc(counted, 1)
                    count_bins(nc, K, pe, past, compared)

                @block.vector
                def _(dve):
                    link = linker(dve, chain)
                    bin_starts(nc, K, dve, link, counts[:, :], EC, bufs, rows, counted)
                    for t in range(NT):
                        last = nc.vector.scalar_tensor_tensor(first3[:, :, t], S3[:, t, :], base[:, t:t + 1],
                                                              counts3[:, t, :], ALU.add, ALU.subtract)
                    link(last)
                    chunk_bins(nc, K, dve, link, ce, ends, past, compared, chunk_bin)

        with stage(nc) as st3:
            hot = st3.sb("hot", [EP, 2, U, P], BF)
            hotT = st3.sb("hotT", [P, 4, U * EP])
            twin = st3.sb("twin", [EP, 2, U, EP], BF)
            pos = st3.sb("pos", [EP, EC])
            posi, lane, chunk = (st3.sb(x, [EP, EC], I32) for x in ("posi", "lane", "chunk"))
            found = S[0:EP, :]
            scatter3 = beside(2, st3)
            made, turned, copied, paired, masked, looked, kept, chain = (
                st3.sem(x) for x in ("made", "turned", "copied", "paired", "masked", "looked", "kept", "chain"))
            with nc.Block() as block:

                @block.gpsimd
                def _(pool):
                    scatter3.whole(pool)

                @block.vector
                def _(dve):
                    def step(i, j, k):
                        if runs(i, EC // U):
                            wait_count(dve, turned, i - 1)
                            nc.vector.tensor_tensor(hot[:, j % 2, :, :],
                                                    K.iota[0:EP, 0:P].unsqueeze(1).broadcast_to([EP, U, P]),
                                                    node_row[:, bass.ds(i * U, U)].unsqueeze(2).broadcast_to([EP, U, P]),
                                                    ALU.is_equal).then_inc(made, 1)
                        if runs(i - 2, EC // U):
                            dve.wait_ge(paired, i - 1)
                            wait_count(dve, looked, i - 3)
                            nc.vector.tensor_tensor(twin[:, j % 2, :, :],
                                                    K.ps[2 + j % 2][0:EP, 0:U * EP].rearrange("p (u e) -> p u e", u=U),
                                                    K.before[0:EP, 0:EP].unsqueeze(1).broadcast_to([EP, U, EP]),
                                                    ALU.mult).then_inc(masked, 1)

                    steps(dve, EC // U, 8, 2, step)
                    dve.wait_ge(kept, EC // U)
                    link = linker(dve, chain)
                    V = nc.vector
                    link(V.tensor_tensor(found, found, tiles[:, :], ALU.mult))
                    link(V.tensor_reduce(pos[:, :], found.rearrange("p (c t) -> p c t", t=NT), AX.X, ALU.add))
                    link(V.tensor_copy(posi[:, :], pos[:, :]))
                    V.tensor_scalar(lane[:, :], posi[:, :], P - 1, None, ALU.bitwise_and)
                    link(V.tensor_scalar(chunk[:, :], posi[:, :], 7, None, ALU.logical_shift_right))
                    link(V.scalar_tensor_tensor(row, lane[:, :], float(CHUNKS), chunk[:, :], ALU.mult, ALU.add))

                @block.tensor
                def _(pe):
                    def step(i, j, k):
                        if runs(i, EC // U):
                            pe.wait_ge(made, i + 1)
                            wait_count(pe, copied, i - 1)
                            for u in range(U):
                                last = nc.tensor.matmul(K.ps[j % 2][:, u * EP:(u + 1) * EP], hot[:, j % 2, u, :],
                                                        K.ident_bf[0:EP, 0:EP], start=True, stop=True)
                            last.then_inc(turned, 1)
                        if runs(i - 1, EC // U):
                            pe.wait_ge(copied, i)
                            wait_count(pe, masked, i - 2)
                            for u in range(U):
                                both = hotT[:, (j - 1) % 4, u * EP:(u + 1) * EP]
                                last = nc.tensor.matmul(K.ps[2 + (j - 1) % 2][0:EP, u * EP:(u + 1) * EP], both, both,
                                                        start=True, stop=True)
                            last.then_inc(paired, 1)
                        if runs(i - 3, EC // U):
                            c, jj = i - 3, (j - 3) % 4
                            pe.wait_ge(masked, c + 1)
                            wait_count(pe, kept, c - 1)
                            for u in range(U):
                                bank = K.ps[4 + jj % 2][0:EP, u * NT:(u + 1) * NT]
                                nc.tensor.matmul(bank, hotT[:, jj, u * EP:(u + 1) * EP],
                                                 first[:, bass.ds(c * (U * NT) + u * NT, NT)], start=True, stop=False)
                                last = nc.tensor.matmul(bank, twin[:, jj % 2, u, :],
                                                        tiles[:, bass.ds(c * (U * NT) + u * NT, NT)],
                                                        start=False, stop=True)
                            last.then_inc(looked, 1)

                    steps(pe, EC // U, 8, 3, step)

                @block.scalar
                def _(act):
                    def step(i, j, k):
                        if runs(i, EC // U):
                            act.wait_ge(turned, i + 1)
                            wait_count(act, looked, i - 3)
                            nc.scalar.activation(hotT[:, j % 4, :], K.ps[j % 2][:, 0:U * EP], ACT.Copy).then_inc(copied, 1)
                        if runs(i - 3, EC // U):
                            c, jj = i - 3, (j - 3) % 4
                            act.wait_ge(looked, c + 1)
                            nc.scalar.activation(found[:, bass.ds(c * (U * NT), U * NT)], K.ps[4 + jj % 2][0:EP, 0:U * NT],
                                                 ACT.Copy).then_inc(kept, 1)

                    steps(act, EC // U, 8, 3, step)


class Keys:

    def __init__(self, st, name):
        self.tile, self.node_row = st.sb(name + "_tile", [EP, EC]), st.sb(name + "_node_row", [EP, EC])
        self.pay = st.sb(name + "_pay", [EP, EC * 3])
        self.row = st.sb(name + "_row", [EP, EC], I32)


def load_keys(nc, K, src, dst, weight, by_src, by_dst):
    with stage(nc) as st:
        blank = st.sb("blank", [P, 2, CHUNKS * 3])
        raw = [st.sb(x, [EP, EC], I32) for x in ("src", "dst")]
        ti, li = ([st.sb(f"{x}{n}", [EP, EC], I32) for n in range(2)] for x in ("ti", "li"))
        wf = st.sb("wf", [EP, EC])
        loaded, blanked, filled, chain = st.sem("loaded"), st.sem("blanked"), st.sem("filled"), st.sem("chain")
        blanks = ((K.src_table, (0.0, -1.0, 0.0)), (K.dst_table, (0.0, -1.0, -1.0)))
        with nc.Block() as block:

            @block.sync
            def _(sp):
                for a, b in ((raw[0], src), (raw[1], dst), (wf, weight)):
                    sp.dma_start(a[:, :], b.rearrange("(p c) -> p c", c=EC)).then_inc(loaded, 16)
                sp.wait_ge(blanked, 1)
                for n, (table, _) in enumerate(blanks):
                    sp.dma_start(table.rearrange("(p s) w -> p (s w)", p=P), blank[:, n, :]).then_inc(filled, 16)
                sp.wait_ge(filled, 32)

            @block.vector
            def _(dve):
                link = linker(dve, chain)
                V = nc.vector
                for n, (_, fill) in enumerate(blanks):
                    for w in range(3):
                        last = V.memset(blank[:, n, :].rearrange("p (s w) -> p s w", w=3)[:, :, w], fill[w])
                last.then_inc(blanked, 1)
                dve.wait_ge(loaded, 48)
                for n in range(2):
                    V.tensor_scalar(ti[n][:, :], raw[n][:, :], 7, None, ALU.logical_shift_right)
                    last = V.tensor_scalar(li[n][:, :], raw[n][:, :], P - 1, None, ALU.bitwise_and)
                link(last)
                for n, (keys, third) in enumerate(((by_src, wf), (by_dst, raw[1]))):
                    pay3 = keys.pay[:, :].rearrange("p (c w) -> p c w", w=3)
                    V.tensor_copy(pay3[:, :, 0], raw[1 - n][:, :])
                    V.tensor_copy(pay3[:, :, 1], li[n][:, :])
                    V.tensor_copy(pay3[:, :, 2], third[:, :])
                    V.tensor_copy(keys.node_row[:, :], li[n][:, :])
                    last = V.tensor_copy(keys.tile[:, :], ti[n][:, :])
                link(last)


def spread_tiles(nc, K, to):
    with stage(nc) as st:
        binf = st.sb("binf", [1, CHUNKS])
        bins = st.sb("bins", [P, CHUNKS])
        chain, numbered, spread = st.sem("chain"), st.sem("numbered"), st.sem("spread")
        with nc.Block() as block:

            @block.tensor
            def _(pe):
                pe.wait_ge(numbered, 1)
                nc.tensor.matmul(K.ps[0][:, 0:CHUNKS], K.ones[0:1, :], binf[:, :], start=True, stop=True).then_inc(spread, 1)

            @block.vector
            def _(dve):
                link = linker(dve, chain)
                nc.vector.tensor_copy(to.idx[:, :], to.pay[:, :].rearrange("p (c w) -> p c w", w=3)[:, :, 0])
                nc.vector.tensor_copy(binf[:, :], to.bin[:, :]).then_inc(numbered, 1)
                dve.wait_ge(spread, 1)
                link(nc.vector.tensor_copy(bins[:, :], K.ps[0][:, 0:CHUNKS]))
                nc.vector.memset(to.same[:, 0:1], 0.0)
                nc.vector.tensor_tensor(to.same[:, 1:CHUNKS], bins[:, 1:CHUNKS], bins[:, 0:CHUNKS - 1], ALU.is_equal)


PER_CHUNK = 2
SHARES = (64, 40, EC - 104)


def place_edges(nc, K, src, dst, weight, by_dst):
    with stage(nc) as st:
        by_src = Keys(st, "src")
        load_keys(nc, K, src, dst, weight, by_src, by_dst)
        with stage(nc) as st2:
            mask = st2.sb("mask", [EP, NT * EC])

            def masks():
                for b in range(NT):
                    last = nc.vector.tensor_scalar(mask[:, b * EC:(b + 1) * EC], by_src.tile[:, :], float(b), None,
                                                   ALU.is_equal)
                return last

            vector_work(nc, masks)
            place(nc, K, mask[:, :], [(mask[:, :], by_src.row[:, :], None)], EP, NT, EC, CHUNKS, K.by_src.bin[:, :])
        place_by_node(nc, K, by_dst.node_row[:, :], by_dst.tile[:, :], by_dst.row[:, :], K.by_dst.bin[:, :],
                      lambda part, st2: Scatter(nc, st2, K.src_table, by_src.row, by_src.pay, sum(SHARES[:part]),
                                                SHARES[part], 8))
    read_table(nc, K.src_table, K.by_src.pay[:, :])
    spread_tiles(nc, K, K.by_src)


def gather_rows(nc, pool, edges, table, rows, idxr, gathered, staged, passed, used, per):
    GR = rows.shape[1]
    half = GR // 2
    n = CHUNKS // half

    def step(i, j, k):
        if runs(i, n):
            nc.gpsimd.tensor_copy(idxr[:, j * half:(j + 1) * half], edges.idx[:, bass.ds(i * half, half)]).then_inc(staged, 1)
        if runs(i - 1, n):
            c, at = i - 1, (j - 1) % 4 * half
            wait_staged(pool, staged, c + 1, passed)
            for g in range(half):
                if g % 4 == 0 and not (isinstance(c, int) and c < 2):
                    wait_staged(pool, used, half // per * (c - 2) + (g + 4) // per, passed)
                row = (j - 1) % 2 * half + g
                nc.gpsimd.indirect_dma_start(rows[:, row, :], None, table,
                                             bass.IndirectOffsetOnAxis(ap=idxr[:, at + g:at + g + 1], axis=0))\
                    .then_inc(gathered[row // per], 16)

    steps(pool, n, 4, 1, step)


def carry(nc, dve, edges, run, bank, c, ran):
    wait_count(dve, ran, c)
    return nc.vector.scalar_tensor_tensor(run[1], run[0], edges.same[:, bass.ds(c, 1)], bank, ALU.mult,
                                          ALU.add).then_inc(ran, 1)


def keep(nc, act, edges, out, run, c, width, ran, kept):
    t = act.value_load(edges.bin[0:1, bass.ds(c, 1)], min_val=0, max_val=NT - 1)
    act.wait_ge(ran, c + 1)
    wait_count(act, kept, c)
    nc.scalar.activation(tile_of(out, t, width), run, ACT.Copy).then_inc(kept, 1)


def spmm(nc, K, edges, table, out):
    GR, R, LAG = 16, 8, 4
    with stage(nc) as st:
        idxr = st.sb("idxr", [P, 2 * GR], I32)
        rows = st.sb("rows", [P, GR, D])
        pick = st.sb("pick", [P, R, P])
        run = st.sb("run", [P, RUNS, D])
        gathered = [st.sem(f"gathered{j}") for j in range(GR)]
        staged, passed, picked, summed, ran, kept, cleared = (
            st.sem(n) for n in ("staged", "passed", "picked", "summed", "ran", "kept", "cleared"))
        with nc.Block() as block:

            @block.gpsimd
            def _(pool):
                gather_rows(nc, pool, edges, table, rows, idxr, gathered, staged, passed, summed, 1)

            @block.vector
            def _(dve):
                nc.vector.memset(out[:, :], 0.0)
                nc.vector.memset(run[:, RUNS - 1, :], 0.0).then_inc(cleared, 1)
                dve.wait_ge(cleared, 1)

                def step(i, j, k):
                    if runs(i - LAG, CHUNKS):
                        c, jj = i - LAG, (j - LAG) % R
                        dve.wait_ge(summed, c + 1)
                        wait_count(dve, kept, c - RUNS + 1)
                        carry(nc, dve, edges, (run[:, (jj - 1) % RUNS, :], run[:, jj % RUNS, :]), K.ps[jj][:, 0:D], c, ran)
                    if runs(i, CHUNKS):
                        wait_count(dve, summed, i - R + 1)
                        nc.vector.tensor_scalar(pick[:, j, :], K.iota[:, 0:P], edges.pay[:, bass.ds(3 * i + 1, 1)],
                                                edges.pay[:, bass.ds(3 * i + 2, 1)], ALU.is_equal,
                                                ALU.mult).then_inc(picked, 1)

                steps(dve, CHUNKS, R, LAG, step)

            @block.tensor
            def _(pe):
                def step(i, j, k):
                    pe.wait_ge(gathered[j], 16 * k + 16)
                    pe.wait_ge(picked, i + 1)
                    wait_count(pe, ran, i - R + 1)
                    nc.tensor.matmul(K.ps[j % R][:, 0:D], pick[:, j % R, :], rows[:, j, :],
                                     start=True, stop=True).then_inc(summed, 1)

                steps(pe, CHUNKS, GR, 0, step)

            @block.scalar
            def _(act):
                act.wait_ge(cleared, 1)

                def step(i, j, k):
                    keep(nc, act, edges, out, run[:, j, :], i, D, ran, kept)

                steps(act, CHUNKS, RUNS, 0, step)


def vector_work(nc, *ops):
    with stage(nc) as st:
        chain = st.sem("chain")
        with nc.Block() as block:

            @block.vector
            def _(dve):
                link = linker(dve, chain)
                for op in ops:
                    link(op())


def layer_norm(nc, K, src, dst, affine=None, table=None, residual=False):
    with stage(nc) as st:
        stats = st.sb("stats", [P, NT * 6])
        mv = st.sb("mv", [P, NT * 2])
        rstd = st.sb("rstd", [P, NT])
        gb = st.sb("gb", [P, 2, D]) if affine else None
        var = mv[:, :].rearrange("p (t s) -> p t s", s=2)[:, :, 1]
        loaded, chain, stat, var_ok, root, normed, stored = (
            st.sem(n) for n in ("loaded", "chain", "stat", "var_ok", "root", "normed", "stored"))
        passed = [st.sem(f"passed{m}") for m in range(2)]
        with nc.Block() as block:

            @block.sync
            def _(sp):
                if affine:
                    for a in range(2):
                        sp.dma_start(gb[:, a, :], affine[a].partition_broadcast(P)).then_inc(loaded, 16)
                if table is not None:
                    def step(t, j, k):
                        sp.wait_ge(normed, t + 1)
                        sp.dma_start(tile_rows(table, t), tile_of(dst, t)).then_inc(stored, 16)

                    steps(sp, NT, 2, 0, step)
                    sp.wait_ge(stored, 16 * NT)

            @block.scalar
            def _(act):
                act.wait_ge(var_ok, 1)
                nc.scalar.activation(rstd[:, :], rstd[:, :], ACT.Sqrt).then_inc(root, 1)

            @block.vector
            def _(dve):
                link = linker(dve, chain)

                def statistics(t, j, k):
                    nc.vector.bn_stats(stats[:, bass.ds(t * 6, 6)], tile_of(src, t)).then_inc(stat, 1)

                steps(dve, NT, 5, 0, statistics)
                dve.wait_ge(stat, NT)
                for t in range(NT):
                    last = nc.vector.bn_aggr(mv[:, 2 * t:2 * t + 2], stats[:, 6 * t:6 * t + 6])
                link(last)
                nc.vector.tensor_scalar(rstd[:, :], var, EPS, None, ALU.add).then_inc(var_ok, 1)
                dve.wait_ge(root, 1)
                link(nc.vector.reciprocal(rstd[:, :], rstd[:, :]))
                if affine:
                    dve.wait_ge(loaded, 32)
                ops = [lambda t: nc.vector.tensor_scalar(
                    tile_of(dst, t), tile_of(src, t), mv[:, bass.ds(2 * t, 1)], rstd[:, bass.ds(t, 1)],
                    ALU.subtract, ALU.mult)]
                if affine:
                    ops = [lambda t: nc.vector.scalar_tensor_tensor(
                               tile_of(dst, t), tile_of(src, t), mv[:, bass.ds(2 * t, 1)], gb[:, 0, :],
                               ALU.subtract, ALU.mult),
                           lambda t: nc.vector.scalar_tensor_tensor(
                               tile_of(dst, t), tile_of(dst, t), rstd[:, bass.ds(t, 1)], gb[:, 1, :],
                               ALU.mult, ALU.add)]
                if residual:
                    ops.append(lambda t: nc.vector.tensor_tensor(tile_of(K.x, t), tile_of(K.x, t), tile_of(dst, t), ALU.add))
                last_op = len(ops) - 1

                def normalise(i, j, k):
                    for m, op in enumerate(ops):
                        if runs(i - m, NT):
                            if m:
                                dve.wait_ge(passed[m - 1], i - m + 1)
                            op(i - m).then_inc(normed if m == last_op else passed[m], 1)

                steps(dve, NT, 5, last_op, normalise)


def dense(nc, K, sources, weights, bias, outs, beside=None, norm=None):
    width = sum(o[0] for o in outs)
    nsrc = len(sources)
    tables = [o for o in outs if o[1] in ("table", "both")]
    with stage(nc) as st:
        w = st.sb("w", [P, nsrc * KD, width])
        b = st.sb("b", [P, width]) if bias is not None else None
        raw = st.sb("raw", [P, 2, nsrc * D])
        xT = st.sb("xT", [P, 2, nsrc * D])
        ring = st.sb("ring", [P, 2, len(tables) or 1, D])
        loaded, biased = st.sem("loaded"), st.sem("biased")
        loads = 16 * (KD * sum(len(x) for x in weights) + (b is not None))
        adds = sum(o[1] == "add" for o in outs)
        staged, turned, copied, summed, written = (st.sem(n) for n in ("staged", "turned", "copied", "summed", "written"))
        stored = [st.sem(f"stored{j}") for j in range(2)]
        scatter = beside(st) if beside else None
        if norm:
            goal, normed_table = norm
            stats = st.sb("stats", [P, NT * 6])
            mv = st.sb("mv", [P, NT * 2])
            rstd = st.sb("rstd", [P, NT])
            offset = st.sb("offset", [P, NT])
            mv3 = mv[:, :].rearrange("p (t s) -> p t s", s=2)
        stat, chain, var_ok, root, scaled, normed, kept = (
            st.sem(x) for x in ("stat", "chain", "var_ok", "root", "scaled", "normed", "kept"))
        with nc.Block() as block:

            @block.gpsimd
            def _(pool):
                if scatter:
                    scatter.whole(pool)

            @block.sync
            def _(sp):
                for s in range(nsrc):
                    at = 0
                    for part in weights[s]:
                        n = part.shape[1]
                        for c in range(KD):
                            sp.dma_start(w[:, s * KD + c, at:at + n], part[c * P:(c + 1) * P, :]).then_inc(loaded, 16)
                        at += n
                if b is not None:
                    sp.dma_start(b[:, :], bias.partition_broadcast(P)).then_inc(loaded, 16)

                def step(t, j4, k):
                    j = j4 % 2
                    sp.wait_ge(written, t + 1)
                    for n, (wd, kind, target, _f) in enumerate(tables):
                        tab, src = (target, ring[:, j, n, 0:wd]) if kind == "table" else (target[1], tile_of(target[0], t, wd))
                        sp.dma_start(tile_rows(tab, t), src).then_inc(stored[j], 16)

                if norm and normed_table is not None:
                    def keep_rows(t, j, k):
                        sp.wait_ge(normed, t + 1)
                        sp.dma_start(tile_rows(normed_table, t), tile_of(goal, t)).then_inc(kept, 16)

                    steps(sp, NT, 4, 0, keep_rows)
                    sp.wait_ge(kept, 16 * NT)
                if tables:
                    steps(sp, NT, 4, 0, step)
                    for j in range(2):
                        sp.wait_ge(stored[j], 16 * len(tables) * ((NT + 1 - j) // 2))

            @block.scalar
            def _(act):
                if norm:
                    act.wait_ge(var_ok, 1)
                    nc.scalar.activation(rstd[:, :], rstd[:, :], ACT.Sqrt).then_inc(root, 1)
                    act.wait_ge(scaled, 1)

                def step(i, j4, k):
                    j = j4 % 2
                    if runs(i, NT):
                        wait_count(act, turned, i - 1)
                        for s, src in enumerate(sources):
                            if norm:
                                last = nc.scalar.activation(raw[:, j, :], tile_of(src, i), ACT.Identity,
                                                            bias=offset[:, bass.ds(i, 1)], scale=rstd[:, bass.ds(i, 1)])
                            else:
                                last = nc.scalar.activation(raw[:, j, s * D:(s + 1) * D], tile_of(src, i), ACT.Copy)
                        last.then_inc(staged, 1)
                    if runs(i - 1, NT):
                        act.wait_ge(turned, i)
                        wait_count(act, summed, i - 2)
                        nc.scalar.activation(xT[:, 1 - j, :], K.ps[1 - j][:, 0:nsrc * D], ACT.Copy).then_inc(copied, 1)

                steps(act, NT, 4, 1, step)

            @block.tensor
            def _(pe):
                def step(i, j4, k):
                    j = j4 % 2
                    if runs(i, NT):
                        pe.wait_ge(staged, i + 1)
                        wait_count(pe, copied, i - 1)
                        for s in range(nsrc * KD):
                            last = nc.tensor.transpose(K.ps[j][:, s * P:(s + 1) * P], raw[:, j, s * P:(s + 1) * P],
                                                       K.ident[:, :])
                        last.then_inc(turned, 1)
                    if runs(i - 1, NT):
                        if isinstance(i, int) and i == 1:
                            pe.wait_ge(loaded, loads)
                        pe.wait_ge(copied, i)
                        wait_count(pe, written, i - 2)
                        at = 0
                        for g, o in enumerate(outs):
                            bank = K.ps[2 + 3 * (1 - j) + g][:, 0:o[0]]
                            for s in range(nsrc * KD):
                                last = nc.tensor.matmul(bank, xT[:, 1 - j, s * P:(s + 1) * P], w[:, s, at:at + o[0]],
                                                        start=(s == 0), stop=(s == nsrc * KD - 1))
                            at += o[0]
                        last.then_inc(summed, 1)

                steps(pe, NT, 4, 1, step)

            @block.vector
            def _(dve):
                if norm:
                    link = linker(dve, chain)
                    V = nc.vector

                    def statistics(t, j, k):
                        V.bn_stats(stats[:, bass.ds(t * 6, 6)], tile_of(sources[0], t)).then_inc(stat, 1)

                    steps(dve, NT, 5, 0, statistics)
                    dve.wait_ge(stat, NT)
                    for t in range(NT):
                        last = V.bn_aggr(mv[:, 2 * t:2 * t + 2], stats[:, 6 * t:6 * t + 6])
                    link(last)
                    V.tensor_scalar(rstd[:, :], mv3[:, :, 1], EPS, None, ALU.add).then_inc(var_ok, 1)
                    dve.wait_ge(root, 1)
                    link(V.reciprocal(rstd[:, :], rstd[:, :]))
                    V.scalar_tensor_tensor(offset[:, :], mv3[:, :, 0], -1.0, rstd[:, :], ALU.mult, ALU.mult)\
                        .then_inc(scaled, 1)
                if b is not None:
                    dve.wait_ge(loaded, loads)

                def step(t, j4, k):
                    j = j4 % 2
                    if norm and goal is not None:
                        nc.vector.tensor_scalar(tile_of(goal, t), tile_of(sources[0], t), mv[:, bass.ds(2 * t, 1)],
                                                rstd[:, bass.ds(t, 1)], ALU.subtract, ALU.mult).then_inc(normed, 1)
                    if b is not None and adds:
                        at = 0
                        for wd, kind, target, _f in outs:
                            if kind == "add":
                                nc.vector.tensor_tensor(tile_of(target, t), tile_of(target, t), b[:, at:at + wd],
                                                        ALU.add).then_inc(biased, 1)
                            at += wd
                        dve.wait_ge(biased, adds * t + adds)
                    dve.wait_ge(summed, t + 1)
                    if any(o[1] == "table" for o in outs):
                        wait_count(dve, stored[j], 16 * len(tables) * (2 * k + j4 // 2))
                    n = at = 0
                    for g, (wd, kind, target, factor) in enumerate(outs):
                        bank = K.ps[2 + 3 * j + g][:, 0:wd]
                        if kind == "add":
                            last = nc.vector.tensor_tensor(tile_of(target, t), tile_of(target, t), bank, ALU.add)
                        elif kind == "relu_add":
                            last = nc.vector.scalar_tensor_tensor(tile_of(K.x, t), bank, 0.0, tile_of(K.x, t),
                                                                  ALU.max, ALU.add)
                        else:
                            to = ring[:, j, n, 0:wd] if kind == "table" else tile_of(target if kind == "sb" else target[0], t, wd)
                            if b is not None:
                                last = nc.vector.tensor_tensor(to, bank, b[:, at:at + wd], ALU.add)
                            elif factor is None:
                                last = nc.vector.tensor_copy(to, bank)
                            else:
                                last = nc.vector.tensor_scalar(to, bank, factor, None, ALU.mult)
                        n += kind in ("table", "both")
                        at += wd
                    last.then_inc(written, 1)

                steps(dve, NT, 4, 0, step)


def routed_ffn(nc, K, r, w1, b1, w2, b2, func, relu_out, beside):
    experts, _, hid = w1.shape
    hm = min(P, hid)
    nh = hid // hm
    n = r.chunks
    R = 4
    with stage(nc) as st:
        b1T = st.sb("b1T", [hm, experts * nh])
        w1r = st.sb("w1r", [P, R, KD, hid])
        w2r = st.sb("w2r", [hm, R, nh, D])
        b2s = st.sb("b2s", [experts, D])
        rest = st.sb("rest", [experts, 2, D])
        b2p = st.sb("b2p", [experts, 3, D], BF)
        b2r = st.sb("b2r", [3, experts * D], BF)
        ones3 = st.sb("ones3", [3, P], BF)
        idxr = st.sb("idxr", [P, R], I32)
        rows = st.sb("rows", [P, R, D])
        xT = st.sb("xT", [P, 2, D])
        hT = st.sb("hT", [hm, 2, nh * P])
        yr = st.sb("yr", [P, R, D])
        fetched = [st.sem(f"fetched{j}") for j in range(R)]
        gathered = [st.sem(f"gathered{j}") for j in range(R)]
        stored = [st.sem(f"stored{j}") for j in range(R)]
        b2_loaded, split, chain, spread = (st.sem(x) for x in ("b2_loaded", "split", "chain", "spread"))
        biased, staged, passed, turned, copied, hidden, acted, summed, written = (
            st.sem(x) for x in ("biased", "staged", "passed", "turned", "copied", "hidden", "acted", "summed", "written"))
        scatter = beside(st) if beside else None
        w1v = w1.rearrange("e (k p) h -> p e k h", p=P)
        w2v = w2.rearrange("e (c p) d -> p e c d", p=hm)
        with nc.Block() as block:

            @block.sync
            def _(sp):
                sp.dma_start(b2s[:, :], b2).then_inc(b2_loaded, 16)

                def step(i, j, k):
                    if runs(i, n):
                        e = sp.value_load(r.bin[0:1, bass.ds(i, 1)], min_val=0, max_val=experts - 1)
                        wait_count(sp, summed, i - R + 1)
                        sp.dma_start(w1r[:, j, :, :], w1v[:, bass.ds(e, 1), :, :].rearrange("p e k h -> p (e k) h")).then_inc(fetched[j], 16)
                        sp.dma_start(w2r[:, j, :, :], w2v[:, bass.ds(e, 1), :, :].rearrange("p e c d -> p (e c) d")).then_inc(fetched[j], 16)
                    if runs(i - R, n):
                        sp.wait_ge(written, i - R + 1)
                        sp.dma_start(tile_rows(K.slot_rows, i - R), yr[:, j, :]).then_inc(stored[j], 16)

                steps(sp, n, R, R, step)
                for j in range(R):
                    sp.wait_ge(stored[j], 16 * ((n + R - 1 - j) // R))

            @block.gpsimd
            def _(pool):
                def step(i, j, k):
                    if runs(i, n):
                        wait_count(pool, turned, i - R + 1)
                        nc.gpsimd.tensor_copy(idxr[:, j:j + 1], r.idx[:, bass.ds(i, 1)]).then_inc(staged, 1)
                        wait_staged(pool, staged, i + 1, passed)
                        nc.gpsimd.indirect_dma_start(rows[:, j, :], None, K.table,
                                                     bass.IndirectOffsetOnAxis(ap=idxr[:, j:j + 1], axis=0))\
                            .then_inc(gathered[j], 16)
                    if scatter:
                        scatter.step(pool, i, j, k)

                steps(pool, n, R, 1, step)
                if scatter:
                    scatter.end(pool)

            @block.tensor
            def _(pe):
                def step(i, j, k):
                    if runs(i, n):
                        pe.wait_ge(gathered[j], 16 * k + 16)
                        wait_count(pe, copied, i - 1)
                        for s in range(KD):
                            last = nc.tensor.transpose(K.ps[j % 2][:, s * P:(s + 1) * P], rows[:, j, s * P:(s + 1) * P],
                                                       K.ident[:, :])
                        last.then_inc(turned, 1)
                    if runs(i - 1, n):
                        c = i - 1
                        jj = (j - 1) % R
                        pe.wait_ge(copied, c + 1)
                        pe.wait_ge(fetched[jj], 32 * ((k if j else k - 1) + 1))
                        wait_count(pe, acted, c - 1)
                        for h in range(nh):
                            for s in range(KD):
                                last = nc.tensor.matmul(K.ps[2 + jj % 2][0:hm, h * P:(h + 1) * P],
                                                        w1r[:, jj, s, h * hm:(h + 1) * hm],
                                                        xT[:, jj % 2, s * P:(s + 1) * P],
                                                        start=(s == 0), stop=(s == KD - 1))
                        last.then_inc(hidden, 1)
                    if runs(i - 2, n):
                        c = i - 2
                        jj = (j - 2) % R
                        e = pe.value_load(r.bin[0:1, bass.ds(c, 1)], min_val=0, max_val=experts - 1)
                        if isinstance(c, int) and c == 0:
                            pe.wait_ge(spread, 48)
                        pe.wait_ge(acted, c + 1)
                        wait_count(pe, written, c - 1)
                        bank = K.ps[4 + jj % 2][:, 0:D]
                        for h in range(nh):
                            nc.tensor.matmul(bank, hT[:, jj % 2, h * P:(h + 1) * P], w2r[:, jj, h, :],
                                             start=(h == 0), stop=False)
                        nc.tensor.matmul(bank, ones3[:, :], b2r[:, bass.ds(e * D, D)], start=False, stop=True)\
                            .then_inc(summed, 1)

                steps(pe, n, R, 2, step)

            @block.scalar
            def _(act):
                act.dma_start(b1T[:, :], b1.rearrange("e (c p) -> p (e c)", p=hm)).then_inc(biased, 16)
                act.wait_ge(split, 1)
                for part in range(3):
                    act.dma_start(b2r[part:part + 1, :], b2p[:, part, :]).then_inc(spread, 16)
                act.wait_ge(biased, 16)

                def step(i, j, k):
                    e = act.value_load(r.bin[0:1, bass.ds(i, 1)], min_val=0, max_val=experts - 1)
                    act.wait_ge(hidden, i + 1)
                    wait_count(act, summed, i - 1)
                    for h in range(nh):
                        last = nc.scalar.activation(hT[:, j % 2, h * P:(h + 1) * P],
                                                    K.ps[2 + j % 2][0:hm, h * P:(h + 1) * P], func,
                                                    bias=b1T[:, bass.ds(e * nh + h, 1)])
                    last.then_inc(acted, 1)

                steps(act, n, R, 0, step)

            @block.vector
            def _(dve):
                link = linker(dve, chain)
                V = nc.vector
                V.memset(ones3[:, :], 1.0)
                dve.wait_ge(b2_loaded, 16)
                link(V.tensor_copy(b2p[:, 0, :], b2s[:, :]))
                link(V.tensor_tensor(rest[:, 0, :], b2s[:, :], b2p[:, 0, :], ALU.subtract))
                link(V.tensor_copy(b2p[:, 1, :], rest[:, 0, :]))
                link(V.tensor_tensor(rest[:, 1, :], rest[:, 0, :], b2p[:, 1, :], ALU.subtract))
                V.tensor_copy(b2p[:, 2, :], rest[:, 1, :]).then_inc(split, 1)

                def step(i, j8, k):
                    j = j8 % R
                    if runs(i, n):
                        dve.wait_ge(turned, i + 1)
                        wait_count(dve, hidden, i - 1)
                        nc.vector.tensor_copy(xT[:, j % 2, :], K.ps[j % 2][:, 0:D]).then_inc(copied, 1)
                    if runs(i - 2, n):
                        jj = (j - 2) % R
                        dve.wait_ge(summed, i - 1)
                        wait_count(dve, stored[jj], 16 * (2 * k + (j8 - 2) // R))
                        if relu_out:
                            ins = nc.vector.tensor_scalar(yr[:, jj, :], K.ps[4 + jj % 2][:, 0:D], 0.0, None, ALU.max)
                        else:
                            ins = nc.vector.tensor_copy(yr[:, jj, :], K.ps[4 + jj % 2][:, 0:D])
                        ins.then_inc(written, 1)

                steps(dve, n, 2 * R, 2, step)


def combine(nc, K, slots, weights, first, dst):
    picks = len(slots)
    R = 4
    with stage(nc) as st:
        rows = st.sb("rows", [P, R * picks, D])
        gathered = [st.sem(f"gathered{j}") for j in range(R)]
        added = st.sem("added")
        with nc.Block() as block:

            @block.gpsimd
            def _(pool):
                for t in range(NT):
                    j = t % R
                    if t >= R:
                        pool.wait_ge(added, picks * (t - R + 1))
                    for p in range(picks):
                        nc.gpsimd.indirect_dma_start(rows[:, j * picks + p, :], None, K.slot_rows,
                                                     bass.IndirectOffsetOnAxis(ap=slots[p][:, t:t + 1], axis=0))\
                            .then_inc(gathered[j], 16)

            @block.vector
            def _(dve):
                def step(t, j, k):
                    dve.wait_ge(gathered[j], 16 * picks * (k + 1))
                    for p in range(picks):
                        row = rows[:, j * picks + p, :]
                        onto = first if p == 0 else dst
                        if p:
                            dve.wait_ge(added, picks * t + p)
                        if weights is None:
                            ins = nc.vector.tensor_tensor(tile_of(dst, t), tile_of(onto, t), row, ALU.add)
                        else:
                            ins = nc.vector.scalar_tensor_tensor(tile_of(dst, t), row, weights[p][:, bass.ds(t, 1)],
                                                                 tile_of(onto, t), ALU.mult, ALU.add)
                        ins.then_inc(added, 1)

                steps(dve, NT, R, 0, step)


def route(nc, K, r, gate, experts, picks, mode, beside):
    gate_w, gate_b = gate
    with stage(nc) as big:
        logits = big.sb("logits", [P, NT * experts])
        masks = [big.sb(f"mask{p}", [P, experts * NT]) for p in range(picks)]
        total = big.sb("total", [P, experts * NT]) if picks > 1 else masks[0]
        lane, chunk = big.sb("lane", [P, picks * NT]), big.sb("chunk", [P, picks * NT])
        token = big.sb("token", [P, NT])
        found = big.sb("found", [P, NT])
        found_i = big.sb("found_i", [P, NT], I32)
        dense(nc, K, [K.x], [[gate_w]], gate_b, [(experts, "sb", logits, None)], beside, norm=(K.xn, K.table))
        with stage(nc) as st:
            top = st.sb("top", [P, NT * 8])
            at = st.sb("at", [P, NT * 8], U32)
            atf = st.sb("atf", [P, NT * 8])
            m = st.sb("m", [P, NT])
            z = st.sb("z", [P, NT])
            chain, asked, answered, numbered = (st.sem(x) for x in ("chain", "asked", "answered", "numbered"))
            top3 = top[:, :].rearrange("p (t e) -> p t e", e=8)
            atf3 = atf[:, :].rearrange("p (t e) -> p t e", e=8)
            lg3 = logits[:, :].rearrange("p (t e) -> p t e", e=experts)
            with nc.Block() as block:

                @block.gpsimd
                def _(pool):
                    nc.gpsimd.iota(found_i[:, :], pattern=[[P, NT]], base=0, channel_multiplier=1).then_inc(numbered, 1)

                @block.scalar
                def _(act):
                    if mode == "top_of_softmax":
                        act.wait_ge(asked, 1)
                        nc.scalar.activation(logits[:, :], logits[:, :], ACT.Exp).then_inc(answered, 1)
                    if mode == "softmax_of_top":
                        act.wait_ge(asked, 1)
                        nc.scalar.activation(m[:, :], m[:, :], ACT.Exp).then_inc(answered, 1)

                @block.vector
                def _(dve):
                    link = linker(dve, chain)
                    V = nc.vector
                    dve.wait_ge(numbered, 1)
                    link(V.tensor_copy(token[:, :], found_i[:, :]))
                    if mode == "top_of_softmax":
                        link(V.tensor_reduce(m[:, :], lg3, AX.X, ALU.max))
                        V.tensor_tensor(lg3, lg3, m[:, :].unsqueeze(2).broadcast_to([P, NT, experts]),
                                        ALU.subtract).then_inc(asked, 1)
                        dve.wait_ge(answered, 1)
                        link(V.tensor_reduce(z[:, :], lg3, AX.X, ALU.add))
                        link(V.reciprocal(z[:, :], z[:, :]))
                        link(V.tensor_tensor(lg3, lg3, z[:, :].unsqueeze(2).broadcast_to([P, NT, experts]), ALU.mult))
                    for t in range(NT):
                        last = V.max(top3[:, t, :], lg3[:, t, :])
                    link(last)
                    for t in range(NT):
                        last = V.max_index(at[:, 8 * t:8 * t + 8], top3[:, t, :], lg3[:, t, :])
                    link(last)
                    link(V.tensor_copy(atf[:, :], at[:, :]))
                    for p in range(picks):
                        for e in range(experts):
                            last = V.tensor_scalar(masks[p][:, e * NT:(e + 1) * NT], atf3[:, :, p], float(e), None,
                                                   ALU.is_equal)
                    link(last)
                    if picks > 1:
                        link(V.tensor_tensor(total[:, :], masks[0][:, :], masks[1][:, :], ALU.add))
                    if mode == "top_of_softmax":
                        V.tensor_copy(r.weights[0][:, :], top3[:, :, 0])
                        link(V.tensor_copy(r.weights[1][:, :], top3[:, :, 1]))
                    if mode == "softmax_of_top":
                        V.tensor_tensor(m[:, :], top3[:, :, 1], top3[:, :, 0], ALU.subtract).then_inc(asked, 1)
                        dve.wait_ge(answered, 1)
                        link(V.tensor_scalar(z[:, :], m[:, :], 1.0, None, ALU.add))
                        link(V.reciprocal(r.weights[0][:, :], z[:, :]))
                        link(V.tensor_tensor(r.weights[1][:, :], r.weights[0][:, :], m[:, :], ALU.mult))

        part = [slice(p * NT, (p + 1) * NT) for p in range(picks)]
        place(nc, K, total[:, :], [(masks[p][:, :], (lane[:, part[p]], chunk[:, part[p]]), r.slots[p][:, :])
                                   for p in range(picks)], P, experts, NT, r.chunks, r.bin[:, 0:r.chunks])
        items_of_slots(nc, K, lane[:, :], chunk[:, :], token[:, :], r.idx[:, 0:r.chunks])


def moe(nc, K, gate, w1, b1, w2, b2, picks, mode, func, relu_out=False, after=None, beside=(None, None)):
    experts = w1.shape[0]
    with stage(nc) as st:
        r = Routing(st, picks, experts, mode is not None)
        route(nc, K, r, gate, experts, picks, mode, beside[0])
        routed_ffn(nc, K, r, w1, b1, w2, b2, func, relu_out, beside[1])
        if after is None:
            combine(nc, K, r.slots, r.weights, K.x, K.x)
        else:
            combine(nc, K, r.slots, r.weights, K.xn, K.agg)
            layer_norm(nc, K, K.agg, K.agg, affine=after, residual=True)


def one_hot(nc, edges, K, hot, i):
    at = edges.pay[:, bass.ds(i * (3 * GS), 3 * GS)].rearrange("p (c w) -> p c w", w=3)[:, :, 1]
    return nc.vector.tensor_tensor(hot, K.iota[:, 0:P].unsqueeze(1).broadcast_to([P, GS, P]),
                                   at.unsqueeze(2).broadcast_to([P, GS, P]), ALU.is_equal)


def attention_scores(nc, K, edges, q, k_table, scores):
    GR = 4 * GS
    S = CHUNKS // GS
    with stage(nc) as st:
        idxr = st.sb("idxr", [P, 2 * GR], I32)
        rows = st.sb("rows", [P, GR, D])
        hot = st.sb("hot", [P, 2, GS, P])
        hotT = st.sb("hotT", [P, 2, GS * P])
        prod = st.sb("prod", [P, 2, GS * D])
        gathered = [st.sem(f"gathered{j}") for j in range(4)]
        staged, passed, onehot, turned, copied, queried, product, scored = (
            st.sem(x) for x in ("staged", "passed", "onehot", "turned", "copied", "queried", "product", "scored"))
        with nc.Block() as block:

            @block.gpsimd
            def _(pool):
                gather_rows(nc, pool, edges, k_table, rows, idxr, gathered, staged, passed, scored, GS)

            @block.vector
            def _(dve):
                def step(i, j, k):
                    if runs(i, S):
                        wait_count(dve, turned, i - 1)
                        one_hot(nc, edges, K, hot[:, j % 2, :, :], i).then_inc(onehot, 1)
                    if runs(i - 2, S):
                        c, jj = i - 2, (j - 2) % 4
                        dve.wait_ge(queried, c + 1)
                        dve.wait_ge(gathered[jj], 16 * GS * ((k if j >= 2 else k - 1) + 1))
                        wait_count(dve, scored, c - 1)
                        for hh in range(2):
                            last = nc.vector.tensor_tensor(
                                prod[:, jj % 2, hh * 2 * D:(hh + 1) * 2 * D].rearrange("p (c d) -> p c d", d=D),
                                K.ps[2 + 2 * (jj % 2) + hh][:, 0:2 * D].rearrange("p (c d) -> p c d", d=D),
                                rows[:, GS * jj + 2 * hh:GS * jj + 2 * hh + 2, :], ALU.mult)
                        last.then_inc(product, 1)
                        dve.wait_ge(product, c + 1)
                        nc.vector.tensor_reduce(scores[:, bass.ds(c * (GS * HEADS), GS * HEADS)],
                                                prod[:, jj % 2, :].rearrange("p (h d) -> p h d", d=DH),
                                                AX.X, ALU.add).then_inc(scored, 1)

                steps(dve, S, 4, 2, step)

            @block.tensor
            def _(pe):
                def step(i, j, k):
                    if runs(i, S):
                        pe.wait_ge(onehot, i + 1)
                        wait_count(pe, copied, i - 1)
                        for g in range(GS):
                            last = nc.tensor.transpose(K.ps[j % 2][:, g * P:(g + 1) * P], hot[:, j % 2, g, :], K.ident[:, :])
                        last.then_inc(turned, 1)
                    if runs(i - 1, S):
                        c, jj = i - 1, (j - 1) % 4
                        pe.wait_ge(copied, c + 1)
                        wait_count(pe, product, c - 1)
                        for g in range(GS):
                            t = pe.value_load(edges.bin[0:1, bass.ds(c * GS + g, 1)], min_val=0, max_val=NT - 1)
                            last = nc.tensor.matmul(K.ps[2 + 2 * (jj % 2) + g // 2][:, g % 2 * D:(g % 2 + 1) * D],
                                                    hotT[:, jj % 2, g * P:(g + 1) * P], tile_of(q, t),
                                                    start=True, stop=True)
                        last.then_inc(queried, 1)

                steps(pe, S, 4, 1, step)

            @block.scalar
            def _(act):
                def step(i, j, k):
                    act.wait_ge(turned, i + 1)
                    wait_count(act, queried, i - 1)
                    nc.scalar.activation(hotT[:, j % 2, :], K.ps[j % 2][:, :], ACT.Copy).then_inc(copied, 1)

                steps(act, S, 4, 0, step)


def turn(nc, K, src, dst):
    groups = [range(g, min(g + 4, PER)) for g in range(0, PER, 4)]
    with stage(nc) as st:
        turned = st.sem("turned")
        with nc.Block() as block:

            @block.tensor
            def _(pe):
                for g, group in enumerate(groups):
                    for o in group:
                        last = nc.tensor.transpose(K.ps[g][:, (o % 4) * P:(o % 4 + 1) * P], src[:, o * P:(o + 1) * P],
                                                   K.ident[:, :])
                    last.then_inc(turned, 1)

            def copies(parity, wait, copy):
                for g, group in enumerate(groups):
                    if g % 2 == parity:
                        wait(turned, g + 1)
                        for o in group:
                            view, shape = dst(o)
                            square = K.ps[g][:, (o % 4) * P:(o % 4 + 1) * P]
                            copy(view, square if shape is None else square.rearrange("p (b h) -> p b h", h=HEADS))

            @block.vector
            def _(dve):
                copies(0, dve.wait_ge, nc.vector.tensor_copy)

            @block.scalar
            def _(act):
                copies(1, act.wait_ge, lambda o, i: nc.scalar.activation(o, i, ACT.Copy))


class Segments:

    def __init__(self, st):
        self.reset = st.sb("reset", [P, SPAN + 1])
        self.of_block = st.sb("of_block", [P, BLOCKS])
        self.of_head = st.sb("of_head", [P, HEADS])
        self.of_headT = st.sb("of_headT", [HEADS, P])
        self.joint = st.sb("joint", [HEADS, BLOCKS])
        self.through_f = st.sb("through_f", [HEADS, BLOCKS])
        self.through_r = st.sb("through_r", [HEADS, BLOCKS])


def by_offset(buf, width):
    return buf.rearrange("p (b o w) -> p b o w", b=BLOCKS, w=width)


def find_segments(nc, K, edges, G):
    B = BLOCKS
    with stage(nc) as st:
        nodes = st.sb("nodes", [P, PER * P])
        nodesT = st.sb("nodesT", [P, SPAN])
        ends = st.sb("ends", [P, 3 * B])
        small = st.sb("small", [HEADS, 3 * B])
        low = st.sb("low", [P, 1])
        nodes4 = nodes[:, :].rearrange("p (o b h) -> p b o h", b=B, h=HEADS)
        node = by_offset(edges.pay[:, :], 3)[:, :, :, 2]
        vector_work(nc, *[lambda h=h: nc.vector.tensor_copy(nodes4[:, :, :, h], node) for h in range(HEADS)])
        turn(nc, K, nodes, lambda o: (nodesT[:, o * P:(o + 1) * P], None))
        chain, packed, moved = st.sem("chain"), st.sem("packed"), st.sem("moved")
        with nc.Block() as block:

            @block.tensor
            def _(pe):
                pe.wait_ge(packed, 1)
                nc.tensor.matmul(K.ps[0][0:HEADS, 0:3 * B], G.of_head[:, :], ends[:, :], start=True, stop=True).then_inc(moved, 1)

            @block.vector
            def _(dve):
                link = linker(dve, chain)
                V = nc.vector
                ident = K.ident[:, :]
                V.tensor_reduce(G.of_block[:, :], ident.rearrange("p (b h) -> p b h", h=HEADS), AX.X, ALU.add)
                V.tensor_reduce(G.of_head[:, :], ident.rearrange("p (b h) -> p h b", h=HEADS), AX.X, ALU.add)
                V.tensor_copy(G.of_headT[:, :].rearrange("g (b h) -> g b h", h=HEADS),
                              K.ident[0:HEADS, 0:HEADS].unsqueeze(1).broadcast_to([HEADS, B, HEADS]))
                link(V.memset(G.reset[:, :], 0.0))
                link(V.tensor_tensor(G.reset[:, 1:SPAN], nodesT[:, 1:SPAN], nodesT[:, 0:SPAN - 1], ALU.not_equal))
                link(V.tensor_scalar(G.reset[:, 1:SPAN], G.reset[:, 1:SPAN], -BIG, None, ALU.mult))
                link(V.tensor_reduce(low[:, :], G.reset[:, :], AX.X, ALU.min))
                for n, value in enumerate((nodesT[:, 0:1], nodesT[:, SPAN - 1:SPAN], low[:, 0:1])):
                    last = V.tensor_scalar(ends[:, n * B:(n + 1) * B], G.of_block[:, :], value, None, ALU.mult)
                last.then_inc(packed, 1)
                dve.wait_ge(moved, 1)
                link(V.tensor_copy(small[:, :], K.ps[0][0:HEADS, 0:3 * B]))
                link(V.memset(G.joint[:, :], -BIG))
                link(V.tensor_tensor(G.joint[:, 1:B], small[:, 1:B], small[:, B:2 * B - 1], ALU.not_equal))
                link(V.tensor_scalar(G.joint[:, 1:B], G.joint[:, 1:B], -BIG, None, ALU.mult))
                link(V.memset(G.through_r[:, :], -BIG))
                V.tensor_tensor(G.through_f[:, :], G.joint[:, :], small[:, 2 * B:3 * B], ALU.min)
                link(V.tensor_tensor(G.through_r[:, 0:B - 1], G.joint[:, 1:B], small[:, 2 * B:3 * B - 1], ALU.min))


def attention_weights(nc, K, G, scores):
    B = BLOCKS
    with stage(nc) as st:
        packed = st.sb("packed", [P, PER * P])
        scoresT = st.sb("scoresT", [P, SPAN])
        peak = st.sb("peak", [P, SPAN])
        ends = st.sb("ends", [P, B])
        small = st.sb("small", [HEADS, B])
        scan = st.sb("scan", [HEADS, B])
        past = st.sb("past", [HEADS, B])
        into = st.sb("into", [P, 1])
        scores4 = by_offset(scores[:, :], HEADS)
        packed4 = packed[:, :].rearrange("p (o b h) -> p b o h", b=B, h=HEADS)
        vector_work(nc, *[lambda b=b: nc.vector.tensor_copy(packed4[:, b, :, :], scores4[:, b, :, :]) for b in range(B)])
        turn(nc, K, packed, lambda o: (scoresT[:, o * P:(o + 1) * P], None))
        with stage(nc) as st2:
            chain, shifted, raised = (st2.sem(x) for x in ("chain", "shifted", "raised"))
            ended, moved, carried, spread = (st2.sem(x) for x in ("ended", "moved", "carried", "spread"))
            with nc.Block() as block:

                @block.tensor
                def _(pe):
                    for way in range(2):
                        pe.wait_ge(ended, way + 1)
                        nc.tensor.matmul(K.ps[0][0:HEADS, 0:B], G.of_head[:, :], ends[:, :], start=True,
                                         stop=True).then_inc(moved, 1)
                        pe.wait_ge(carried, way + 1)
                        nc.tensor.matmul(K.ps[1][:, 0:B], G.of_headT[:, :], past[:, :], start=True, stop=True).then_inc(spread, 1)

                @block.vector
                def _(dve):
                    link = linker(dve, chain)
                    V = nc.vector
                    for way, (reset, over, goal, last, through, at, fro, to) in enumerate((
                            (G.reset[:, 0:SPAN], scoresT[:, :], peak[:, :], peak[:, SPAN - 1:SPAN], G.through_f[:, :],
                             slice(0, B - 1), slice(1, B), 0),
                            (G.reset[:, 1:SPAN + 1], scoresT[:, :], packed[:, 0:SPAN], packed[:, 0:1], G.through_r[:, :],
                             slice(1, B), slice(0, B - 1), B - 1))):
                        flip = (lambda a: a) if way == 0 else (lambda a: a[:, ::-1])
                        link(V.tensor_tensor_scan(flip(goal), flip(reset), flip(over), -BIG, ALU.add, ALU.max))
                        V.tensor_scalar(ends[:, :], G.of_block[:, :], last, None, ALU.mult).then_inc(ended, 1)
                        dve.wait_ge(moved, way + 1)
                        link(V.tensor_copy(small[:, :], K.ps[0][0:HEADS, 0:B]))
                        link(V.tensor_tensor_scan(flip(scan[:, :]), flip(through), flip(small[:, :]), -BIG, ALU.add, ALU.max))
                        link(V.memset(past[:, :], -BIG))
                        V.tensor_tensor(past[:, fro], scan[:, at], G.joint[:, 1:B], ALU.add).then_inc(carried, 1)
                        dve.wait_ge(spread, way + 1)
                        link(V.tensor_tensor(ends[:, :], K.ps[1][:, 0:B], G.of_block[:, :], ALU.mult))
                        link(V.tensor_reduce(into[:, :], ends[:, :], AX.X, ALU.add))
                        if way == 0:
                            link(V.tensor_tensor_scan(goal, reset, over, into[:, 0:1], ALU.add, ALU.max))
                        else:
                            link(V.tensor_tensor_scan(flip(goal), flip(reset), flip(over), into[:, 0:1], ALU.add, ALU.max))
                    link(V.tensor_tensor(peak[:, :], peak[:, :], packed[:, 0:SPAN], ALU.max))
                    V.tensor_tensor(scoresT[:, :], scoresT[:, :], peak[:, :], ALU.subtract).then_inc(shifted, 1)

                @block.scalar
                def _(act):
                    act.wait_ge(shifted, 1)
                    nc.scalar.activation(scoresT[:, :], scoresT[:, :], ACT.Exp).then_inc(raised, 1)

        turn(nc, K, scoresT, lambda o: (scores4[:, :, o, :], True))


def attention_values(nc, K, edges, v_table, weights, acc):
    GR, W = 4 * GS, D + HEADS
    S = CHUNKS // GS
    with stage(nc) as st:
        idxr = st.sb("idxr", [P, 2 * GR], I32)
        rows = st.sb("rows", [P, GR, D])
        hot = st.sb("hot", [P, 2, GS, P])
        msg = st.sb("msg", [P, 2, GS, W])
        run = st.sb("run", [P, 2 * GS, W])
        gathered = [st.sem(f"gathered{j}") for j in range(4)]
        staged, passed, placed, weighed, summed, ran, kept, cleared = (
            st.sem(x) for x in ("staged", "passed", "placed", "weighed", "summed", "ran", "kept", "cleared"))
        with nc.Block() as block:

            @block.gpsimd
            def _(pool):
                gather_rows(nc, pool, edges, v_table, rows, idxr, gathered, staged, passed, weighed, GS)

            @block.vector
            def _(dve):
                nc.vector.memset(acc[:, :], 0.0)
                nc.vector.memset(run[:, 2 * GS - 1, :], 0.0).then_inc(cleared, 1)
                dve.wait_ge(cleared, 1)

                def step(i, j, k):
                    if runs(i - 2, S):
                        dve.wait_ge(summed, i - 1)
                        wait_count(dve, kept, (i - 3) * GS)
                        for g in range(GS):
                            n = j % 2 * GS + g
                            carry(nc, dve, edges, (run[:, (n - 1) % (2 * GS), :], run[:, n, :]), K.ps[n][:, 0:W],
                                  (i - 2) * GS + g, ran)
                    if runs(i, S):
                        one_hot(nc, edges, K, hot[:, j % 2, :, :], i)
                        dve.wait_ge(gathered[j], 16 * GS * (k + 1))
                        nc.vector.tensor_tensor(
                            msg[:, j % 2, :, 0:D].rearrange("p c (h d) -> p c h d", d=DH),
                            rows[:, GS * j:GS * (j + 1), :].rearrange("p c (h d) -> p c h d", d=DH),
                            weights[:, bass.ds(i * (GS * HEADS), GS * HEADS)].rearrange("p (c h) -> p c h", h=HEADS)
                            .unsqueeze(3).broadcast_to([P, GS, HEADS, DH]), ALU.mult).then_inc(weighed, 1)

                steps(dve, S, 4, 2, step)

            @block.tensor
            def _(pe):
                def step(i, j, k):
                    pe.wait_ge(weighed, i + 1)
                    pe.wait_ge(placed, i + 1)
                    wait_count(pe, ran, (i - 1) * GS)
                    for g in range(GS):
                        last = nc.tensor.matmul(K.ps[j % 2 * GS + g][:, 0:W], hot[:, j % 2, g, :], msg[:, j % 2, g, :],
                                                start=True, stop=True)
                    last.then_inc(summed, 1)

                steps(pe, S, 4, 0, step)

            @block.scalar
            def _(act):
                act.wait_ge(cleared, 1)

                def step(i, j, k):
                    if runs(i, S):
                        wait_count(act, summed, i - 1)
                        nc.scalar.activation(msg[:, j % 2, :, D:W],
                                             weights[:, bass.ds(i * (GS * HEADS), GS * HEADS)]
                                             .rearrange("p (c h) -> p c h", h=HEADS), ACT.Copy).then_inc(placed, 1)
                    if runs(i - 2, S):
                        for g in range(GS):
                            keep(nc, act, edges, acc, run[:, j % 2 * GS + g, :], (i - 2) * GS + g, W, ran, kept)

                steps(act, S, 4, 2, step)


def node_mlp(nc, K, src, w1, b1, w2, b2):
    hid = w1.shape[1]
    nh = hid // P
    with stage(nc) as st:
        w1s = st.sb("w1s", [P, KD, hid])
        w2s = st.sb("w2s", [P, nh, D])
        b1T = st.sb("b1T", [P, nh])
        b2s = st.sb("b2s", [P, D])
        raw = st.sb("raw", [P, 2, D])
        xT = st.sb("xT", [P, 2, D])
        hT = st.sb("hT", [P, 2, hid])
        loaded, staged, biased, turned, copied, hidden, acted, summed, added = (
            st.sem(x) for x in ("loaded", "staged", "biased", "turned", "copied", "hidden", "acted", "summed", "added"))
        with nc.Block() as block:

            @block.sync
            def _(sp):
                sp.dma_start(w1s[:, :, :], w1.rearrange("(k p) h -> p k h", p=P)).then_inc(loaded, 16)
                sp.dma_start(w2s[:, :, :], w2.rearrange("(c p) d -> p c d", p=P)).then_inc(loaded, 16)
                sp.dma_start(b1T[:, :], b1.rearrange("(c p) -> p c", p=P)).then_inc(loaded, 16)
                sp.dma_start(b2s[:, :], b2.partition_broadcast(P)).then_inc(loaded, 16)

            @block.scalar
            def _(act):
                act.wait_ge(loaded, 64)

                def step(i, j, k):
                    act.wait_ge(hidden, i + 1)
                    wait_count(act, summed, i - 1)
                    for h in range(nh):
                        last = nc.scalar.activation(hT[:, j, h * P:(h + 1) * P],
                                                    K.ps[2 + 2 * j + h // 4][:, h % 4 * P:(h % 4 + 1) * P], ACT.Relu,
                                                    bias=b1T[:, h:h + 1])
                    last.then_inc(acted, 1)

                steps(act, NT, 2, 0, step)

            @block.tensor
            def _(pe):
                pe.wait_ge(loaded, 64)

                def step(i, j4, k):
                    j = j4 % 2
                    if runs(i, NT):
                        pe.wait_ge(staged, i + 1)
                        wait_count(pe, copied, i)
                        for s in range(KD):
                            last = nc.tensor.transpose(K.ps[0][:, s * P:(s + 1) * P], raw[:, j, s * P:(s + 1) * P],
                                                       K.ident[:, :])
                        last.then_inc(turned, 1)
                    if runs(i - 1, NT):
                        c, jj = i - 1, 1 - j
                        pe.wait_ge(copied, c + 1)
                        wait_count(pe, acted, c - 1)
                        for h in range(nh):
                            for s in range(KD):
                                last = nc.tensor.matmul(K.ps[2 + 2 * jj + h // 4][:, h % 4 * P:(h % 4 + 1) * P],
                                                        w1s[:, s, h * P:(h + 1) * P], xT[:, jj, s * P:(s + 1) * P],
                                                        start=(s == 0), stop=(s == KD - 1))
                        last.then_inc(hidden, 1)
                    if runs(i - 2, NT):
                        c, jj = i - 2, j
                        pe.wait_ge(acted, c + 1)
                        wait_count(pe, added, c - 1)
                        bank = K.ps[6 + jj][:, 0:D]
                        for h in range(nh):
                            last = nc.tensor.matmul(bank, hT[:, jj, h * P:(h + 1) * P], w2s[:, h, :], start=(h == 0),
                                                    stop=(h == nh - 1))
                        last.then_inc(summed, 1)

                steps(pe, NT, 4, 2, step)

            @block.vector
            def _(dve):
                def step(i, j4, k):
                    j = j4 % 2
                    if runs(i, NT):
                        wait_count(dve, turned, i - 1)
                        nc.vector.tensor_copy(raw[:, j, :], tile_of(src, i)).then_inc(staged, 1)
                        if isinstance(i, int) and i == 0:
                            dve.wait_ge(loaded, 64)
                        nc.vector.tensor_tensor(tile_of(K.x, i), tile_of(K.x, i), b2s[:, :], ALU.add).then_inc(biased, 1)
                    if runs(i - 1, NT):
                        dve.wait_ge(turned, i)
                        wait_count(dve, hidden, i - 2)
                        nc.vector.tensor_copy(xT[:, 1 - j, :], K.ps[0][:, 0:D]).then_inc(copied, 1)
                    if runs(i - 3, NT):
                        dve.wait_ge(biased, i - 2)
                        dve.wait_ge(summed, i - 2)
                        nc.vector.tensor_tensor(tile_of(K.x, i - 3), tile_of(K.x, i - 3), K.ps[6 + (1 - j)][:, 0:D],
                                                ALU.add).then_inc(added, 1)

                steps(dve, NT, 4, 3, step)


class Statistics:

    def __init__(self, st):
        self.stats = st.sb("stats", [P, KD, NT * 6])
        self.scale = st.sb("scale", [P, KD])
        self.shift = st.sb("shift", [P, KD])


def write_tile(nc, S, dst, bank, bs, t, written):
    for o in range(KD):
        last = nc.vector.tensor_scalar(dst[:, bass.ds(t * P + o * NPAD, P)], bank(o), bs[:, o:o + 1], None, ALU.add)
    last.then_inc(written, 1)


def measure_tile(nc, dve, S, dst, t, written, measured):
    dve.wait_ge(written, t + 1)
    n = LAST if isinstance(t, int) and t == NT - 1 else P
    for o in range(KD):
        last = nc.vector.bn_stats(S.stats[:, o, bass.ds(t * 6, 6)], dst[:, bass.ds(t * P + o * NPAD, n)])
    last.then_inc(measured, 1)


def node_to_feature(nc, K, src, also, w, b, dst, S):
    with stage(nc) as st:
        ws = st.sb("ws", [P, KD, D])
        bs = st.sb("bs", [P, KD])
        raw = st.sb("raw", [P, 4, D])
        xT = st.sb("xT", [P, 2, D])
        loaded, staged, turned, copied, summed, written, measured = (
            st.sem(x) for x in ("loaded", "staged", "turned", "copied", "summed", "written", "measured"))
        with nc.Block() as block:

            @block.sync
            def _(sp):
                sp.dma_start(ws[:, :, :], w.rearrange("(k p) n -> p k n", p=P)).then_inc(loaded, 16)
                sp.dma_start(bs[:, :], b.rearrange("(k p) -> p k", p=P)).then_inc(loaded, 16)

            @block.scalar
            def _(act):
                def step(i, j, k):
                    act.wait_ge(turned, i + 1)
                    wait_count(act, summed, i - 1)
                    nc.scalar.activation(xT[:, j % 2, :], K.ps[j % 2][:, 0:D], ACT.Copy).then_inc(copied, 1)

                steps(act, NT, 4, 0, step)

            @block.tensor
            def _(pe):
                def step(i, j, k):
                    if runs(i, NT):
                        pe.wait_ge(staged, i + 1)
                        wait_count(pe, copied, i - 1)
                        for s in range(KD):
                            last = nc.tensor.transpose(K.ps[j % 2][:, s * P:(s + 1) * P], raw[:, j, s * P:(s + 1) * P],
                                                       K.ident[:, :])
                        last.then_inc(turned, 1)
                    if runs(i - 1, NT):
                        if isinstance(i, int) and i == 1:
                            pe.wait_ge(loaded, 32)
                        pe.wait_ge(copied, i)
                        wait_count(pe, written, i - 2)
                        for o in range(KD):
                            for s in range(KD):
                                last = nc.tensor.matmul(K.ps[2 + 2 * ((j - 1) % 2) + o][:, 0:P], ws[:, s, o * P:(o + 1) * P],
                                                        xT[:, (j - 1) % 2, s * P:(s + 1) * P], start=(s == 0),
                                                        stop=(s == KD - 1))
                        last.then_inc(summed, 1)

                steps(pe, NT, 4, 1, step)

            @block.vector
            def _(dve):
                def step(i, j, k):
                    if runs(i, NT):
                        wait_count(dve, turned, i - 3)
                        nc.vector.tensor_tensor(raw[:, j, :], tile_of(src, i), tile_of(also, i), ALU.add).then_inc(staged, 1)
                    if runs(i - 3, NT):
                        if isinstance(i, int) and i == 3:
                            dve.wait_ge(loaded, 32)
                        dve.wait_ge(summed, i - 2)
                        write_tile(nc, S, dst, lambda o: K.ps[2 + 2 * ((j - 3) % 2) + o][:, 0:P], bs, i - 3, written)
                    if runs(i - 4, NT):
                        measure_tile(nc, dve, S, dst, i - 4, written, measured)

                steps(dve, NT, 4, 4, step)
                dve.wait_ge(measured, NT)


def feature_to_feature(nc, K, src, w, b, dst, S):
    with stage(nc) as st:
        ws = st.sb("ws", [P, KD, D])
        bs = st.sb("bs", [P, KD])
        normed = st.sb("normed", [P, 4, D])
        loaded, ready, summed, written, measured = (st.sem(x) for x in ("loaded", "ready", "summed", "written", "measured"))
        with nc.Block() as block:

            @block.sync
            def _(sp):
                sp.dma_start(ws[:, :, :], w.rearrange("(k p) n -> p k n", p=P)).then_inc(loaded, 16)
                sp.dma_start(bs[:, :], b.rearrange("(k p) -> p k", p=P)).then_inc(loaded, 16)

            @block.scalar
            def _(act):
                def step(t, j, k):
                    wait_count(act, summed, t - 3)
                    for o in range(KD):
                        last = nc.scalar.activation(normed[:, j, o * P:(o + 1) * P], src[:, bass.ds(t * P + o * NPAD, P)],
                                                    ACT.Relu, bias=S.shift[:, o:o + 1], scale=S.scale[:, o:o + 1])
                    last.then_inc(ready, 1)

                steps(act, NT, 4, 0, step)

            @block.tensor
            def _(pe):
                pe.wait_ge(loaded, 32)

                def step(t, j, k):
                    pe.wait_ge(ready, t + 1)
                    wait_count(pe, written, t - 1)
                    for o in range(KD):
                        for s in range(KD):
                            last = nc.tensor.matmul(K.ps[2 * (j % 2) + o][:, 0:P], ws[:, s, o * P:(o + 1) * P],
                                                    normed[:, j, s * P:(s + 1) * P], start=(s == 0), stop=(s == KD - 1))
                    last.then_inc(summed, 1)

                steps(pe, NT, 4, 0, step)

            @block.vector
            def _(dve):
                dve.wait_ge(loaded, 32)

                def step(t, j, k):
                    if runs(t, NT):
                        dve.wait_ge(summed, t + 1)
                        write_tile(nc, S, dst, lambda o: K.ps[2 * (j % 2) + o][:, 0:P], bs, t, written)
                    if runs(t - 1, NT):
                        measure_tile(nc, dve, S, dst, t - 1, written, measured)

                steps(dve, NT, 4, 1, step)
                dve.wait_ge(measured, NT)


def batch_norm_scale(nc, K, gamma, beta, S):
    with stage(nc) as st:
        mv = st.sb("mv", [P, KD, 2])
        gb = st.sb("gb", [P, 2, KD])
        rstd = st.sb("rstd", [P, KD])
        tmp = st.sb("tmp", [P, KD])
        loaded, chain, asked, root = (st.sem(x) for x in ("loaded", "chain", "asked", "root"))
        with nc.Block() as block:

            @block.sync
            def _(sp):
                sp.dma_start(gb[:, 0, :], gamma.rearrange("(k p) -> p k", p=P)).then_inc(loaded, 16)
                sp.dma_start(gb[:, 1, :], beta.rearrange("(k p) -> p k", p=P)).then_inc(loaded, 16)

            @block.scalar
            def _(act):
                act.wait_ge(asked, 1)
                nc.scalar.activation(rstd[:, :], rstd[:, :], ACT.Sqrt).then_inc(root, 1)

            @block.vector
            def _(dve):
                link = linker(dve, chain)
                V = nc.vector
                for o in range(KD):
                    last = V.bn_aggr(mv[:, o, :], S.stats[:, o, :])
                link(last)
                V.tensor_scalar(rstd[:, :], mv[:, :, 1], EPS, None, ALU.add).then_inc(asked, 1)
                dve.wait_ge(root, 1)
                dve.wait_ge(loaded, 32)
                link(V.reciprocal(rstd[:, :], rstd[:, :]))
                link(V.tensor_tensor(S.scale[:, :], rstd[:, :], gb[:, 0, :], ALU.mult))
                link(V.tensor_tensor(tmp[:, :], S.scale[:, :], mv[:, :, 0], ALU.mult))
                link(V.tensor_tensor(S.shift[:, :], gb[:, 1, :], tmp[:, :], ALU.subtract))


def batch_norm_relu_to_nodes(nc, K, src, scale, shift, h, table):
    with stage(nc) as st:
        raw = st.sb("raw", [P, 2, D])
        normed, turned, written, stored = (st.sem(x) for x in ("normed", "turned", "written", "stored"))
        with nc.Block() as block:

            @block.scalar
            def _(act):
                def step(t, j, k):
                    wait_count(act, turned, t - 1)
                    for o in range(KD):
                        last = nc.scalar.activation(raw[:, j, o * P:(o + 1) * P], src[:, bass.ds(t * P + o * NPAD, P)],
                                                    ACT.Relu, bias=shift[:, o:o + 1], scale=scale[:, o:o + 1])
                    last.then_inc(normed, 1)

                steps(act, NT, 2, 0, step)

            @block.tensor
            def _(pe):
                def step(t, j, k):
                    pe.wait_ge(normed, t + 1)
                    wait_count(pe, written, t - 1)
                    for o in range(KD):
                        last = nc.tensor.transpose(K.ps[j][:, o * P:(o + 1) * P], raw[:, j, o * P:(o + 1) * P], K.ident[:, :])
                    last.then_inc(turned, 1)

                steps(pe, NT, 2, 0, step)

            @block.vector
            def _(dve):
                def step(t, j, k):
                    dve.wait_ge(turned, t + 1)
                    if h is None:
                        ins = nc.vector.tensor_tensor(tile_of(K.x, t), tile_of(K.x, t), K.ps[j][:, 0:D], ALU.add)
                    else:
                        ins = nc.vector.tensor_copy(tile_of(h, t), K.ps[j][:, 0:D])
                    ins.then_inc(written, 1)

                steps(dve, NT, 2, 0, step)

            @block.sync
            def _(sp):
                if h is not None:
                    def step(t, j, k):
                        sp.wait_ge(written, t + 1)
                        sp.dma_start(tile_rows(table, t), tile_of(h, t)).then_inc(stored, 16)

                    steps(sp, NT, 2, 0, step)
                    sp.wait_ge(stored, 16 * NT)


def layer0_gnn(nc, K, A, beside):
    layer_norm(nc, K, K.x, K.xn, table=K.table)
    spmm(nc, K, K.by_src, K.table, K.agg)
    dense(nc, K, [K.agg], [[A["L0_gnn_weight"]]], None, [(D, "relu_add", None, None)], beside)


def layer1_gnn(nc, K, A, beside):
    layer_norm(nc, K, K.x, K.xn, table=K.table)
    spmm(nc, K, K.by_src, K.table, K.agg)
    dense(nc, K, [K.xn, K.agg], [[A["L1_gnn_weight"][0:D, :]], [A["L1_gnn_weight"][D:2 * D, :]]],
          A["L1_gnn_bias"], [(D, "add", K.x, None)], beside)


def layer2_gnn(nc, K, A):
    q = K.agg
    read_table(nc, K.dst_table, K.by_dst.pay[:, :])
    spread_tiles(nc, K, K.by_dst)
    W = D + HEADS
    with stage(nc) as st:
        G = Segments(st)
        find_segments(nc, K, K.by_dst, G)
        scores = st.sb("scores", [P, CHUNKS * HEADS])
        for l in range(2):
            dense(nc, K, [K.xn if l else K.x], [[A["L2_gnn_Wq"][l], A["L2_gnn_Wk"][l], A["L2_gnn_Wv"][l]]], None,
                  [(D, "sb", q, float(DH) ** -0.5), (D, "table", K.table, None), (D, "table", K.table2, None)],
                  norm=None if l else (K.xn, None))
            attention_scores(nc, K, K.by_dst, q, K.table, scores)
            attention_weights(nc, K, G, scores)
            with stage(nc) as st2:
                acc = st2.sb("acc", [P, NT * W])
                z = st2.sb("z", [P, NT * HEADS])
                acc4 = acc[:, :].rearrange("p (t w) -> p t w", w=W)
                z3 = z[:, :].rearrange("p (t h) -> p t h", h=HEADS)
                agg4 = K.agg[:, :].rearrange("p (t h d) -> p t h d", t=NT, h=HEADS)
                attention_values(nc, K, K.by_dst, K.table2, scores, acc)
                vector_work(
                    nc,
                    lambda: nc.vector.tensor_scalar(z3, acc4[:, :, D:W], 1e-9, None, ALU.add),
                    lambda: nc.vector.reciprocal(z[:, :], z[:, :]),
                    lambda: nc.vector.tensor_tensor(agg4, acc4[:, :, 0:D].rearrange("p t (h d) -> p t h d", h=HEADS),
                                                    z3.unsqueeze(3).broadcast_to([P, NT, HEADS, DH]), ALU.mult))
            dense(nc, K, [K.agg], [[A["L2_gnn_Wo"][l]]], None, [(D, "add", K.xn, None)])
            layer_norm(nc, K, K.xn, K.xn, affine=(A["L2_gnn_ln_g"][l], A["L2_gnn_ln_b"][l]))
    node_mlp(nc, K, K.xn, A["L2_gnn_w1"], A["L2_gnn_b1"], A["L2_gnn_w2"], A["L2_gnn_b2"])


def layer3_gnn(nc, K, A):
    with stage(nc) as st:
        yT = st.sb("yT", [P, KD * NPAD])
        S = Statistics(st)
        dense(nc, K, [K.x], [[A["L3_gnn_W_in"]]], A["L3_gnn_b_in"], [(D, "both", (K.xn, K.table), None)],
              norm=(None, None))
        layers = A["L3_gnn_W1"].shape[0]
        for l in range(layers):
            spmm(nc, K, K.by_src, K.table, K.agg)
            node_to_feature(nc, K, K.agg, K.xn, A["L3_gnn_W1"][l], A["L3_gnn_b1"][l], yT, S)
            batch_norm_scale(nc, K, A["L3_gnn_g1"][l], A["L3_gnn_be1"][l], S)
            feature_to_feature(nc, K, yT, A["L3_gnn_W2"][l], A["L3_gnn_b2"][l], K.agg, S)
            batch_norm_scale(nc, K, A["L3_gnn_g_out"][l], A["L3_gnn_b_out"][l], S)
            last = l == layers - 1
            batch_norm_relu_to_nodes(nc, K, K.agg, S.scale, S.shift, None if last else K.xn, K.table)


def build(nc, A, out, upto=99):
    with stage(nc) as st:
        st.stack.enter_context(nc.allow_non_contiguous_dma(reason="short rows of biases and of the L3 router"))
        K = Core(nc, st)
        make_constants(nc, K)
        dst_keys = Keys(st, "dst")
        place_edges(nc, K, A["src"], A["dst"], A["edge_weight"], dst_keys)
        ffn = [PER_CHUNK * token_chunks(2, A[w].shape[0]) for w in ("L0_ffn_w1", "L1_ffn_W1")]
        shares = [(24, 2), (32, 2), (ffn[0], PER_CHUNK), (60, 2), (EC - 116 - sum(ffn), 2), (ffn[1], PER_CHUNK)]
        firsts = [sum(cols for cols, _ in shares[:n]) for n in range(len(shares))]
        beside = [lambda st2, first=first, cols=cols, unroll=unroll: Scatter(
            nc, st2, K.dst_table, dst_keys.row, dst_keys.pay, first, cols, unroll)
            for first, (cols, unroll) in zip(firsts, shares)]
        K.x, K.xn, K.agg = (st.sb(n, [P, NT * D]) for n in ("x", "xn", "agg"))
        load_nodes(nc, K, A["x"])
        layers = [
            lambda: layer0_gnn(nc, K, A, beside[0]),
            lambda: moe(nc, K, (A["L0_ffn_gate_w"], A["L0_ffn_gate_b"]), A["L0_ffn_w1"], A["L0_ffn_b1"], A["L0_ffn_w2"], A["L0_ffn_b2"],
                        2, "softmax_of_top", ACT.Relu, after=(A["L0_ffn_gamma"], A["L0_ffn_beta"]),
                        beside=beside[1:3]),
            lambda: layer1_gnn(nc, K, A, beside[3]),
            lambda: moe(nc, K, (A["L1_ffn_Wg"], A["L1_ffn_bg"]), A["L1_ffn_W1"], A["L1_ffn_b1"], A["L1_ffn_W2"], A["L1_ffn_b2"],
                        2, None, ACT.Gelu, beside=beside[4:6]),
            lambda: layer2_gnn(nc, K, A),
            lambda: moe(nc, K, (A["L2_ffn_gate_w"], A["L2_ffn_gate_b"]), A["L2_ffn_W1"], A["L2_ffn_b1"], A["L2_ffn_W2"], A["L2_ffn_b2"],
                        2, "top_of_softmax", ACT.Gelu),
            lambda: layer3_gnn(nc, K, A),
            lambda: moe(nc, K, (A["L3_ffn_router_w"].rearrange("e d -> d e"), A["L3_ffn_router_b"]), A["L3_ffn_W1"], A["L3_ffn_b1"],
                        A["L3_ffn_W2"], A["L3_ffn_b2"], 1, None, ACT.Relu, relu_out=True),
        ]
        for layer in layers[:upto]:
            layer()
        store_nodes(nc, K, out)


def kernel(**inputs):
    import numpy as np
    import concourse.bacc as bacc
    from concourse.bass_utils import run_bass_kernel_spmd

    nc = bacc.Bacc("TRN2", target_bir_lowering=False, num_devices=1)
    arrays, A = {}, {}
    for name, value in inputs.items():
        a = np.ascontiguousarray(value)
        arrays[f"in_{name}"] = a
        A[name] = nc.dram_tensor(f"in_{name}", a.shape, mybir.dt.from_np(a.dtype), kind="ExternalInput").ap()
    out = nc.dram_tensor("out", (NODES, D), FP, kind="ExternalOutput").ap()
    build(nc, A, out)
    r = run_bass_kernel_spmd(nc, [arrays], core_ids=[0])
    return r.results[0]["out"]
```
